# Optimizing a Trainium2 kernel written in Bass

```python
import numpy as np
import jax
import jax.numpy as jnp

def _softmax(x, axis=-1):
    return jax.nn.softmax(x, axis=axis)

def _gelu(x):
    return jax.nn.gelu(x, approximate=True)

def _silu(x):
    return jax.nn.silu(x)

def _sigmoid(x):
    return jax.nn.sigmoid(x)

def _layernorm(x, axis=-1, eps=1e-05):
    m = jnp.mean(x, axis=axis, keepdims=True)
    v = jnp.var(x, axis=axis, keepdims=True)
    return (x - m) / jnp.sqrt(v + eps)

def _scatter_add(tgt, idx, src, axis=0):
    return tgt.at[idx].add(src)

def _segment_sum(src, seg, n):
    return jax.ops.segment_sum(src, seg, n)
kernel_name = 'mk_vit_tower_d2_tok_img768_r4_2e6e39'

def setup_inputs(seed: int=0):
    np.random.seed(seed)
    _w = jnp.asarray

    def _rec_inputs():
        import jax
        import jax.numpy as jnp
        _rk = jax.random.key(seed)
        x = -0.000222058 + 0.999998 * jax.random.normal(jax.random.fold_in(_rk, 1), (32, 128, 192, 1), jnp.float32)
        return x
    x = _rec_inputs()

    def _L0_tok_setup():
        import jax, jax.numpy as jnp
        from jax import lax
        import numpy as np
        DIM = 192
        K = 7
        PAD = K // 2
        EPS = 1e-06
        key = jax.random.key(seed)
        ks = jax.random.split(key, 6)
        B, L = (64, 128)
        x = jax.random.normal(ks[0], (B, L, DIM, 1), dtype=jnp.float32)
        fan_dw = 1 * K * 1
        dw_w = jax.random.uniform(ks[1], (DIM, 1, K, 1), jnp.float32, -1.0 / np.sqrt(fan_dw), 1.0 / np.sqrt(fan_dw))
        fan_pw = DIM
        pw_w = jax.random.uniform(ks[2], (DIM, DIM), jnp.float32, -1.0 / np.sqrt(fan_pw), 1.0 / np.sqrt(fan_pw))
        pw_b = jax.random.uniform(ks[3], (DIM,), jnp.float32, -1.0 / np.sqrt(fan_pw), 1.0 / np.sqrt(fan_pw))
        ln_g = jnp.ones((DIM,), jnp.float32)
        ln_b = jnp.zeros((DIM,), jnp.float32)
        return {'x': x, 'dw_w': dw_w, 'pw_w': pw_w, 'pw_b': pw_b, 'ln_g': ln_g, 'ln_b': ln_b}
    _L0_tok_all = _L0_tok_setup()
    _L0_tok_in = {k: v for k, v in _L0_tok_all.items() if k in ('dw_w', 'pw_w', 'pw_b', 'ln_g', 'ln_b')}
    del _L0_tok_all

    def _L0_attn_setup():
        import jax, jax.numpy as jnp
        import numpy as np
        import math
        B, S, E = (2, 512, 192)
        H = 12
        V = 50257
        EPS = 1e-05

        def _layernorm(x, w):
            mu = jnp.mean(x, axis=-1, keepdims=True)
            var = jnp.mean(jnp.square(x - mu), axis=-1, keepdims=True)
            return (x - mu) * jax.lax.rsqrt(var + EPS) * w
        key = jax.random.key(seed)
        ks = jax.random.split(key, 7)
        x = jax.random.normal(ks[0], (B, S, E), dtype=jnp.float32)
        e = jax.random.normal(ks[1], (B, S, E), dtype=jnp.float32)
        p = jax.random.normal(ks[2], (B, S, E), dtype=jnp.float32)
        ln_w = jnp.ones((E,), dtype=jnp.float32)
        W_qk = 0.02 * jax.random.normal(ks[3], (H, E), dtype=jnp.float32)
        W_o = 0.02 / math.sqrt(2 * 12) * jax.random.normal(ks[4], (E, H * E), dtype=jnp.float32)
        wte = 0.02 * jax.random.normal(ks[5], (V, E), dtype=jnp.float32)
        return {'x': x, 'e': e, 'p': p, 'ln_w': ln_w, 'W_qk': W_qk, 'W_o': W_o, 'wte': wte}
    _L0_attn_all = _L0_attn_setup()
    _L0_attn_in = {k: v for k, v in _L0_attn_all.items() if k in ('e', 'p', 'ln_w', 'W_qk', 'W_o', 'wte')}
    del _L0_attn_all

    def _L0_ffn_setup():
        import jax, jax.numpy as jnp
        import numpy as np
        GT0 = [[0, 1, 0, 0, 1, 0], [0, 1, 0, 0, 0, 1], [0, 0, 1, 0, 1, 0], [0, 0, 1, 0, 0, 1], [0, 0, 0, 1, 1, 0], [0, 0, 0, 1, 0, 1]]
        NCLS = 6
        K = 1

        def _expert_pairs():
            pairs = []
            for i in range(NCLS):
                p = [(j - 1, k - 1) for j in range(1, 6) for k in range(1, 6) if j != k and GT0[i][j] == 1 and (GT0[i][k] == 1)]
                pairs.append(p)
            return pairs
        PAIRS = _expert_pairs()
        B, P, D, H = (64, 64, 192, 768)

        def _gelu(t):
            return jax.nn.gelu(t, approximate=False)
        key = jax.random.key(seed)
        ks = jax.random.split(key, 8)
        s = 0.02
        x = jax.random.normal(ks[0], (B, NCLS + P, D), dtype=jnp.float32)
        mids = jax.random.randint(ks[1], (B,), 0, 6)
        moe0_W1 = jax.random.normal(ks[2], (D, H), dtype=jnp.float32) * s
        moe0_b1 = jnp.zeros((H,), jnp.float32)
        moe0_W2 = jax.random.normal(ks[3], (H, D), dtype=jnp.float32) * s
        moe0_b2 = jnp.zeros((D,), jnp.float32)
        A1_W = jax.random.normal(ks[4], (5, D, H), dtype=jnp.float32) * s
        A1_b = jnp.zeros((5, H), jnp.float32)
        A2_W = jax.random.normal(ks[5], (5, H, D), dtype=jnp.float32) * s
        A2_b = jnp.zeros((5, D), jnp.float32)
        G_W = jax.random.normal(ks[6], (NCLS, D, 2), dtype=jnp.float32) * s
        return {'x': x, 'moe0_W1': moe0_W1, 'moe0_b1': moe0_b1, 'moe0_W2': moe0_W2, 'moe0_b2': moe0_b2, 'A1_W': A1_W, 'A1_b': A1_b, 'A2_W': A2_W, 'A2_b': A2_b, 'G_W': G_W, 'mids': mids}
    _L0_ffn_all = _L0_ffn_setup()
    _L0_ffn_in = {k: v for k, v in _L0_ffn_all.items() if k in ('moe0_W1', 'moe0_b1', 'moe0_W2', 'moe0_b2', 'A1_W', 'A1_b', 'A2_W', 'A2_b', 'G_W', 'mids')}
    del _L0_ffn_all

    def _L1_attn_setup():
        import jax, jax.numpy as jnp
        import numpy as np
        FEATS = 192
        HEAD = 12
        HD = FEATS // HEAD
        B, N = (128, 197)
        key = jax.random.key(seed)
        k0, k1, k2 = jax.random.split(key, 3)
        x = jax.random.normal(k0, (B, N, FEATS), dtype=jnp.float32)
        W_qkv = jax.random.normal(k1, (HEAD, HD, 3 * HD), dtype=jnp.float32) * 0.05
        b_qkv = jnp.zeros((HEAD, 3 * HD), dtype=jnp.float32)
        W_out = jax.random.normal(k2, (FEATS, FEATS), dtype=jnp.float32) * 0.02
        b_out = jnp.zeros((FEATS,), dtype=jnp.float32)
        return {'x': x, 'W_qkv': W_qkv, 'b_qkv': b_qkv, 'W_out': W_out, 'b_out': b_out}
    _L1_attn_all = _L1_attn_setup()
    _L1_attn_in = {k: v for k, v in _L1_attn_all.items() if k in ('W_qkv', 'b_qkv', 'W_out', 'b_out')}
    del _L1_attn_all

    def _L1_ffn_setup():
        import jax, jax.numpy as jnp
        import numpy as np
        B, S, D_IN, D_HID, D_OUT = (32, 128, 192, 768, 192)
        key = jax.random.key(seed)
        k1, k2, k3, k4 = jax.random.split(key, 4)
        init_k = float(np.sqrt(1.0 / D_IN))
        init_k2 = float(np.sqrt(1.0 / D_HID))
        x = jax.random.normal(k1, (B, S, D_IN), dtype=jnp.float32)
        in_weight = jax.random.uniform(k2, (D_HID, D_IN), dtype=jnp.float32, minval=-init_k, maxval=init_k)
        in_bias = jax.random.uniform(k3, (D_HID,), dtype=jnp.float32, minval=-init_k, maxval=init_k)
        out_weight = jax.random.uniform(k4, (D_HID, D_OUT), dtype=jnp.float32, minval=-init_k2, maxval=init_k2)
        return {'x': x, 'in_weight': in_weight, 'in_bias': in_bias, 'out_weight': out_weight}
    _L1_ffn_all = _L1_ffn_setup()
    _L1_ffn_in = {k: v for k, v in _L1_ffn_all.items() if k in ('in_weight', 'in_bias', 'out_weight')}
    del _L1_ffn_all
    return {'x': x, 'L0_tok_dw_w': _L0_tok_in['dw_w'], 'L0_tok_pw_w': _L0_tok_in['pw_w'], 'L0_tok_pw_b': _L0_tok_in['pw_b'], 'L0_tok_ln_g': _L0_tok_in['ln_g'], 'L0_tok_ln_b': _L0_tok_in['ln_b'], 'L0_attn_e': _L0_attn_in['e'], 'L0_attn_p': _L0_attn_in['p'], 'L0_attn_ln_w': _L0_attn_in['ln_w'], 'L0_attn_W_qk': _L0_attn_in['W_qk'], 'L0_attn_W_o': _L0_attn_in['W_o'], 'L0_attn_wte': _L0_attn_in['wte'], 'L0_ffn_moe0_W1': _L0_ffn_in['moe0_W1'], 'L0_ffn_moe0_b1': _L0_ffn_in['moe0_b1'], 'L0_ffn_moe0_W2': _L0_ffn_in['moe0_W2'], 'L0_ffn_moe0_b2': _L0_ffn_in['moe0_b2'], 'L0_ffn_A1_W': _L0_ffn_in['A1_W'], 'L0_ffn_A1_b': _L0_ffn_in['A1_b'], 'L0_ffn_A2_W': _L0_ffn_in['A2_W'], 'L0_ffn_A2_b': _L0_ffn_in['A2_b'], 'L0_ffn_G_W': _L0_ffn_in['G_W'], 'L0_ffn_mids': _L0_ffn_in['mids'], 'L1_attn_W_qkv': _L1_attn_in['W_qkv'], 'L1_attn_b_qkv': _L1_attn_in['b_qkv'], 'L1_attn_W_out': _L1_attn_in['W_out'], 'L1_attn_b_out': _L1_attn_in['b_out'], 'L1_ffn_in_weight': _L1_ffn_in['in_weight'], 'L1_ffn_in_bias': _L1_ffn_in['in_bias'], 'L1_ffn_out_weight': _L1_ffn_in['out_weight']}

def reference(x, L0_tok_dw_w, L0_tok_pw_w, L0_tok_pw_b, L0_tok_ln_g, L0_tok_ln_b, L0_attn_e, L0_attn_p, L0_attn_ln_w, L0_attn_W_qk, L0_attn_W_o, L0_attn_wte, L0_ffn_moe0_W1, L0_ffn_moe0_b1, L0_ffn_moe0_W2, L0_ffn_moe0_b2, L0_ffn_A1_W, L0_ffn_A1_b, L0_ffn_A2_W, L0_ffn_A2_b, L0_ffn_G_W, L0_ffn_mids, L1_attn_W_qkv, L1_attn_b_qkv, L1_attn_W_out, L1_attn_b_out, L1_ffn_in_weight, L1_ffn_in_bias, L1_ffn_out_weight):
    import jax
    import jax.numpy as jnp

    def _L0_tok_ref(x, dw_w, pw_w, pw_b, ln_g, ln_b):
        import jax, jax.numpy as jnp
        from jax import lax
        import numpy as np
        DIM = 192
        K = 7
        PAD = K // 2
        EPS = 1e-06
        h = jnp.transpose(x, (0, 2, 1, 3))
        h = lax.conv_general_dilated(h, dw_w, window_strides=(1, 1), padding=((PAD, PAD), (0, 0)), dimension_numbers=('NCHW', 'OIHW', 'NCHW'), feature_group_count=DIM)
        h = h[..., 0]
        y = jnp.einsum('bdl,ed->ble', h, pw_w) + pw_b
        mu = jnp.mean(y, axis=-1, keepdims=True)
        var = jnp.mean(jnp.square(y - mu), axis=-1, keepdims=True)
        y = (y - mu) * lax.rsqrt(var + EPS) * ln_g + ln_b
        return jax.nn.relu(y)

    def _L0_attn_ref(x, e, p, ln_w, W_qk, W_o, wte):
        import jax, jax.numpy as jnp
        import numpy as np
        import math
        B, S, E = (2, 512, 192)
        H = 12
        V = 50257
        EPS = 1e-05

        def _layernorm(x, w):
            mu = jnp.mean(x, axis=-1, keepdims=True)
            var = jnp.mean(jnp.square(x - mu), axis=-1, keepdims=True)
            return (x - mu) * jax.lax.rsqrt(var + EPS) * w
        xb, sb, eb = x.shape
        xn = _layernorm(x, ln_w)
        avg_wte = jnp.mean(wte, axis=0)
        Q = xn[:, None, :, :] * W_qk[None, :, None, :]
        attn = jnp.einsum('bhse,bhte->bhst', Q, Q) / math.sqrt(eb)
        causal = jnp.tril(jnp.ones((sb, sb), dtype=bool))
        attn = jnp.where(causal[None, None], attn, -jnp.inf)
        attn = jax.nn.softmax(attn, axis=-1)
        Vv = xn[:, None, :, :] - avg_wte[None, None, None, :]
        out = jnp.einsum('bhst,bhte->bhse', attn, Vv)
        N_reg = 1.0 / jnp.arange(1, sb + 1, dtype=jnp.float32)
        out = out * N_reg[None, None, :, None]
        out = out.transpose(0, 2, 1, 3).reshape(xb, sb, H * eb)
        out = out @ W_o.T
        return out

    def _L0_ffn_ref(x, moe0_W1, moe0_b1, moe0_W2, moe0_b2, A1_W, A1_b, A2_W, A2_b, G_W, mids):
        import jax, jax.numpy as jnp
        import numpy as np
        GT0 = [[0, 1, 0, 0, 1, 0], [0, 1, 0, 0, 0, 1], [0, 0, 1, 0, 1, 0], [0, 0, 1, 0, 0, 1], [0, 0, 0, 1, 1, 0], [0, 0, 0, 1, 0, 1]]
        NCLS = 6
        K = 1

        def _expert_pairs():
            pairs = []
            for i in range(NCLS):
                p = [(j - 1, k - 1) for j in range(1, 6) for k in range(1, 6) if j != k and GT0[i][j] == 1 and (GT0[i][k] == 1)]
                pairs.append(p)
            return pairs
        PAIRS = _expert_pairs()
        B, P, D, H = (64, 64, 192, 768)

        def _gelu(t):
            return jax.nn.gelu(t, approximate=False)
        cls_tokens = x[:, :NCLS]
        patch_tokens = x[:, NCLS:]
        patch_out = _gelu(patch_tokens @ moe0_W1 + moe0_b1) @ moe0_W2 + moe0_b2
        cls_outs = []
        for i in range(NCLS):
            tok = cls_tokens[:, i]
            eouts = [_gelu(tok @ A1_W[a] + A1_b[a]) @ A2_W[c] + A2_b[c] for a, c in PAIRS[i]]
            out = jnp.stack(eouts, axis=-1)
            gate = jax.nn.softmax(tok @ G_W[i], axis=-1)
            thr = jnp.sort(gate, axis=-1)[..., -(K + 1)]
            mask = (gate > thr[..., None]).astype(gate.dtype)
            g = gate * mask
            g = g / jnp.clip(jnp.sum(g, axis=-1, keepdims=True), 1e-06)
            cls_outs.append(jnp.sum(out * g[:, None, :], axis=-1))
        cls_out = jnp.stack(cls_outs, axis=1)
        return jnp.concatenate([cls_out, patch_out], axis=1)

    def _L1_attn_ref(x, W_qkv, b_qkv, W_out, b_out):
        import jax, jax.numpy as jnp
        import numpy as np
        FEATS = 192
        HEAD = 12
        HD = FEATS // HEAD
        B, N = (128, 197)
        b, n, f = x.shape
        h, hd = (W_qkv.shape[0], W_qkv.shape[1])
        xh = x.reshape(b, n, h, hd)
        qkv = jnp.einsum('bnhd,hde->bnhe', xh, W_qkv) + b_qkv
        q, k, v = jnp.split(qkv, 3, axis=-1)
        scale = jnp.asarray(f, x.dtype) ** 0.5
        scores = jnp.einsum('bihd,bjhd->bhij', q, k) / scale
        p = jax.nn.softmax(scores, axis=-1)
        attn = jnp.einsum('bhij,bjhd->bihd', p, v)
        out = attn.reshape(b, n, f) @ W_out + b_out
        return out

    def _L1_ffn_ref(x, in_weight, in_bias, out_weight):
        import jax, jax.numpy as jnp
        import numpy as np
        B, S, D_IN, D_HID, D_OUT = (32, 128, 192, 768, 192)
        lead = x.shape[:-1]
        xt = x.reshape(-1, in_weight.shape[1])
        h = jax.nn.gelu(jnp.einsum('td,hd->th', xt, in_weight) + in_bias, approximate=False)
        out = jnp.einsum('th,ho->to', h, out_weight)
        return out.reshape(*lead, out_weight.shape[1])
    h = _L0_tok_ref(x, L0_tok_dw_w, L0_tok_pw_w, L0_tok_pw_b, L0_tok_ln_g, L0_tok_ln_b)
    h = h + _L0_attn_ref(_layernorm(h, axis=-1), L0_attn_e, L0_attn_p, L0_attn_ln_w, L0_attn_W_qk, L0_attn_W_o, L0_attn_wte)
    h = h + _L0_ffn_ref(_layernorm(h, axis=-1), L0_ffn_moe0_W1, L0_ffn_moe0_b1, L0_ffn_moe0_W2, L0_ffn_moe0_b2, L0_ffn_A1_W, L0_ffn_A1_b, L0_ffn_A2_W, L0_ffn_A2_b, L0_ffn_G_W, L0_ffn_mids)
    h = h + _L1_attn_ref(_layernorm(h, axis=-1), L1_attn_W_qkv, L1_attn_b_qkv, L1_attn_W_out, L1_attn_b_out)
    h = h + _L1_ffn_ref(_layernorm(h, axis=-1), L1_ffn_in_weight, L1_ffn_in_bias, L1_ffn_out_weight)
    return h

_drawn_inputs = setup_inputs


def setup_inputs(seed=0):
    import zlib

    import numpy as np

    out = dict(_drawn_inputs(seed))
    spreads = {'L0_tok_ln_g': (1.0, 0.2),
     'L0_tok_ln_b': (0.0, 0.1),
     'L0_attn_ln_w': (1.0, 0.6),
     'L0_ffn_moe0_b1': (0.0, 0.1),
     'L0_ffn_moe0_b2': (0.0, 0.1),
     'L0_ffn_A1_b': (0.0, 0.8),
     'L0_ffn_A2_b': (0.0, 0.277),
     'L1_attn_b_qkv': (0.0, 0.1),
     'L1_attn_b_out': (0.0, 0.1)}
    factors = {'L0_attn_W_qk': 8.0, 'L0_attn_wte': 8.0, 'L1_attn_W_qkv': 3.007, 'L1_ffn_in_bias': 2.851}
    for name, (base, spread) in spreads.items():
        noise = np.random.default_rng([zlib.crc32(name.encode()), seed]).standard_normal(out[name].shape)
        drawn = base * np.exp(spread * noise) if base else spread * noise
        out[name] = jnp.asarray(drawn.astype(out[name].dtype))
    for name, factor in factors.items():
        out[name] = (out[name] * factor).astype(out[name].dtype)
    return out
```

```python
from contextlib import ExitStack

import concourse.bass as bass
from concourse import mybir

F32 = mybir.dt.float32
F32R = mybir.dt.float32r
BF16 = mybir.dt.bfloat16
ALU = mybir.AluOpType
ACT = mybir.ActivationFunctionType
AX = mybir.AxisListType

B, L, D = 32, 128, 192
DC = D // 2
TAPS, HALO = 7, 3
LP = L + 2 * HALO
H = 12
HG = 4
BANK = 512
GW = H * D
VOCAB = 50257
WR = 8
WPIECE = VOCAB // (L * WR)
WTAIL = VOCAB - WPIECE * L * WR
EPS_TOK, EPS_LN = 1e-6, 1e-5


def f32(ap):
    return ap.bitcast(F32)


def mixing_phase(nc, io, keep):
    with ExitStack() as ctx:
        def sb(name, shape, dt=F32):
            return ctx.enter_context(nc.sbuf_tensor(name, shape, dt))

        def psum(name, shape, dt=F32):
            return ctx.enter_context(nc.psum_tensor(name, shape, dt))

        def sem(name):
            return ctx.enter_context(nc.semaphore(name))

        h, ident, nhalf, identr = keep["h"], keep["ident"], keep["nhalf"], keep["identr"]
        wte_acc, w5 = keep["wte_acc"], keep["w5"]

        x_pad = sb("x_pad", [DC, 2, B, LP])
        taps = sb("taps", [DC, 2, TAPS])
        pw = sb("pw", [DC + 1, 2, D])
        ln_g = sb("ln_g", [L, D])
        ln_b = sb("ln_b", [L, D])
        ln_w = sb("ln_w", [L, D])
        wqk = sb("wqk", [DC, 2, H])
        nreg = sb("nreg", [L, 1])
        identb = sb("identb", [L, L], BF16)
        maskf = sb("maskf", [L, L])
        maskb = sb("maskb", [L, HG, L], BF16)
        conv = [sb(f"conv{q}", [DC + 1, 2, L]) for q in range(2)]
        stats = sb("stats", [L, 2, 6])
        mv1 = sb("mv1", [L, 2, 2])
        mv2 = sb("mv2", [L, 2, 2])
        rstd1 = sb("rstd1", [L, 2])
        rstd2 = sb("rstd2", [L, 2])
        ytmp = sb("ytmp", [L, D])
        ypre = sb("ypre", [L, D])
        hc = [sb(f"hc{q}", [L, D]) for q in range(2)]
        xn = [sb(f"xn{q}", [L, 2 * D], F32R) for q in range(2)]
        xs = [sb(f"xs{q}", [L, 3, L], F32R) for q in range(2)]
        xt = [sb(f"xt{q}", [DC, 2, L]) for q in range(2)]
        ys = sb("ys", [DC, 2, H, L])
        nmax = sb("nmax", [L, 2, H])
        rsum = sb("rsum", [L, 2, H])
        rinv = sb("rinv", [L, 2, H])
        probs = sb("probs", [L, 2, H, L])
        probs_t = sb("probs_t", [L, H, L])
        g = [sb(f"g{q}", [L, GW]) for q in range(2)]
        wte = sb("wte", [L, 2, WR * D])

        ring = [psum(f"ring{i}", [L, BANK]) for i in range(3)]
        y_ps = psum("y_ps", [L, BANK])
        o_ps = psum("o_ps", [L, BANK])
        s_ps = psum("s_ps", [L, 3, BANK])

        first_in = sem("first_in")
        rest_in = sem("rest_in")
        w_in = sem("w_in")
        wte_in = [sem(f"wte_in{q}") for q in range(2)]
        halo_set = sem("halo_set")
        const_ready = sem("const_ready")
        wqk_sq = sem("wqk_sq")
        w_hi = sem("w_hi")
        w_lo = sem("w_lo")
        conv_ready = sem("conv_ready")
        conv_step = sem("conv_step")
        y_ready = sem("y_ready")
        y_bank_free = sem("y_bank_free")
        stats_step = sem("stats_step")
        ln1_stats = sem("ln1_stats")
        ln1_rstd = sem("ln1_rstd")
        ypre_ready = sem("ypre_ready")
        relu_ready = sem("relu_ready")
        ln2_stats = sem("ln2_stats")
        ln2_rstd = sem("ln2_rstd")
        hc_ready = sem("hc_ready")
        xn_hi = sem("xn_hi")
        xn_lo = sem("xn_lo")
        xs_in_bank = sem("xs_in_bank")
        xt_in_bank = sem("xt_in_bank")
        xs_ready = sem("xs_ready")
        xt_ready = sem("xt_ready")
        ys0_ready = sem("ys0_ready")
        ys1_ready = sem("ys1_ready")
        s_ready = sem("s_ready")
        nmax_ready = sem("nmax_ready")
        exp_ready = sem("exp_ready")
        rinv_step = sem("rinv_step")
        rinv_ready = sem("rinv_ready")
        probs_ready = sem("probs_ready")
        pt_in_bank = sem("pt_in_bank")
        g_in_bank = sem("g_in_bank")
        pv_ready = sem("pv_ready")
        h_added = sem("h_added")
        wte_added = sem("wte_added")
        bank_free = [sem(f"bank_free{i}") for i in range(3)]

        block = ctx.enter_context(nc.Block())

        x_v = io["x"].rearrange("(c p) b l -> p c b l", c=2)
        wo_v = io["w_o"]
        wte_v = io["wte"][0:WPIECE * L * WR, :].rearrange("(n p r) d -> n p (r d)", p=L, r=WR)
        WO_ROWS = ([(0, 128, 0)], [(128, 192, 0), (0, 64, 64)], [(64, 192, 0)])
        raw = [g[0][:, :], g[1][:, :], probs[:].rearrange("p a h l -> p (a h l)")[:, 0:GW]]
        G_BANK = (1, 2, 0, 1, 2)
        G_COLS = [(j * BANK, min((j + 1) * BANK, GW)) for j in range(5)]

        @block.sync
        def _(sp):
            for c in range(2):
                sp.dma_start(x_pad[:, c, 0:2, HALO:HALO + L], x_v[:, c, 0:2]).then_inc(first_in, 16)
            sp.dma_start(taps[:], io["dw_w"].rearrange("(c p) k -> p c k", c=2)).then_inc(first_in, 16)
            sp.dma_start(pw[0:DC], io["pw_w"].rearrange("(c p) e -> p c e", c=2)).then_inc(first_in, 16)
            sp.dma_start(pw[DC:DC + 1, 0, :], io["pw_b"]).then_inc(first_in, 16)
            sp.dma_start(ln_g[:], io["ln_g"].to_broadcast([L, D])).then_inc(first_in, 16)
            sp.dma_start(ln_b[:], io["ln_b"].to_broadcast([L, D])).then_inc(first_in, 16)
            sp.dma_start(ln_w[:], io["ln_w"].to_broadcast([L, D])).then_inc(first_in, 16)
            sp.dma_start(wqk[:], io["w_qk"].rearrange("(c p) h -> p c h", c=2)).then_inc(first_in, 16)
            sp.dma_start(nreg[:], io["nreg"]).then_inc(first_in, 16)
            sp.dma_start(ident[:], io["ident"]).then_inc(first_in, 16)
            sp.dma_start(maskf[:], io["mask"]).then_inc(first_in, 16)
            for i, parts in enumerate(WO_ROWS):
                for lo, hi, at in parts:
                    sp.dma_start(raw[i][at:at + hi - lo], wo_v[lo:hi]).then_inc(w_in, 16)
            for c in range(2):
                sp.dma_start(x_pad[:, c, 2:B, HALO:HALO + L], x_v[:, c, 2:B]).then_inc(rest_in, 16)
            sp.dma_start(wte_acc[:, 0, :], wte_v[0]).then_inc(wte_in[0], 16)
            for n in (1, 2):
                sp.dma_start(wte[:, n % 2], wte_v[n]).then_inc(wte_in[n % 2], 16)
            with sp.Fori(0, (WPIECE - 3) // 2) as it:
                for n0 in (3, 4):
                    sp.wait_ge(wte_added, it * 2 + (n0 - 2))
                    sp.dma_start(wte[:, n0 % 2], wte_v[it * 2 + n0]).then_inc(wte_in[n0 % 2], 16)

        @block.gpsimd
        def _(pool):
            def wte_piece(n):
                if n == 1:
                    pool.wait_ge(wte_in[0], 16)
                if n >= 2:
                    pool.wait_ge(wte_added, n - 1)
                pool.wait_ge(wte_in[n % 2], 16 * (n // 2 + 1))
                nc.gpsimd.tensor_tensor(wte_acc[:, 0, :], wte_acc[:, 0, :], wte[:, n % 2],
                                        ALU.add).then_inc(wte_added, 1)

            def rstd_1(k, q):
                pool.wait_ge(ln1_stats, k + 1)
                nc.gpsimd.tensor_tensor(rstd1[:, q:q + 1], mv1[:, q, 1:2], nhalf[:], ALU.pow).then_inc(ln1_rstd, 1)

            def rstd_2(k, q):
                pool.wait_ge(ln2_stats, k + 1)
                nc.gpsimd.tensor_tensor(rstd2[:, q:q + 1], mv2[:, q, 1:2], nhalf[:], ALU.pow).then_inc(ln2_rstd, 1)

            def scale_1(k, q):
                pool.wait_ge(xt_ready, k + 1)
                nc.gpsimd.tensor_tensor(ys[:, 1], xt[q][:, 1, None, :].to_broadcast([DC, H, L]),
                                        wqk[:, 1, :, None].to_broadcast([DC, H, L]), ALU.mult).then_inc(ys1_ready, 1)

            def normalise(k, q):
                pool.wait_ge(rinv_ready, k + 1)
                nc.gpsimd.tensor_tensor(probs[:, q], probs[:, q], rinv[:, q, :, None].to_broadcast([L, H, L]),
                                        ALU.mult).then_inc(probs_ready, 1)

            def step(k, q, pieces, ahead2, ahead1):
                for n in pieces:
                    wte_piece(n)
                if ahead2:
                    rstd_1(k + 2, q)
                if ahead1:
                    scale_1(k + 1, 1 - q)
                if ahead2:
                    rstd_2(k + 2, q)
                normalise(k, q)

            pool.wait_ge(halo_set, 5)
            for k in range(2):
                rstd_1(k, k)
                rstd_2(k, k)
            pool.wait_ge(wqk_sq, 2)
            scale_1(0, 0)
            pieces = list(range(1, WPIECE))
            step(0, 0, pieces[0:2], True, True)
            step(1, 1, pieces[2:3], True, True)
            first = pieces[3]
            with pool.Fori(0, 7) as it:
                for u in range(4):
                    k = it * 4 + (2 + u)
                    for j in ((0, 1), (2,), (3, 4), (5,))[u]:
                        n0 = first + j
                        pool.wait_ge(wte_added, it * 6 + (n0 - 1))
                        pool.wait_ge(wte_in[n0 % 2], it * 48 + 16 * ((n0 + 1) // 2 + (n0 % 2 == 0)))
                        nc.gpsimd.tensor_tensor(wte_acc[:, 0, :], wte_acc[:, 0, :], wte[:, n0 % 2],
                                                ALU.add).then_inc(wte_added, 1)
                    step(k, u % 2, (), True, True)
            done = first + 42
            rest = list(range(done, WPIECE))
            step(30, 0, rest[0:2], False, True)
            step(31, 1, rest[2:], False, False)

        @block.vector
        def _(dve):
            def convolve(k, q):
                for c in range(2):
                    for t in range(TAPS):
                        src = x_pad[:, c, k, t:t + L]
                        dst = conv[q][0:DC, c, :]
                        w = taps[:, c, t:t + 1]
                        if t == 0:
                            ins = nc.vector.tensor_scalar(dst, src, w, None, ALU.mult)
                        else:
                            dve.wait_ge(conv_step, k * (2 * (TAPS - 1)) + (c * (TAPS - 1) + t))
                            ins = nc.vector.scalar_tensor_tensor(dst, src, w, dst, ALU.mult, ALU.add)
                        if t < TAPS - 1:
                            ins.then_inc(conv_step, 1)
                        else:
                            ins.then_inc(conv_ready, 1)

            def ln1_a(k, q):
                dve.wait_ge(y_ready, k + 1)
                nc.vector.bn_stats(stats[:, 0], y_ps[:, 0:D]).then_inc(stats_step, 1)
                dve.drain()
                nc.vector.bn_aggr(mv1[:, q], stats[:, 0]).then_inc(stats_step, 1)
                dve.wait_ge(stats_step, k * 4 + 2)
                nc.vector.tensor_scalar(mv1[:, q, 1:2], mv1[:, q, 1:2], EPS_TOK, None, ALU.add).then_inc(ln1_stats, 1)

            def ln1_b(k, q):
                dve.wait_ge(ln1_rstd, k + 1)
                nc.vector.scalar_tensor_tensor(ytmp[:], y_ps[:, 0:D], mv1[:, q, 0:1], ln_g[:], ALU.subtract,
                                               ALU.mult).then_inc(y_bank_free, 1)
                dve.wait_ge(y_bank_free, k + 1)
                nc.vector.scalar_tensor_tensor(ypre[:], ytmp[:], rstd1[:, q:q + 1], ln_b[:], ALU.mult,
                                               ALU.add).then_inc(ypre_ready, 1)

            def ln2_a(k, q):
                dve.wait_ge(relu_ready, k + 1)
                nc.vector.bn_stats(stats[:, 1], h[:, k, :]).then_inc(stats_step, 1)
                dve.drain()
                nc.vector.bn_aggr(mv2[:, q], stats[:, 1]).then_inc(stats_step, 1)
                dve.wait_ge(stats_step, k * 4 + 4)
                nc.vector.tensor_scalar(mv2[:, q, 1:2], mv2[:, q, 1:2], 1.0 + EPS_LN, EPS_LN * EPS_LN, ALU.mult,
                                        ALU.add).then_inc(ln2_stats, 1)

            def ln2_b(k, q):
                dve.wait_ge(ln2_rstd, k + 1)
                nc.vector.scalar_tensor_tensor(hc[q][:], h[:, k, :], mv2[:, q, 0:1], ln_w[:], ALU.subtract,
                                               ALU.mult).then_inc(hc_ready, 1)

            def low_part(k, q):
                dve.wait_ge(xn_hi, k + 1)
                nc.vector.scalar_tensor_tensor(xn[q][:, D:2 * D], hc[q][:], rstd2[:, q:q + 1], f32(xn[q][:, 0:D]),
                                               ALU.mult, ALU.subtract).then_inc(xn_lo, 1)

            def take_xs(k, q):
                dve.wait_ge(xs_in_bank, k + 1)
                nc.vector.tensor_copy(xs[q][:].rearrange("p a b -> p (a b)"), ring[0][:, 0:3 * L]).then_inc(bank_free[0], 1)

            def scale_0(k, q):
                dve.wait_ge(xt_ready, k + 1)
                nc.vector.tensor_tensor(ys[:, 0], xt[q][:, 0, None, :].to_broadcast([DC, H, L]),
                                        wqk[:, 0, :, None].to_broadcast([DC, H, L]), ALU.mult).then_inc(ys0_ready, 1)

            def row_max(k, q):
                dve.wait_ge(s_ready, k + 1)
                nc.vector.tensor_reduce(nmax[:, q, :], s_ps[:].rearrange("p b (h l) -> p (b h) l", l=L), AX.X, ALU.max,
                                        negate=True).then_inc(nmax_ready, 1)

            def take_probs_t(k, j):
                dve.wait_ge(pt_in_bank, k * 3 + (j + 1))
                nc.vector.tensor_copy(probs_t[:, HG * j:HG * j + HG, :].rearrange("p h l -> p (h l)"),
                                      ring[j][:]).then_inc(bank_free[j], 1)

            def inverse_sum(k, q):
                dve.wait_ge(exp_ready, k + 1)
                nc.vector.reciprocal(rinv[:, q, :], rsum[:, q, :]).then_inc(rinv_step, 1)
                dve.wait_ge(rinv_step, k + 1)
                nc.vector.tensor_scalar(rinv[:, q, :], rinv[:, q, :], nreg[:], None, ALU.mult).then_inc(rinv_ready, 1)

            def add_to_h(k):
                dve.wait_ge(pv_ready, k + 1)
                nc.vector.tensor_tensor(h[:, k, :], o_ps[:, 0:D], h[:, k, :], ALU.add).then_inc(h_added, 1)

            def step(k, q, ahead2, ahead1, back1, back2):
                if ahead2:
                    convolve(k + 2, q)
                if back2:
                    add_to_h(k - 2)
                row_max(k, q)
                if ahead2:
                    ln1_a(k + 2, q)
                if back1:
                    take_probs_t(k - 1, 0)
                    take_probs_t(k - 1, 1)
                if ahead1:
                    take_xs(k + 1, 1 - q)
                    scale_0(k + 1, 1 - q)
                if ahead2:
                    ln1_b(k + 2, q)
                    ln2_a(k + 2, q)
                    ln2_b(k + 2, q)
                inverse_sum(k, q)
                if ahead2:
                    low_part(k + 2, q)

            nc.vector.memset(nhalf[:], -0.5).then_inc(halo_set, 1)
            for q in range(2):
                nc.vector.memset(conv[q][DC:DC + 1, 0, :], 1.0).then_inc(halo_set, 1)
            nc.vector.memset(x_pad[:, :, :, 0:HALO], 0.0).then_inc(halo_set, 1)
            nc.vector.memset(x_pad[:, :, :, HALO + L:LP], 0.0).then_inc(halo_set, 1)
            dve.wait_ge(first_in, 16 * 12)
            dve.wait_ge(halo_set, 5)
            convolve(0, 0)
            convolve(1, 1)
            nc.vector.tensor_copy(identr[:], ident[:]).then_inc(const_ready, 1)
            nc.vector.tensor_copy(identb[:], ident[:]).then_inc(const_ready, 1)
            nc.vector.tensor_copy(maskb[:], maskf[:, None, :].to_broadcast([L, HG, L])).then_inc(const_ready, 1)
            nc.vector.tensor_tensor(wqk[:], wqk[:], wqk[:], ALU.mult).then_inc(wqk_sq, 1)
            dve.wait_ge(wqk_sq, 1)
            nc.vector.tensor_scalar(wqk[:], wqk[:], float(D) ** -0.5, None, ALU.mult).then_inc(wqk_sq, 1)
            for k in range(2):
                ln1_a(k, k)
                ln1_b(k, k)
                ln2_a(k, k)
                ln2_b(k, k)
                low_part(k, k)
            dve.wait_ge(wqk_sq, 2)
            take_xs(0, 0)
            scale_0(0, 0)
            dve.wait_ge(w_in, 16 * 4)
            dve.wait_ge(w_hi, 3)
            nc.vector.tensor_tensor(w5[:, 3, :], raw[0], f32(w5[:, 0, :]), ALU.subtract).then_inc(w_lo, 1)
            nc.vector.tensor_tensor(w5[0:64, 4, :], raw[1][0:64], f32(w5[0:64, 1, :]), ALU.subtract).then_inc(w_lo, 1)
            dve.wait_ge(rest_in, 32)
            step(0, 0, True, True, False, False)
            step(1, 1, True, True, True, False)
            with dve.Fori(0, 14) as it:
                for q in range(2):
                    step(it * 2 + (2 + q), q, True, True, True, True)
            step(30, 0, False, True, True, True)
            step(31, 1, False, False, True, True)
            take_probs_t(31, 0)
            take_probs_t(31, 1)
            add_to_h(30)
            add_to_h(31)

        @block.scalar
        def _(act):
            def relu(k):
                act.wait_ge(ypre_ready, k + 1)
                nc.scalar.activation(h[:, k, :], ypre[:], ACT.Relu).then_inc(relu_ready, 1)

            def high_part(k, q):
                act.wait_ge(hc_ready, k + 1)
                nc.scalar.activation(xn[q][:, 0:D], hc[q][:], ACT.Identity, scale=rstd2[:, q:q + 1]).then_inc(xn_hi, 1)

            def take_xt(k, q):
                act.wait_ge(xt_in_bank, k + 1)
                nc.scalar.activation(xt[q][:].rearrange("p c l -> p (c l)"), o_ps[0:DC, 0:2 * L],
                                     ACT.Copy).then_inc(xt_ready, 1)

            def take_probs_t(k):
                act.wait_ge(pt_in_bank, k * 3 + 3)
                nc.scalar.activation(probs_t[:, 2 * HG:H, :].rearrange("p h l -> p (h l)"), ring[2][:],
                                     ACT.Copy).then_inc(bank_free[2], 1)

            def exps(k, q, heads):
                assert heads
                for i in heads:
                    ins = nc.scalar.activation(probs[:, q, i, :], s_ps[:, i // HG, L * (i % HG):L * (i % HG) + L],
                                               ACT.Exp, bias=nmax[:, q, i:i + 1], accum_out=rsum[:, q, i:i + 1])
                if heads[-1] == H - 1:
                    ins.then_inc(exp_ready, 1)

            def take_g(k, q, j):
                lo, hi = G_COLS[j]
                act.wait_ge(g_in_bank, k * 5 + (j + 1))
                nc.scalar.activation(g[q][:, lo:hi], ring[G_BANK[j]][:, 0:hi - lo],
                                     ACT.Copy).then_inc(bank_free[G_BANK[j]], 1)

            def step(k, q, ahead2, ahead1, back1):
                if back1:
                    take_probs_t(k - 1)
                if ahead1:
                    take_xt(k + 1, 1 - q)
                act.wait_ge(nmax_ready, k + 1)
                exps(k, q, (0, 1))
                for j in range(5):
                    take_g(k, q, j)
                    exps(k, q, (2 + 2 * j, 3 + 2 * j))
                    if ahead2 and j == 1:
                        relu(k + 2)
                if ahead2:
                    high_part(k + 2, q)

            act.wait_ge(w_in, 16 * 4)
            for i in range(3):
                nc.scalar.activation(w5[:, i, :], raw[i], ACT.Copy).then_inc(w_hi, 1)
            for k in range(2):
                relu(k)
                high_part(k, k)
            take_xt(0, 0)
            act.wait_ge(w_lo, 2)
            act.wait_ge(w_hi, 3)
            step(0, 0, True, True, False)
            step(1, 1, True, True, True)
            with act.Fori(0, 14) as it:
                for q in range(2):
                    step(it * 2 + (2 + q), q, True, True, True)
            step(30, 0, False, True, True)
            step(31, 1, False, False, True)
            take_probs_t(31)

        @block.tensor
        def _(pe):
            def pointwise(k, q):
                pe.wait_ge(conv_ready, k * 2 + 2)
                if not (isinstance(k, int) and k == 0):
                    pe.wait_ge(y_bank_free, k)
                nc.tensor.matmul(y_ps[:, 0:D], conv[q][:, 0, :], pw[:, 0, :], start=True, stop=False)
                nc.tensor.matmul(y_ps[:, 0:D], conv[q][0:DC, 1, :], pw[0:DC, 1, :], start=False,
                                 stop=True).then_inc(y_ready, 1)

            def wait_bank(i, n):
                if not (isinstance(n, int) and n <= 0):
                    pe.wait_ge(bank_free[i], n)

            def transpose_xn(k, q, used, back2):
                pe.wait_ge(xn_lo, k + 1)
                wait_bank(0, used)
                for i in range(3):
                    ins = nc.tensor.transpose(ring[0][:, L * i:L * i + L].bitcast(F32R), xn[q][:, L * i:L * i + L],
                                              identr[:])
                ins.then_inc(xs_in_bank, 1)
                if back2:
                    pe.wait_ge(h_added, k - 2)
                for c in range(2):
                    nc.tensor.matmul(o_ps[0:DC, L * c:L * c + L], xn[q][:, DC * c:DC * c + DC], identr[:],
                                     start=(c == 0), stop=False, skip_group_check=True)
                    ins = nc.tensor.matmul(o_ps[0:DC, L * c:L * c + L], xn[q][:, D + DC * c:D + DC * c + DC],
                                           identr[:], start=False, stop=(c == 1), skip_group_check=True)
                ins.then_inc(xt_in_bank, 1)

            def scores(k, q):
                pe.wait_ge(ys0_ready, k + 1)
                pe.wait_ge(ys1_ready, k + 1)
                if not (isinstance(k, int) and k == 0):
                    pe.wait_ge(exp_ready, k)
                for j in range(3):
                    nc.tensor.matmul(s_ps[:, j, :], identb[:], maskb[:].rearrange("p h l -> p (h l)"), start=True,
                                     stop=False)
                    for c in range(2):
                        ins = nc.tensor.matmul(s_ps[:, j, :], xt[q][:, c, :],
                                               ys[:, c, HG * j:HG * j + HG, :].rearrange("p h l -> p (h l)"),
                                               start=False, stop=(c == 1))
                ins.then_inc(s_ready, 1)

            def transpose_probs(k, q, used):
                pe.wait_ge(probs_ready, k + 1)
                for j in range(3):
                    wait_bank(j, used[j])
                    for i in range(HG):
                        ins = nc.tensor.transpose(ring[j][:, L * i:L * i + L], probs[:, q, HG * j + i, :], ident[:])
                    ins.then_inc(pt_in_bank, 1)

            def value_products(k, q, used, start):
                pe.wait_ge(bank_free[0], start)
                stack = [xs[q][:, i, :] for i in (0, 1, 2, 0)]
                for j in range(5):
                    lo, hi = G_COLS[j]
                    b = G_BANK[j]
                    wait_bank(b, used[b] + (1 if j >= 3 else 0))
                    for i in range(4):
                        nc.tensor.matmul(ring[b][:, 0:hi - lo], stack[i], w5[:, i, lo:hi], start=(i == 0), stop=False)
                    nc.tensor.matmul(ring[b][:, 0:hi - lo], xs[q][0:64, 1, :], w5[0:64, 4, lo:hi], start=False,
                                     stop=True).then_inc(g_in_bank, 1)

            def attend(k, q):
                for j in range(H):
                    ins = nc.tensor.matmul(o_ps[:, 0:D], probs_t[:, j, :], g[q][:, D * j:D * j + D], start=(j == 0),
                                           stop=(j == H - 1))
                ins.then_inc(pv_ready, 1)

            def step(k, q, ahead2, ahead1, back1, b0, b1, b2, after):
                scores(k, q)
                if ahead2:
                    pointwise(k + 2, q)
                n = 0
                if back1:
                    transpose_probs(k - 1, 1 - q, (b0, b1, b2))
                    n = 1
                m = 0
                if ahead1:
                    transpose_xn(k + 1, 1 - q, b0 + n, after)
                    m = 1
                value_products(k, q, (b0 + n + m, b1 + n, b2 + n), b0)
                if back1:
                    if ahead1:
                        pe.wait_ge(xt_ready, k + 2)
                    else:
                        pe.wait_ge(h_added, k - 1)
                    attend(k - 1, 1 - q)

            pe.wait_ge(first_in, 16 * 12)
            pointwise(0, 0)
            pointwise(1, 1)
            pe.wait_ge(const_ready, 3)
            transpose_xn(0, 0, 0, False)
            pe.wait_ge(w_lo, 2)
            step(0, 0, True, True, False, 1, 0, 0, False)
            step(1, 1, True, True, True, 3, 2, 2, False)
            with pe.Fori(0, 14) as it:
                for q in range(2):
                    k = it * 2 + (2 + q)
                    step(k, q, True, True, True, it * 6 + (6 + 3 * q), it * 6 + (5 + 3 * q), it * 6 + (5 + 3 * q), True)
            step(30, 0, False, True, True, 90, 89, 89, True)
            step(31, 1, False, False, True, 93, 92, 92, True)
            transpose_probs(31, 1, (95, 95, 95))
            pe.wait_ge(bank_free[0], 96)
            pe.wait_ge(bank_free[1], 96)
            pe.wait_ge(bank_free[2], 96)
            pe.wait_ge(h_added, 31)
            attend(31, 1)


def wte_phase(nc, io, keep):
    with ExitStack() as ctx:
        def sb(name, shape, dt=F32):
            return ctx.enter_context(nc.sbuf_tensor(name, shape, dt))

        def sem(name):
            return ctx.enter_context(nc.semaphore(name))

        h, wte_acc, w5 = keep["h"], keep["wte_acc"], keep["w5"]
        tail = sb("wte_tail", [WTAIL, D])
        share = sb("share", [L, 1])
        nneg = sb("nneg", [L, 1])
        avg = sb("avg", [L, 3, L])
        fix = sb("fix", [L, D])
        avg_ps = ctx.enter_context(nc.psum_tensor("avg_ps", [L, BANK], F32))
        fix_ps = ctx.enter_context(nc.psum_tensor("fix_ps", [L, BANK], F32))
        tail_in = sem("tail_in")
        share_set = sem("share_set")
        avg_ready = sem("avg_ready")
        avg_taken = sem("avg_taken")
        nneg_ready = sem("nneg_ready")
        fix_ready = sem("fix_ready")
        fix_taken = sem("fix_taken")
        h_fixed = sem("h_fixed")
        block = ctx.enter_context(nc.Block())
        PARTS = ((0, 128), (64, 192), (128, 192))
        DVE_IMAGES = 21

        @block.sync
        def _(sp):
            sp.dma_start(tail[:], io["wte"][VOCAB - WTAIL:VOCAB, :]).then_inc(tail_in, 16)
            sp.dma_start(nneg[:], io["nreg"]).then_inc(tail_in, 16)
            sp.wait_ge(tail_in, 32)

        @block.tensor
        def _(pe):
            pe.wait_ge(share_set, 1)
            pe.wait_ge(tail_in, 32)
            for i, (lo, hi) in enumerate(PARTS):
                out = avg_ps[0:hi - lo, i:i + 1]
                for r in range(WR):
                    nc.tensor.matmul(out, wte_acc[:, 0, r * D + lo:r * D + hi], share[:], start=(r == 0), stop=False,
                                     skip_group_check=True)
                ins = nc.tensor.matmul(out, tail[:, lo:hi], share[0:WTAIL], start=False, stop=True,
                                       skip_group_check=True)
            ins.then_inc(avg_ready, 1)
            pe.wait_ge(avg_taken, 4)
            for j in range(H):
                cols = slice(D * j, D * j + D)
                nc.tensor.matmul(fix_ps[:, 0:D], avg[:, 0, :], f32(w5[:, 0, cols]), start=(j == 0), stop=False)
                nc.tensor.matmul(fix_ps[:, 0:D], avg[:, 1, :], f32(w5[:, 2, cols]), start=False, stop=False)
                nc.tensor.matmul(fix_ps[:, 0:D], avg[:, 0, :], f32(w5[:, 3, cols]), start=False, stop=False)
                ins = nc.tensor.matmul(fix_ps[:, 0:D], avg[0:64, 2, :], f32(w5[0:64, 4, cols]), start=False,
                                       stop=(j == H - 1))
            ins.then_inc(fix_ready, 1)

        @block.vector
        def _(dve):
            nc.vector.memset(share[:], 1.0 / VOCAB).then_inc(share_set, 1)
            nc.vector.memset(avg[0:64, 1, :], 0.0).then_inc(avg_taken, 1)
            dve.wait_ge(avg_ready, 1)
            nc.vector.tensor_copy(avg[:, 0, :], avg_ps[:, 0:1].to_broadcast([L, L])).then_inc(avg_taken, 1)
            nc.vector.tensor_copy(avg[64:128, 1, :], avg_ps[64:128, 1:2].to_broadcast([64, L])).then_inc(avg_taken, 1)
            nc.vector.tensor_copy(avg[0:64, 2, :], avg_ps[0:64, 2:3].to_broadcast([64, L])).then_inc(avg_taken, 1)
            dve.wait_ge(tail_in, 32)
            nc.vector.tensor_scalar(nneg[:], nneg[:], -1.0, None, ALU.mult).then_inc(nneg_ready, 1)
            dve.wait_ge(nneg_ready, 1)
            dve.wait_ge(fix_ready, 1)
            nc.vector.tensor_scalar(fix[:], fix_ps[:, 0:D], nneg[:], None, ALU.mult).then_inc(fix_taken, 1)
            dve.wait_ge(fix_taken, 1)
            nc.vector.tensor_tensor(h[:, 0:DVE_IMAGES, :], h[:, 0:DVE_IMAGES, :],
                                    fix[:, None, :].to_broadcast([L, DVE_IMAGES, D]), ALU.add).then_inc(h_fixed, 1)

        @block.gpsimd
        def _(pool):
            pool.wait_ge(fix_taken, 1)
            nc.gpsimd.tensor_tensor(h[:, DVE_IMAGES:B, :], h[:, DVE_IMAGES:B, :],
                                    fix[:, None, :].to_broadcast([L, B - DVE_IMAGES, D]), ALU.add).then_inc(h_fixed, 1)


HID = 768
HJ = HID // 128
PAIR = 2
NPAIR = B // PAIR
NCLS = 6
NEXP = 5
STACKS = ([(0, 128, 0)], [(128, 192, 0), (0, 64, 64)], [(64, 192, 0)])


def feed_forward_phase(nc, io, keep, layer):
    with ExitStack() as ctx:
        def sb(name, shape, dt=F32):
            return ctx.enter_context(nc.sbuf_tensor(f"{name}_f{layer}", shape, dt))

        def psum(name, shape, dt=F32):
            return ctx.enter_context(nc.psum_tensor(f"{name}_f{layer}", shape, dt))

        def sem(name):
            return ctx.enter_context(nc.semaphore(f"{name}_f{layer}"))

        h, ident, nhalf, identr = keep["h"], keep["ident"], keep["nhalf"], keep["identr"]
        first = layer == 0
        T2 = PAIR * L

        raw1 = sb("raw1", [128, 3, HID])
        raw2 = sb("raw2", [128, HJ, D])
        w1 = sb("w1", [128, 5, HID], F32R)
        w2 = sb("w2", [128, 2, HJ, D], F32R)
        b1 = sb("b1", [128, HJ])
        xf = sb("xf", [L, PAIR, D])
        xn = [sb(f"xn{q}", [L, PAIR, 2 * D], F32R) for q in range(2)]
        xs = [sb(f"xs{q}", [128, 3, T2], F32R) for q in range(2)]
        gf = sb("gf", [128, HJ, T2])
        gh = [sb(f"gh{q}", [128, HJ, T2], F32R) for q in range(2)]
        gl = [sb(f"gl{q}", [128, HJ, T2], F32R) for q in range(2)]
        stats = sb("stats", [L, PAIR, 6])
        mv = sb("mv", [L, 2, PAIR, 2])
        rstd = sb("rstd", [L, 2, PAIR])
        if first:
            b2f = sb("b2f", [1, D])
            b2 = sb("b2", [1, 2, D], F32R)
            ones = sb("ones", [1, L], F32R)

        x_ps = [psum(f"x_ps{i}", [128, BANK]) for i in range(PAIR)]
        hid_ps = [psum(f"hid_ps{i}", [128, BANK]) for i in range(3)]
        out_ps = [psum(f"out_ps{q}", [L, BANK]) for q in range(2)]

        w_in = sem("w_in")
        w_split = sem("w_split")
        stats_ready = sem("stats_ready")
        stats_step = sem("stats_step")
        rstd_ready = sem("rstd_ready")
        xf_ready = sem("xf_ready")
        xf_used = sem("xf_used")
        xn_hi = sem("xn_hi")
        xn_lo = sem("xn_lo")
        x_in_bank = sem("x_in_bank")
        xs_ready = sem("xs_ready")
        hid_in_bank = sem("hid_in_bank")
        gelu_ready = sem("gelu_ready")
        g_hi = sem("g_hi")
        g_lo = sem("g_lo")
        out_ready = sem("out_ready")
        h_added = sem("h_added")
        stored = sem("stored")
        LOADS = 7 if first else 6
        SPLITS = 8 if first else 5
        cls = keep["cls"] if first else None
        if first:
            tok_in = sem("tok_in")
            cls_in = sem("cls_in")

        block = ctx.enter_context(nc.Block())

        @block.sync
        def _(sp):
            name = "ffn0" if first else "ffn1"
            for i, parts in enumerate(STACKS):
                for lo, hi, at in parts:
                    sp.dma_start(raw1[at:at + hi - lo, i, :], io[f"{name}_w1"][lo:hi]).then_inc(w_in, 16)
            sp.dma_start(raw2[:], io[f"{name}_w2"].rearrange("(j p) d -> p j d", p=128)).then_inc(w_in, 16)
            sp.dma_start(b1[:], io[f"{name}_b1"]).then_inc(w_in, 16)
            if first:
                sp.dma_start(b2f[:], io["ffn0_b2"]).then_inc(w_in, 16)
                for i in range(NCLS):
                    q, t = i // 2, i % 2
                    sp.dma_start(cls["tok"][B * q:B * q + B, t, :], h[i:i + 1, :, :]).then_inc(tok_in, 16)
                for e in range(NEXP):
                    sp.dma_start(cls["a1"][:, e], io["a1"][e].rearrange("(c p) f -> p c f", c=2)).then_inc(cls_in, 16)
                    sp.dma_start(cls["a2"][:, e], io["a2"][e].rearrange("(j p) d -> p j d", p=128)).then_inc(cls_in, 16)
                sp.dma_start(cls["a1b"][:], io["a1b"]).then_inc(cls_in, 16)
                sp.dma_start(cls["gw"][:], io["gw"].rearrange("(c p) n -> p c n", c=2)).then_inc(cls_in, 16)
                for t in range(2):
                    sp.dma_start(cls["b_high"][:, t, :], io["a2b"][3 + t:4 + t].to_broadcast([3 * B, D])).then_inc(cls_in, 16)
                for q in range(3):
                    sp.dma_start(cls["b_low"][B * q:B * q + B, :], io["a2b"][q:q + 1].to_broadcast([B, D])).then_inc(cls_in, 16)
                sp.wait_ge(cls_in, 16 * (2 * NEXP + 7))
            else:
                out_v = io["out"].rearrange("b l d -> l b d")
                with sp.Fori(0, NPAIR) as u:
                    sp.wait_ge(h_added, u + 1)
                    sp.dma_start(out_v[:, bass.ds(u * PAIR, PAIR), :], h[:, bass.ds(u * PAIR, PAIR), :]).then_inc(stored, 16)
                sp.wait_ge(stored, 16 * NPAIR)

        @block.gpsimd
        def _(pool):
            def rstd_of(u, q):
                pool.wait_ge(stats_ready, u + 1)
                nc.gpsimd.tensor_tensor(rstd[:, q, :], mv[:, q, :, 1], nhalf[:].to_broadcast([L, PAIR]),
                                        ALU.pow).then_inc(rstd_ready, 1)

            rstd_of(0, 0)
            rstd_of(1, 1)
            with pool.Fori(0, (NPAIR - 2) // 2) as it:
                for q in range(2):
                    rstd_of(it * 2 + (2 + q), q)

        @block.vector
        def _(dve):
            def normalise(u, q):
                for i in range(PAIR):
                    nc.vector.bn_stats(stats[:, i], h[:, u * PAIR + i, :])
                    dve.drain()
                    ins = nc.vector.bn_aggr(mv[:, q, i], stats[:, i])
                ins.then_inc(stats_step, 1)
                dve.wait_ge(stats_step, u + 1)
                nc.vector.tensor_scalar(mv[:, q, :, 1], mv[:, q, :, 1], EPS_LN, None, ALU.add).then_inc(stats_ready, 1)

            def centre(u, q):
                dve.wait_ge(rstd_ready, u + 1)
                for i in range(PAIR):
                    nc.vector.tensor_scalar(xf[:, i, :], h[:, u * PAIR + i, :], mv[:, q, i, 0:1], rstd[:, q, i:i + 1],
                                            ALU.subtract, ALU.mult).then_inc(xf_ready, 1)

            def low_part(u, q):
                dve.wait_ge(xn_hi, u + 1)
                nc.vector.tensor_tensor(xn[q][:, :, D:2 * D], xf[:], f32(xn[q][:, :, 0:D]),
                                        ALU.subtract).then_inc(xn_lo, 1)
                dve.wait_ge(xn_lo, u + 1)

            def take_xs(u, q):
                for i in range(PAIR):
                    dve.wait_ge(x_in_bank, u * PAIR + (i + 1))
                    nc.vector.tensor_copy(xs[q][:, :, L * i:L * i + L],
                                          x_ps[i][:, 0:3 * L].rearrange("p (s l) -> p s l", l=L)).then_inc(xs_ready, 1)

            def low_gelu(u, q):
                dve.wait_ge(g_hi, u + 1)
                nc.vector.tensor_tensor(gl[q][:], gf[:], f32(gh[q][:]), ALU.subtract).then_inc(g_lo, 1)

            def add_to_h(u, q):
                dve.wait_ge(out_ready, u + 1)
                hp = h[:, bass.ds(u * PAIR, PAIR), :] if not isinstance(u, int) else h[:, u * PAIR:u * PAIR + PAIR, :]
                nc.vector.tensor_tensor(hp, out_ps[q][:, 0:PAIR * D].rearrange("p (i d) -> p i d", i=PAIR), hp,
                                        ALU.add).then_inc(h_added, 1)

            def step(u, q, ahead3, ahead2, ahead1, back1):
                if ahead2:
                    take_xs(u + 2, q)
                if back1:
                    add_to_h(u - 1, 1 - q)
                if ahead3:
                    normalise(u + 3, 1 - q)
                if ahead1:
                    low_gelu(u + 1, 1 - q)
                if ahead3:
                    centre(u + 3, 1 - q)
                    low_part(u + 3, 1 - q)

            dve.wait_ge(w_in, 16 * LOADS)
            for u in range(3):
                if u == 2:
                    take_xs(0, 0)
                normalise(u, u % 2)
                centre(u, u % 2)
                low_part(u, u % 2)
                if u == 0:
                    nc.vector.tensor_copy(w1[:, 0:3, :], raw1[:]).then_inc(w_split, 1)
                    dve.wait_ge(w_split, 1)
                    nc.vector.tensor_tensor(w1[:, 3, :], raw1[:, 0, :], f32(w1[:, 0, :]),
                                            ALU.subtract).then_inc(w_split, 1)
                    nc.vector.tensor_tensor(w1[0:64, 4, :], raw1[0:64, 1, :], f32(w1[0:64, 1, :]),
                                            ALU.subtract).then_inc(w_split, 1)
                if u == 1:
                    nc.vector.tensor_copy(w2[:, 0], raw2[:]).then_inc(w_split, 1)
                    dve.wait_ge(w_split, 4)
                    nc.vector.tensor_tensor(w2[:, 1], raw2[:], f32(w2[:, 0]), ALU.subtract).then_inc(w_split, 1)
                    if first:
                        nc.vector.tensor_copy(b2[:, 0], b2f[:]).then_inc(w_split, 1)
                        dve.wait_ge(w_split, 6)
                        nc.vector.tensor_tensor(b2[:, 1], b2f[:], f32(b2[:, 0]), ALU.subtract).then_inc(w_split, 1)
                        nc.vector.tensor_scalar(ones[:], ident[0:1, :], 0.0, 1.0, ALU.mult, ALU.add).then_inc(w_split, 1)
            take_xs(1, 1)
            low_gelu(0, 0)
            if first:
                dve.wait_ge(tok_in, 16 * NCLS)
            step(0, 0, True, True, True, False)
            step(1, 1, True, True, True, True)
            with dve.Fori(0, (NPAIR - 6) // 2) as it:
                for q in range(2):
                    step(it * 2 + (2 + q), q, True, True, True, True)
            for u in range(NPAIR - 4, NPAIR):
                step(u, u % 2, u + 3 < NPAIR, u + 2 < NPAIR, u + 1 < NPAIR, True)
            add_to_h(NPAIR - 1, (NPAIR - 1) % 2)

        @block.scalar
        def _(act):
            def high_part(u, q):
                act.wait_ge(xf_ready, u * PAIR + PAIR)
                nc.scalar.activation(xn[q][:, :, 0:D], xf[:], ACT.Copy).then_inc(xn_hi, 1)

            def high_gelu(u, q):
                act.wait_ge(gelu_ready, u * 3 + 3)
                nc.scalar.activation(gh[q][:], gf[:], ACT.Copy).then_inc(g_hi, 1)

            def gelu(u):
                for i in range(3):
                    act.wait_ge(hid_in_bank, u * 3 + (i + 1))
                    if i == 0 and not (isinstance(u, int) and u == 0):
                        act.wait_ge(g_lo, u)
                    for j in range(2):
                        c = 2 * i + j
                        ins = nc.scalar.activation(gf[:, c, :], hid_ps[i][:, T2 * j:T2 * j + T2], ACT.Gelu,
                                                   bias=b1[:, c:c + 1])
                    ins.then_inc(gelu_ready, 1)

            def step(u, q, ahead3, ahead1):
                if ahead1:
                    gelu(u + 1)
                    high_gelu(u + 1, 1 - q)
                if ahead3:
                    high_part(u + 3, 1 - q)

            act.wait_ge(w_in, 16 * LOADS)
            for u in range(3):
                high_part(u, u % 2)
            gelu(0)
            high_gelu(0, 0)
            step(0, 0, True, True)
            step(1, 1, True, True)
            with act.Fori(0, (NPAIR - 6) // 2) as it:
                for q in range(2):
                    step(it * 2 + (2 + q), q, True, True)
            for u in range(NPAIR - 4, NPAIR):
                step(u, u % 2, u + 3 < NPAIR, u + 1 < NPAIR)

        @block.tensor
        def _(pe):
            def transpose_x(u, q):
                pe.wait_ge(xn_lo, u + 1)
                if not (isinstance(u, int) and u == 0):
                    pe.wait_ge(xs_ready, u * PAIR)
                for i in range(PAIR):
                    for s in range(3):
                        ins = nc.tensor.transpose(x_ps[i][:, L * s:L * s + L].bitcast(F32R),
                                                  xn[q][:, i, L * s:L * s + L], identr[:])
                    ins.then_inc(x_in_bank, 1)

            def hidden(u, q):
                pe.wait_ge(xs_ready, u * PAIR + PAIR)
                for c in range(HJ):
                    bank, at = hid_ps[c // 2], T2 * (c % 2)
                    if c % 2 == 0 and not (isinstance(u, int) and u == 0):
                        pe.wait_ge(gelu_ready, u * 3 + (c // 2 - 2))
                    cols = slice(128 * c, 128 * c + 128)
                    for s in range(4):
                        nc.tensor.matmul(bank[:, at:at + T2], w1[:, s, cols], xs[q][:, s % 3, :], start=(s == 0),
                                         stop=False)
                    ins = nc.tensor.matmul(bank[:, at:at + T2], w1[0:64, 4, cols], xs[q][0:64, 1, :], start=False,
                                           stop=True)
                    if c % 2 == 1:
                        ins.then_inc(hid_in_bank, 1)

            def project(u, q):
                pe.wait_ge(g_hi, u + 1)
                pe.wait_ge(g_lo, u + 1)
                if not (isinstance(u, int) and u < 2):
                    pe.wait_ge(h_added, u - 1)
                for i in range(PAIR):
                    out = out_ps[q][:, D * i:D * i + D]
                    t = slice(L * i, L * i + L)
                    if first:
                        nc.tensor.matmul(out, ones[:], b2[:, 0], start=True, stop=False)
                        nc.tensor.matmul(out, ones[:], b2[:, 1], start=False, stop=False)
                    for c in range(HJ):
                        nc.tensor.matmul(out, gh[q][:, c, t], w2[:, 0, c, :], start=(c == 0 and not first), stop=False)
                        nc.tensor.matmul(out, gh[q][:, c, t], w2[:, 1, c, :], start=False, stop=False)
                        ins = nc.tensor.matmul(out, gl[q][:, c, t], w2[:, 0, c, :], start=False, stop=(c == HJ - 1))
                ins.then_inc(out_ready, 1)

            def step(u, q, ahead2, ahead1):
                if ahead2:
                    transpose_x(u + 2, q)
                if ahead1:
                    hidden(u + 1, 1 - q)
                project(u, q)

            transpose_x(0, 0)
            pe.wait_ge(w_split, SPLITS)
            hidden(0, 0)
            transpose_x(1, 1)
            step(0, 0, True, True)
            step(1, 1, True, True)
            with pe.Fori(0, (NPAIR - 6) // 2) as it:
                for q in range(2):
                    step(it * 2 + (2 + q), q, True, True)
            for u in range(NPAIR - 4, NPAIR):
                step(u, u % 2, u + 2 < NPAIR, u + 1 < NPAIR)


def class_token_phase(nc, io, keep):
    with ExitStack() as ctx:
        def sb(name, shape, dt=F32):
            return ctx.enter_context(nc.sbuf_tensor(f"{name}_c", shape, dt))

        def psum(name, shape, dt=F32):
            return ctx.enter_context(nc.psum_tensor(f"{name}_c", shape, dt))

        def sem(name):
            return ctx.enter_context(nc.semaphore(f"{name}_c"))

        h, ident, nhalf, cls = keep["h"], keep["ident"], keep["nhalf"], keep["cls"]
        tok, a1, a2 = cls["tok"], cls["a1"], cls["a2"]
        Q, R = 3, 3 * B
        stats = sb("stats", [R, 2, 6])
        mv = sb("mv", [R, 2, 2])
        rstd = sb("rstd", [R, 2])
        xf = sb("xf", [R, 2, D])
        xt = sb("xt", [DC, 2, 2, R])
        hid_q = sb("hid_q", [128, HJ, 2, R])
        hid_t = sb("hid_t", [128, HJ, 2, R])
        lg = sb("lg", [R, 2, 2])
        gm = sb("gm", [R, 2])
        ge = sb("ge", [R, 2, 2])
        gate = sb("gate", [R, 2, 2])
        part = sb("part", [R, 2, D])
        part2 = sb("part2", [R, 2, D])
        res = sb("res", [R, 2, D])

        xt_ps = psum("xt_ps", [DC, BANK])
        lg_ps = psum("lg_ps", [R, BANK])
        hid_ps = [psum(f"hid_ps{i}", [128, BANK]) for i in range(4)]
        high_ps = psum("high_ps", [R, BANK])
        low_ps = psum("low_ps", [R, BANK])

        step_done = sem("step_done")
        var_ready = sem("var_ready")
        rstd_ready = sem("rstd_ready")
        xf_ready = sem("xf_ready")
        xt_in_bank = sem("xt_in_bank")
        xt_ready = sem("xt_ready")
        lg_ready = sem("lg_ready")
        shifted = sem("shifted")
        exp_ready = sem("exp_ready")
        hid_in_bank = sem("hid_in_bank")
        gelu_ready = sem("gelu_ready")
        out_ready = sem("out_ready")
        res_ready = sem("res_ready")
        stored = sem("stored")
        block = ctx.enter_context(nc.Block())

        def columns(e):
            if e < Q:
                return lambda c: xt[:, c, :, B * e:B * e + B]
            return lambda c: xt[:, c, e - Q, :]

        @block.sync
        def _(sp):
            sp.wait_ge(res_ready, 1)
            for i in range(NCLS):
                q, t = i // 2, i % 2
                sp.dma_start(h[i:i + 1, :, :], res[B * q:B * q + B, t, :]).then_inc(stored, 16)
            sp.wait_ge(stored, 16 * NCLS)

        @block.gpsimd
        def _(pool):
            pool.wait_ge(var_ready, 1)
            nc.gpsimd.tensor_tensor(rstd[:], mv[:, :, 1], nhalf[0:R].to_broadcast([R, 2]), ALU.pow).then_inc(rstd_ready, 1)

        @block.tensor
        def _(pe):
            pe.wait_ge(xf_ready, 2)
            for t in range(2):
                for c in range(2):
                    at = (2 * c + t) * R
                    ins = nc.tensor.transpose(xt_ps[:, at:at + R], xf[:, t, DC * c:DC * c + DC], ident[0:R, 0:R])
            ins.then_inc(xt_in_bank, 1)
            pe.wait_ge(xt_ready, 1)
            for t in range(2):
                for c in range(2):
                    ins = nc.tensor.matmul(lg_ps[:, 2 * NCLS * t:2 * NCLS * (t + 1)], xt[:, c, t, :], cls["gw"][:, c, :],
                                           start=(c == 0), stop=(c == 1))
            ins.then_inc(lg_ready, 1)
            for e in range(NEXP):
                n = 2 * B if e < Q else R
                for half in range(2):
                    u = 2 * e + half
                    if u >= 4:
                        pe.wait_ge(gelu_ready, u - 3)
                    for j in range(3):
                        out = hid_ps[u % 4][:, n * j:n * j + n]
                        if e < Q:
                            out = out.rearrange("p (t b) -> p t b", t=2)
                        f = (3 * half + j) * 128
                        for c in range(2):
                            ins = nc.tensor.matmul(out, a1[:, e, c, f:f + 128], columns(e)(c), start=(c == 0),
                                                   stop=(c == 1))
                    ins.then_inc(hid_in_bank, 1)
            pe.wait_ge(gelu_ready, 2 * NEXP)
            for t in range(2):
                for j in range(HJ):
                    nc.tensor.matmul(high_ps[:, D * t:D * t + D], hid_q[:, j, t, :], a2[:, Q + t, j, :], start=(j == 0),
                                     stop=(j == HJ - 1))
                for q in range(Q):
                    rows = slice(B * q, B * q + B)
                    for j in range(HJ):
                        ins = nc.tensor.matmul(low_ps[rows, D * t:D * t + D], hid_t[:, j, t, rows], a2[:, q, j, :],
                                               start=(j == 0), stop=(j == HJ - 1))
            ins.then_inc(out_ready, 1)

        @block.scalar
        def _(act):
            act.wait_ge(shifted, 1)
            nc.scalar.activation(ge[:], lg[:], ACT.Exp).then_inc(exp_ready, 1)
            for e in range(NEXP):
                n = 2 * B if e < Q else R
                for half in range(2):
                    u = 2 * e + half
                    act.wait_ge(hid_in_bank, u + 1)
                    for j in range(3):
                        f = 3 * half + j
                        src = hid_ps[u % 4][:, n * j:n * j + n]
                        if e < Q:
                            src = src.rearrange("p (t b) -> p t b", t=2)
                            dst = hid_q[:, f, :, B * e:B * e + B]
                        else:
                            dst = hid_t[:, f, e - Q, :]
                        ins = nc.scalar.activation(dst, src, ACT.Gelu, bias=cls["a1b"][:, e, f:f + 1])
                    ins.then_inc(gelu_ready, 1)

        @block.vector
        def _(dve):
            done = [0]

            def small(ins):
                done[0] += 1
                ins.then_inc(step_done, 1)
                dve.wait_ge(step_done, done[0])

            for t in range(2):
                small(nc.vector.bn_stats(stats[:, t], tok[:, t, :]))
                small(nc.vector.bn_aggr(mv[:, t], stats[:, t]))
            nc.vector.tensor_scalar(mv[:, :, 1], mv[:, :, 1], EPS_LN, None, ALU.add).then_inc(var_ready, 1)
            dve.wait_ge(rstd_ready, 1)
            for t in range(2):
                nc.vector.tensor_scalar(xf[:, t, :], tok[:, t, :], mv[:, t, 0:1], rstd[:, t:t + 1], ALU.subtract,
                                        ALU.mult).then_inc(xf_ready, 1)
            dve.wait_ge(xt_in_bank, 1)
            nc.vector.tensor_copy(xt[:].rearrange("p c t r -> p (c t r)"), xt_ps[:, 0:4 * R]).then_inc(xt_ready, 1)
            dve.wait_ge(lg_ready, 1)
            for t in range(2):
                for q in range(Q):
                    rows, i = slice(B * q, B * q + B), 2 * q + t
                    at = 2 * NCLS * t + 2 * i
                    small(nc.vector.tensor_copy(lg[rows, t, :], lg_ps[rows, at:at + 2]))
            small(nc.vector.tensor_reduce(gm[:], lg[:], AX.X, ALU.max))
            small(nc.vector.tensor_tensor(lg[:], lg[:], gm[:, :, None].to_broadcast([R, 2, 2]), ALU.subtract))
            nc.vector.tensor_copy(gate[:], lg[:]).then_inc(shifted, 1)
            dve.wait_ge(exp_ready, 1)
            dve.wait_ge(shifted, 1)
            small(nc.vector.tensor_reduce(gm[:], ge[:], AX.X, ALU.add))
            small(nc.vector.reciprocal(gm[:], gm[:]))
            small(nc.vector.tensor_tensor(ge[:], ge[:], gm[:, :, None].to_broadcast([R, 2, 2]), ALU.mult))
            small(nc.vector.tensor_reduce(gm[:], ge[:], AX.X, ALU.min))
            small(nc.vector.tensor_tensor(gate[:], ge[:], gm[:, :, None].to_broadcast([R, 2, 2]), ALU.is_gt))
            small(nc.vector.tensor_tensor(gate[:], gate[:], ge[:], ALU.mult))
            small(nc.vector.tensor_reduce(gm[:], gate[:], AX.X, ALU.add))
            small(nc.vector.tensor_scalar(gm[:], gm[:], 1e-6, None, ALU.max))
            small(nc.vector.reciprocal(gm[:], gm[:]))
            small(nc.vector.tensor_tensor(gate[:], gate[:], gm[:, :, None].to_broadcast([R, 2, 2]), ALU.mult))
            dve.wait_ge(out_ready, 1)
            small(nc.vector.tensor_tensor(part[:].rearrange("p t d -> p (t d)"), high_ps[:, 0:2 * D],
                                          cls["b_high"][:].rearrange("p t d -> p (t d)"), ALU.add))
            small(nc.vector.tensor_tensor(part2[:], low_ps[:, 0:2 * D].rearrange("p (t d) -> p t d", t=2),
                                          cls["b_low"][:, None, :].to_broadcast([R, 2, D]), ALU.add))
            for t in range(2):
                small(nc.vector.scalar_tensor_tensor(res[:, t, :], part[:, t, :], gate[:, t, 0:1], tok[:, t, :],
                                                     ALU.mult, ALU.add))
            for t in range(2):
                ins = nc.vector.scalar_tensor_tensor(res[:, t, :], part2[:, t, :], gate[:, t, 1:2], res[:, t, :],
                                                     ALU.mult, ALU.add)
                if t == 0:
                    small(ins)
            ins.then_inc(res_ready, 1)


HD = D // H
ROWS = 4
GR = H // ROWS
GF = ROWS * HD


def attention_phase(nc, io, keep):
    with ExitStack() as ctx:
        def sb(name, shape, dt=F32):
            return ctx.enter_context(nc.sbuf_tensor(f"{name}_a", shape, dt))

        def psum(name, shape, dt=F32):
            return ctx.enter_context(nc.psum_tensor(f"{name}_a", shape, dt))

        def sem(name):
            return ctx.enter_context(nc.semaphore(f"{name}_a"))

        h, ident, nhalf, identr = keep["h"], keep["ident"], keep["nhalf"], keep["identr"]
        SCALE = float(D) ** -0.5
        ONE = HD

        wqk_raw = sb("wqk_raw", [2 * GF, GR, 2, 128])
        wqk = sb("wqk", [2 * GF, GR, 2, 128], F32R)
        wqk_lo = sb("wqk_lo", [GF, GR, 2, 128], F32R)
        wv_raw = sb("wv_raw", [2 * GF, GR, GF])
        wv = sb("wv", [2 * GF, GR, GF], F32R)
        wv_lo = sb("wv_lo", [GF, GR, GF], F32R)
        bqk = sb("bqk", [128, GR, 2])
        bv = sb("bv", [L, D])
        wo = sb("wo", [128, GR, D])
        stats = sb("stats", [L, 6])
        mv = sb("mv", [L, 2, 2])
        rstd = sb("rstd", [L, 2])
        xf = sb("xf", [L, D])
        xn = [sb(f"xn{q}", [L, GR, 2, GF], F32R) for q in range(2)]
        xs = [sb(f"xs{q}", [128, GR, L], F32R) for q in range(2)]
        qt = [sb(f"qt{q}", [128, GR, L]) for q in range(2)]
        kt = [sb(f"kt{q}", [128, GR, L]) for q in range(2)]
        v = [sb(f"v{q}", [L, GR, ROWS, 32]) for q in range(2)]
        nmax = sb("nmax", [L, 2, ROWS, GR])
        probs = sb("probs", [L, 2, ROWS * GR, L])
        probs_t = sb("probs_t", [L, ROWS * GR, L])
        rsum = sb("rsum", [L, 2, ROWS * GR])
        rinv = sb("rinv", [L, 2, ROWS * GR])
        ot = sb("ot", [128, GR, L])

        s_ps = psum("s_ps", [L, ROWS, BANK])
        r_ps = [psum(f"r_ps{i}", [128, BANK]) for i in range(4)]

        pads_set = sem("pads_set")
        w_in = sem("w_in")
        w_split = sem("w_split")
        bq_scaled = sem("bq_scaled")
        aggr_step = sem("aggr_step")
        var_ready = sem("var_ready")
        rstd_ready = sem("rstd_ready")
        xf_ready = sem("xf_ready")
        xn_hi = sem("xn_hi")
        xn_lo = sem("xn_lo")
        x_in_bank = sem("x_in_bank")
        q_in_bank = sem("q_in_bank")
        k_in_bank = sem("k_in_bank")
        v_in_bank = sem("v_in_bank")
        s_ready = sem("s_ready")
        nmax_ready = sem("nmax_ready")
        exp_ready = sem("exp_ready")
        pt_in_bank = sem("pt_in_bank")
        o_in_bank = sem("o_in_bank")
        rinv_ready = sem("rinv_ready")
        probs_ready = sem("probs_ready")
        y_in_bank = sem("y_in_bank")
        r_free = [sem(f"r_free{i}") for i in range(4)]
        block = ctx.enter_context(nc.Block())

        @block.sync
        def _(sp):
            sp.wait_ge(pads_set, 4)
            w = io["w_qkv"].rearrange("(g p) d e -> p d g e", p=ROWS)
            for p in range(ROWS):
                for part in range(2):
                    rows = slice(GF * part + HD * p, GF * part + HD * p + HD)
                    for i in range(2):
                        sp.dma_start(wqk_raw[rows, :, i, 32 * p:32 * p + HD],
                                     w[p][:, :, HD * i:HD * i + HD]).then_inc(w_in, 16)
                    sp.dma_start(wv_raw[rows, :, HD * p:HD * p + HD], w[p][:, :, 2 * HD:3 * HD]).then_inc(w_in, 16)
                sp.dma_start(bqk[32 * p:32 * p + HD], io["b_qk"][p]).then_inc(w_in, 16)
            sp.dma_start(bv[:], io["b_v"].to_broadcast([L, D])).then_inc(w_in, 16)
            w = io["w_out"].rearrange("(g p d) e -> p d g e", p=ROWS, g=GR)
            for p in range(ROWS):
                sp.dma_start(wo[32 * p:32 * p + HD], w[p]).then_inc(w_in, 16)
            sp.dma_start(wo[ONE:ONE + 1, 0, :], io["b_out"]).then_inc(w_in, 16)
        LOADS = 8 * ROWS + 2

        @block.gpsimd
        def _(pool):
            def rstd_of(k, q):
                pool.wait_ge(var_ready, k + 1)
                nc.gpsimd.tensor_tensor(rstd[:, q:q + 1], mv[:, q, 1:2], nhalf[:], ALU.pow).then_inc(rstd_ready, 1)

            def normalise(k, q):
                for half in range(2):
                    heads = slice(H // 2 * half, H // 2 * half + H // 2)
                    pool.wait_ge(rinv_ready, k * 2 + (half + 1))
                    nc.gpsimd.tensor_tensor(probs[:, q, heads], probs[:, q, heads],
                                            rinv[:, q, heads, None].to_broadcast([L, H // 2, L]),
                                            ALU.mult).then_inc(probs_ready, 1)

            rstd_of(0, 0)
            rstd_of(1, 1)
            with pool.Fori(0, (B - 2) // 2) as it:
                for q in range(2):
                    rstd_of(it * 2 + (2 + q), q)
                    normalise(it * 2 + q, q)
            normalise(B - 2, 0)
            normalise(B - 1, 1)

        @block.vector
        def _(dve):
            def variance(k, q):
                nc.vector.bn_stats(stats[:], h[:, k, :])
                dve.drain()
                nc.vector.bn_aggr(mv[:, q], stats[:]).then_inc(aggr_step, 1)
                dve.wait_ge(aggr_step, k + 1)
                nc.vector.tensor_scalar(mv[:, q, 1:2], mv[:, q, 1:2], EPS_LN, None, ALU.add).then_inc(var_ready, 1)

            def centre(k, q):
                dve.wait_ge(rstd_ready, k + 1)
                nc.vector.tensor_scalar(xf[:], h[:, k, :], mv[:, q, 0:1], rstd[:, q:q + 1], ALU.subtract,
                                        ALU.mult).then_inc(xf_ready, 1)

            def low_part(k, q):
                dve.wait_ge(xn_hi, k + 1)
                nc.vector.tensor_tensor(xn[q][:, :, 1, :], xf[:].rearrange("l (g f) -> l g f", g=GR),
                                        f32(xn[q][:, :, 0, :]), ALU.subtract).then_inc(xn_lo, 1)
                dve.wait_ge(xn_lo, k + 1)

            def take_xs(k, q):
                dve.wait_ge(x_in_bank, k + 1)
                nc.vector.tensor_copy(xs[q][:].rearrange("p g l -> p (g l)"), r_ps[0][:, 0:GR * L]).then_inc(r_free[0], 1)

            def take_qk(k, q):
                dve.wait_ge(q_in_bank, k + 1)
                nc.vector.scalar_tensor_tensor(qt[q][:], r_ps[1][:, 0:GR * L].rearrange("p (g l) -> p g l", g=GR), SCALE,
                                               bqk[:, :, 0:1].to_broadcast([128, GR, L]), ALU.mult,
                                               ALU.add).then_inc(r_free[1], 1)
                dve.wait_ge(k_in_bank, k + 1)
                nc.vector.tensor_tensor(kt[q][:], r_ps[2][:, 0:GR * L].rearrange("p (g l) -> p g l", g=GR),
                                        bqk[:, :, 1:2].to_broadcast([128, GR, L]), ALU.add).then_inc(r_free[2], 1)

            def take_v(k, q):
                dve.wait_ge(v_in_bank, k + 1)
                nc.vector.tensor_tensor(v[q][:].rearrange("l g p d -> l (g p) d")[:, :, 0:HD],
                                        r_ps[0][:, 0:D].rearrange("l (i d) -> l i d", i=H),
                                        bv[:].rearrange("l (i d) -> l i d", i=H), ALU.add).then_inc(r_free[0], 1)

            def row_max(k, q, half):
                dve.wait_ge(s_ready, k * 2 + (half + 1))
                nc.vector.tensor_reduce(nmax[:, q, 2 * half:2 * half + 2, :],
                                        s_ps[:, 2 * half:2 * half + 2, 0:GR * L].rearrange(
                                            "l p (g m) -> l p g m", g=GR),
                                        AX.X, ALU.max, negate=True).then_inc(nmax_ready, 1)

            def take_probs_t(k):
                dve.wait_ge(pt_in_bank, k * 3 + 1)
                nc.vector.tensor_copy(probs_t[:, 0:4, :].rearrange("t i l -> t (i l)"), r_ps[0][:]).then_inc(r_free[0], 1)

            def inverse_sum(k, q, half):
                heads = slice(H // 2 * half, H // 2 * half + H // 2)
                dve.wait_ge(exp_ready, k * 2 + (half + 1))
                nc.vector.reciprocal(rinv[:, q, heads], rsum[:, q, heads]).then_inc(rinv_ready, 1)

            def add_to_h(k):
                dve.wait_ge(y_in_bank, k + 1)
                nc.vector.tensor_tensor(h[:, k, :], r_ps[3][:, 0:D], h[:, k, :], ALU.add).then_inc(r_free[3], 1)

            def step(k, q, main, ahead2, ahead1, back1, back2):
                if ahead2:
                    variance(k + 2, q)
                if main:
                    row_max(k, q, 0)
                if ahead1:
                    take_xs(k + 1, 1 - q)
                if ahead2:
                    centre(k + 2, q)
                if main:
                    row_max(k, q, 1)
                    inverse_sum(k, q, 0)
                    take_v(k, q)
                if ahead1:
                    take_qk(k + 1, 1 - q)
                if ahead2:
                    low_part(k + 2, q)
                if back2:
                    add_to_h(k - 2)
                if main:
                    inverse_sum(k, q, 1)
                if back1:
                    take_probs_t(k - 1)

            nc.vector.memset(wqk_raw[:].rearrange("p g i m -> p (g i m)"), 0.0).then_inc(pads_set, 1)
            nc.vector.memset(wv_raw[:], 0.0).then_inc(pads_set, 1)
            nc.vector.memset(bqk[:], 0.0).then_inc(pads_set, 1)
            nc.vector.memset(wo[:], 0.0).then_inc(pads_set, 1)
            for q in range(2):
                nc.vector.memset(v[q][:], 0.0).then_inc(pads_set, 1)
            dve.wait_ge(pads_set, 6)
            for k in range(2):
                variance(k, k)
                centre(k, k)
                low_part(k, k)
            dve.wait_ge(w_in, 16 * LOADS)
            nc.vector.tensor_copy(wqk[:], wqk_raw[:]).then_inc(w_split, 1)
            nc.vector.tensor_copy(wv[:], wv_raw[:]).then_inc(w_split, 1)
            nc.vector.tensor_scalar(bqk[:, :, 0:1], bqk[:, :, 0:1], SCALE, None, ALU.mult).then_inc(bq_scaled, 1)
            dve.wait_ge(w_split, 2)
            nc.vector.tensor_tensor(wqk_lo[:], wqk_raw[0:GF], f32(wqk[0:GF]), ALU.subtract).then_inc(w_split, 1)
            nc.vector.tensor_tensor(wv_lo[:], wv_raw[0:GF], f32(wv[0:GF]), ALU.subtract).then_inc(w_split, 1)
            dve.wait_ge(bq_scaled, 1)
            take_xs(0, 0)
            take_qk(0, 0)
            step(0, 0, True, True, True, False, False)
            step(1, 1, True, True, True, True, False)
            with dve.Fori(0, (B - 4) // 2) as it:
                for q in range(2):
                    step(it * 2 + (2 + q), q, True, True, True, True, True)
            step(B - 2, 0, True, False, True, True, True)
            step(B - 1, 1, True, False, False, True, True)
            step(B, 0, False, False, False, True, True)
            step(B + 1, 1, False, False, False, False, True)

        @block.scalar
        def _(act):
            def high_part(k, q):
                act.wait_ge(xf_ready, k + 1)
                nc.scalar.activation(xn[q][:, :, 0, :], xf[:].rearrange("l (g f) -> l g f", g=GR),
                                     ACT.Copy).then_inc(xn_hi, 1)

            def exps(k, q, half):
                act.wait_ge(nmax_ready, k * 2 + (half + 1))
                for p in (2 * half, 2 * half + 1):
                    for g in range(GR):
                        ins = nc.scalar.activation(probs[:, q, GR * p + g, :], s_ps[:, p, L * g:L * g + L], ACT.Exp,
                                                   bias=nmax[:, q, p, g:g + 1],
                                                   accum_out=rsum[:, q, GR * p + g:GR * p + g + 1])
                ins.then_inc(exp_ready, 1)

            def take_probs_t(k, i):
                act.wait_ge(pt_in_bank, k * 3 + (i + 1))
                nc.scalar.activation(probs_t[:, 4 * i:4 * i + 4, :].rearrange("t i l -> t (i l)"), r_ps[i][:],
                                     ACT.Copy).then_inc(r_free[i], 1)

            def take_o(k):
                act.wait_ge(o_in_bank, k + 1)
                nc.scalar.activation(ot[:].rearrange("p g l -> p (g l)"), r_ps[3][:, 0:GR * L], ACT.Identity,
                                     bias=ident[:, ONE:ONE + 1]).then_inc(r_free[3], 1)

            def step(k, q, main, ahead2, back1, back2):
                if main:
                    exps(k, q, 0)
                if back2:
                    take_o(k - 2)
                if ahead2:
                    high_part(k + 2, q)
                if main:
                    exps(k, q, 1)
                if back1:
                    take_probs_t(k - 1, 1)
                    take_probs_t(k - 1, 2)

            high_part(0, 0)
            high_part(1, 1)
            step(0, 0, True, True, False, False)
            step(1, 1, True, True, True, False)
            with act.Fori(0, (B - 4) // 2) as it:
                for q in range(2):
                    step(it * 2 + (2 + q), q, True, True, True, True)
            step(B - 2, 0, True, False, True, True)
            step(B - 1, 1, True, False, True, True)
            step(B, 0, False, False, True, True)
            step(B + 1, 1, False, False, False, True)

        @block.tensor
        def _(pe):
            def wait_free(i, n):
                if not (isinstance(n, int) and n <= 0):
                    pe.wait_ge(r_free[i], n)

            def transpose_x(k, q, used):
                pe.wait_ge(xn_lo, k + 1)
                wait_free(0, used)
                for g in range(GR):
                    ins = nc.tensor.transpose(r_ps[0][:, L * g:L * g + L].bitcast(F32R),
                                              xn[q][:, g].rearrange("l s f -> l (s f)"), identr[:])
                ins.then_inc(x_in_bank, 1)

            def project_qk(k, q, used_qk):
                for i, ready in ((0, q_in_bank), (1, k_in_bank)):
                    wait_free(1 + i, used_qk)
                    for g in range(GR):
                        out = r_ps[1 + i][:, L * g:L * g + L]
                        nc.tensor.matmul(out, wqk[:, g, i, :], xs[q][:, g, :], start=True, stop=False)
                        ins = nc.tensor.matmul(out, wqk_lo[:, g, i, :], xs[q][0:GF, g, :], start=False, stop=True)
                    ins.then_inc(ready, 1)

            def project_v(k, q, used):
                wait_free(0, used)
                for g in range(GR):
                    out = r_ps[0][:, GF * g:GF * g + GF]
                    nc.tensor.matmul(out, xs[q][:, g, :], wv[:, g, :], start=True, stop=False)
                    ins = nc.tensor.matmul(out, xs[q][0:GF, g, :], wv_lo[:, g, :], start=False, stop=True)
                ins.then_inc(v_in_bank, 1)

            def scores(k, q, half):
                if not (isinstance(k, int) and k == 0):
                    pe.wait_ge(exp_ready, k * 2 + (half - 1))
                for g in range(GR):
                    for p in (2 * half, 2 * half + 1):
                        rows = slice(32 * p, 32 * p + HD)
                        ins = nc.tensor.matmul(s_ps[:, p, L * g:L * g + L], qt[q][rows, g, :], kt[q][rows, g, :],
                                               start=True, stop=True)
                ins.then_inc(s_ready, 1)

            def transpose_probs(k, q, used):
                for i in range(3):
                    if i < 2:
                        pe.wait_ge(probs_ready, k * 2 + (i + 1))
                    wait_free(i, used[i])
                    for j in range(4):
                        ins = nc.tensor.transpose(r_ps[i][:, L * j:L * j + L], probs[:, q, 4 * i + j, :], ident[:])
                    ins.then_inc(pt_in_bank, 1)

            def attend(k, q, used_o):
                wait_free(3, used_o)
                for g in range(GR):
                    for p in range(ROWS):
                        ins = nc.tensor.matmul(r_ps[3][32 * p:32 * p + 32, L * g:L * g + L], v[q][:, g, p, :],
                                               probs_t[:, GR * p + g, :], start=True, stop=True)
                ins.then_inc(o_in_bank, 1)

            def project_out(k, used):
                wait_free(3, used)
                for g in range(GR):
                    ins = nc.tensor.matmul(r_ps[3][:, 0:D], ot[:, g, :], wo[:, g, :], start=(g == 0), stop=(g == GR - 1))
                ins.then_inc(y_in_bank, 1)

            def step(k, q, main, ahead1, back1, back2, r0, r12, r3):
                if main:
                    last_qk = r12 - 1 if back2 else r12
                    pe.wait_ge(r_free[1], last_qk)
                    pe.wait_ge(r_free[2], last_qk)
                    scores(k, q, 0)
                if back2:
                    pe.wait_ge(r_free[0], r0)
                    pe.wait_ge(r_free[1], r12)
                    pe.wait_ge(r_free[2], r12)
                    attend(k - 2, q, r3)
                if ahead1:
                    transpose_x(k + 1, 1 - q, r0)
                    r0 = r0 + 1
                if main:
                    scores(k, q, 1)
                    project_v(k, q, r0)
                    r0 = r0 + 1
                if ahead1:
                    project_qk(k + 1, 1 - q, r12)
                    r12 = r12 + 1
                if back2:
                    project_out(k - 2, r3 + 1)
                if back1:
                    transpose_probs(k - 1, 1 - q, (r0, r12, r12))

            transpose_x(0, 0, 0)
            pe.wait_ge(w_split, 4)
            pe.wait_ge(r_free[0], 1)
            project_qk(0, 0, 0)
            step(0, 0, True, True, False, False, 1, 1, 0)
            for k in range(1, 4):
                step(k, k % 2, True, True, True, k > 1, 3 * k, 2 * k, 2 * k - 4)
            with pe.Fori(0, (B - 6) // 2) as it:
                for q in range(2):
                    step(it * 2 + (4 + q), q, True, True, True, True, it * 6 + (12 + 3 * q), it * 4 + (8 + 2 * q),
                         it * 4 + (4 + 2 * q))
            step(B - 2, 0, True, True, True, True, 3 * B - 6, 2 * B - 4, 2 * B - 8)
            step(B - 1, 1, True, False, True, True, 3 * B - 3, 2 * B - 2, 2 * B - 6)
            step(B, 0, False, False, True, True, 3 * B - 1, 2 * B - 1, 2 * B - 4)
            step(B + 1, 1, False, False, False, True, 3 * B, 2 * B, 2 * B - 2)


def program(nc, io):
    with ExitStack() as ctx:
        def sb(name, shape, dt=F32):
            return ctx.enter_context(nc.sbuf_tensor(name, shape, dt))

        keep = {
            "h": sb("h", [L, B, D]),
            "ident": sb("ident", [L, L]),
            "identr": sb("identr", [L, L], F32R),
            "nhalf": sb("nhalf", [L, 1]),
        }
        with ExitStack() as early:
            keep["wte_acc"] = early.enter_context(nc.sbuf_tensor("wte_acc", [L, 1, WR * D], F32))
            keep["w5"] = early.enter_context(nc.sbuf_tensor("w5", [L, 5, GW], F32R))
            mixing_phase(nc, io, keep)
            wte_phase(nc, io, keep)
        with ExitStack() as classes:
            def cls_sb(name, shape):
                return classes.enter_context(nc.sbuf_tensor(f"cls_{name}", shape, F32))

            keep["cls"] = {
                "tok": cls_sb("tok", [3 * B, 2, D]),
                "a1": cls_sb("a1", [DC, NEXP, 2, HID]),
                "a1b": cls_sb("a1b", [128, NEXP, HJ]),
                "a2": cls_sb("a2", [128, NEXP, HJ, D]),
                "b_high": cls_sb("b_high", [3 * B, 2, D]),
                "b_low": cls_sb("b_low", [3 * B, D]),
                "gw": cls_sb("gw", [DC, 2, 2 * NCLS]),
            }
            feed_forward_phase(nc, io, keep, 0)
            class_token_phase(nc, io, keep)
        attention_phase(nc, io, keep)
        feed_forward_phase(nc, io, keep, 1)


def kernel(**inputs):
    import numpy as np
    import concourse.bacc as bacc
    from concourse.bass_utils import run_bass_kernel_spmd

    def get(name):
        return np.asarray(inputs[name])

    data = {
        "x": get("x")[..., 0].transpose(2, 0, 1),
        "dw_w": get("L0_tok_dw_w")[:, 0, :, 0],
        "pw_w": get("L0_tok_pw_w").T,
        "pw_b": get("L0_tok_pw_b")[None],
        "ln_g": get("L0_tok_ln_g")[None],
        "ln_b": get("L0_tok_ln_b")[None],
        "ln_w": get("L0_attn_ln_w")[None],
        "w_qk": get("L0_attn_W_qk").T,
        "w_o": get("L0_attn_W_o").reshape(D, H, D).transpose(2, 1, 0).reshape(D, H * D),
        "wte": get("L0_attn_wte"),
        "ffn0_w1": get("L0_ffn_moe0_W1"),
        "ffn0_b1": get("L0_ffn_moe0_b1").reshape(HJ, 128).T,
        "ffn0_w2": get("L0_ffn_moe0_W2"),
        "ffn0_b2": get("L0_ffn_moe0_b2")[None],
        "a1": get("L0_ffn_A1_W"),
        "a1b": get("L0_ffn_A1_b").reshape(NEXP, HJ, 128).transpose(2, 0, 1),
        "a2": get("L0_ffn_A2_W"),
        "a2b": get("L0_ffn_A2_b"),
        "gw": get("L0_ffn_G_W").transpose(1, 0, 2).reshape(D, 2 * NCLS),
        "w_qkv": get("L1_attn_W_qkv"),
        "b_qk": get("L1_attn_b_qkv")[:, 0:2 * HD].reshape(GR, ROWS, 2, HD).transpose(1, 3, 0, 2),
        "b_v": get("L1_attn_b_qkv")[:, 2 * HD:].reshape(1, D),
        "w_out": get("L1_attn_W_out"),
        "b_out": get("L1_attn_b_out")[None],
        "ffn1_w1": get("L1_ffn_in_weight").T,
        "ffn1_b1": get("L1_ffn_in_bias").reshape(HJ, 128).T,
        "ffn1_w2": get("L1_ffn_out_weight"),
        "ident": np.eye(L, dtype=np.float32),
        "mask": np.triu(np.full((L, L), -1e30, np.float32), 1),
        "nreg": (1.0 / np.arange(1, L + 1, dtype=np.float32))[:, None].astype(np.float32),
    }
    nc = bacc.Bacc("TRN2", target_bir_lowering=False, num_devices=1)
    io, arrays = {}, {}
    for name, a in data.items():
        a = np.ascontiguousarray(a)
        arrays[f"in_{name}"] = a
        io[name] = nc.dram_tensor(f"in_{name}", a.shape, mybir.dt.from_np(a.dtype), kind="ExternalInput").ap()
    io["out"] = nc.dram_tensor("out_0", (B, L, D), F32, kind="ExternalOutput").ap()
    program(nc, io)
    r = run_bass_kernel_spmd(nc, [arrays], core_ids=[0])
    return r.results[0]["out_0"]
```

```python
from contextlib import ExitStack

import concourse.bass as bass
from concourse import mybir

F32 = mybir.dt.float32
F32R = mybir.dt.float32r
BF16 = mybir.dt.bfloat16
ALU = mybir.AluOpType
ACT = mybir.ActivationFunctionType
AX = mybir.AxisListType

B, L, D = 32, 128, 192
DC = D // 2
TAPS, HALO = 7, 3
LP = L + 2 * HALO
H = 12
HG = 4
BANK = 512
GW = H * D
VOCAB = 50257
WR = 8
WPIECE = VOCAB // (L * WR)
WTAIL = VOCAB - WPIECE * L * WR
EPS_TOK, EPS_LN = 1e-6, 1e-5


HID = 768
HJ = HID // 128
STACKS = ([(0, 128, 0)], [(128, 192, 0), (0, 64, 64)], [(64, 192, 0)])


def load_feed_forward(sp, io, keep, name, loaded):
    n = 0
    for i, parts in enumerate(STACKS):
        for lo, hi, at in parts:
            sp.dma_start(keep["raw1"][at:at + hi - lo, i, :], io[f"{name}_w1"][lo:hi]).then_inc(loaded, 16)
            n += 1
    sp.dma_start(keep["raw2"][:], io[f"{name}_w2"].rearrange("(j p) d -> p j d", p=128)).then_inc(loaded, 16)
    sp.dma_start(keep["b1"][:], io[f"{name}_b1"]).then_inc(loaded, 16)
    return n + 2


FF_LOADS = 6
SCALE = float(D) ** -0.5


def f32(ap):
    return ap.bitcast(F32)


def mixing_phase(nc, io, keep):
    with ExitStack() as ctx:
        def sb(name, shape, dt=F32):
            return ctx.enter_context(nc.sbuf_tensor(name, shape, dt))

        def psum(name, shape, dt=F32):
            return ctx.enter_context(nc.psum_tensor(name, shape, dt))

        def sem(name):
            return ctx.enter_context(nc.semaphore(name))

        h, ident, nhalf, identr = keep["h"], keep["ident"], keep["nhalf"], keep["identr"]

        wte_acc = sb("wte_acc", [L, WR * D])
        w5 = sb("w5", [L, 5, GW], F32R)
        x_pad = sb("x_pad", [DC, 2, B, LP])
        taps = sb("taps", [DC, 2, TAPS])
        pw = sb("pw", [DC + 1, 2, D])
        ln_g = sb("ln_g", [L, D])
        ln_b = sb("ln_b", [L, D])
        ln_w = sb("ln_w", [L, D])
        wqk = sb("wqk", [DC, 2, H])
        nreg = sb("nreg", [L, 1])
        identb = sb("identb", [L, L], BF16)
        maskf = sb("maskf", [L, L])
        maskb = sb("maskb", [L, HG, L], BF16)
        conv = [sb(f"conv{q}", [DC + 1, 2, L]) for q in range(2)]
        stats = sb("stats", [L, 2, 6])
        mv1 = sb("mv1", [L, 2, 2])
        mv2 = sb("mv2", [L, 2, 2])
        rstd1 = sb("rstd1", [L, 2])
        rstd2 = sb("rstd2", [L, 2])
        ytmp = sb("ytmp", [L, D])
        ypre = sb("ypre", [L, D])
        hc = sb("hc", [L, 2, D])
        xn = [sb(f"xn{q}", [L, 2 * D], F32R) for q in range(2)]
        xs = [sb(f"xs{q}", [L, 3, L], F32R) for q in range(2)]
        xt = [sb(f"xt{q}", [DC, 2, L]) for q in range(2)]
        ys = sb("ys", [DC, 2, H, L])
        nmax = sb("nmax", [L, 2, H])
        rsum = sb("rsum", [L, 2, H])
        rinv = sb("rinv", [L, 2, H])
        probs = sb("probs", [L, 2, H, L])
        probs_t = sb("probs_t", [L, H, L])
        g = [sb(f"g{q}", [L, GW]) for q in range(2)]
        wte = sb("wte", [L, 2, WR * D])
        wte_tail = sb("wte_tail", [WTAIL, D])
        share = sb("share", [L, 1])
        nneg = sb("nneg", [L, 1])
        wo_sum = sb("wo_sum", [L, 4, D])
        wte_sum, fix = ypre, ytmp
        avg = hc[:].rearrange("l a d -> l (a d)").rearrange("l (i m) -> l i m", i=3)

        ring = [psum(f"ring{i}", [L, BANK]) for i in range(3)]
        y_ps = psum("y_ps", [L, BANK])
        o_ps = psum("o_ps", [L, BANK])
        s_ps = psum("s_ps", [L, 3, BANK])

        conv_in = sem("conv_in")
        pw_in = sem("pw_in")
        first_in = sem("first_in")
        rest_in = sem("rest_in")
        ff_in = sem("ff_in")
        w_in = sem("w_in")
        wte_in = [sem(f"wte_in{q}") for q in range(2)]
        halo_set = sem("halo_set")
        identr_ready = sem("identr_ready")
        mask_ready = sem("mask_ready")
        wqk_sq = sem("wqk_sq")
        w_hi = sem("w_hi")
        w_lo = sem("w_lo")
        conv_ready = sem("conv_ready")
        conv_step = sem("conv_step")
        y_ready = sem("y_ready")
        y_bank_free = sem("y_bank_free")
        stats_step = sem("stats_step")
        ln1_stats = sem("ln1_stats")
        ln1_rstd = sem("ln1_rstd")
        ypre_ready = sem("ypre_ready")
        relu_ready = sem("relu_ready")
        ln2_stats = sem("ln2_stats")
        ln2_rstd = sem("ln2_rstd")
        hc_ready = sem("hc_ready")
        xn_hi = sem("xn_hi")
        xn_lo = sem("xn_lo")
        xs_in_bank = sem("xs_in_bank")
        xt_in_bank = sem("xt_in_bank")
        xs_ready = sem("xs_ready")
        xt_ready = sem("xt_ready")
        ys0_ready = sem("ys0_ready")
        ys1_ready = sem("ys1_ready")
        s_ready = sem("s_ready")
        nmax_ready = sem("nmax_ready")
        exp_ready = sem("exp_ready")
        rinv_step = sem("rinv_step")
        rinv_ready = sem("rinv_ready")
        probs_ready = sem("probs_ready")
        pt_in_bank = sem("pt_in_bank")
        g_in_bank = sem("g_in_bank")
        pv_ready = sem("pv_ready")
        h_added = sem("h_added")
        wte_added = sem("wte_added")
        bank_free = [sem(f"bank_free{i}") for i in range(3)]
        tail_in = sem("tail_in")
        nneg_ready = sem("nneg_ready")
        share_set = sem("share_set")
        wte_summed = sem("wte_summed")
        wo_summed = sem("wo_summed")
        avg_in_bank = sem("avg_in_bank")
        avg_taken = sem("avg_taken")
        fix_in_bank = sem("fix_in_bank")
        fix_ready = sem("fix_ready")
        h_fixed = sem("h_fixed")

        block = ctx.enter_context(nc.Block())

        x_v = io["x"].rearrange("(c p) b l -> p c b l", c=2)
        wo_v = io["w_o"]
        wte_v = io["wte"][0:WPIECE * L * WR, :].rearrange("(n p r) d -> n p (r d)", p=L, r=WR)
        WO_ROWS = ([(0, 128, 0)], [(128, 192, 0), (0, 64, 64)], [(64, 192, 0)])
        raw = [g[0][:, :], g[1][:, :], probs[:].rearrange("p a h l -> p (a h l)")[:, 0:GW]]
        POOL_IMAGES = 16
        G_BANK = (1, 2, 0, 1, 2)
        G_COLS = [(j * BANK, min((j + 1) * BANK, GW)) for j in range(5)]

        @block.sync
        def _(sp):
            for c in range(2):
                sp.dma_start(x_pad[:, c, 0:2, HALO:HALO + L], x_v[:, c, 0:2]).then_inc(conv_in, 16)
            sp.dma_start(taps[:], io["dw_w"].rearrange("(c p) k -> p c k", c=2)).then_inc(conv_in, 16)
            sp.dma_start(pw[0:DC], io["pw_w"].rearrange("(c p) e -> p c e", c=2)).then_inc(pw_in, 16)
            sp.dma_start(pw[DC:DC + 1, 0, :], io["pw_b"]).then_inc(pw_in, 16)
            sp.dma_start(ident[:], io["ident"]).then_inc(first_in, 16)
            sp.dma_start(ln_g[:], io["ln_g"].to_broadcast([L, D])).then_inc(first_in, 16)
            sp.dma_start(ln_b[:], io["ln_b"].to_broadcast([L, D])).then_inc(first_in, 16)
            sp.dma_start(ln_w[:], io["ln_w"].to_broadcast([L, D])).then_inc(first_in, 16)
            sp.dma_start(wqk[:], io["w_qk"].rearrange("(c p) h -> p c h", c=2)).then_inc(first_in, 16)
            sp.dma_start(nreg[:], io["nreg"]).then_inc(first_in, 16)
            sp.dma_start(maskf[:], io["mask"]).then_inc(first_in, 16)
            for i, parts in enumerate(WO_ROWS):
                for lo, hi, at in parts:
                    sp.dma_start(raw[i][at:at + hi - lo], wo_v[lo:hi]).then_inc(w_in, 16)
            for c in range(2):
                sp.dma_start(x_pad[:, c, 2:B, HALO:HALO + L], x_v[:, c, 2:B]).then_inc(rest_in, 16)
            sp.dma_start(wte_acc[:], wte_v[0]).then_inc(wte_in[0], 16)
            for n in (1, 2):
                sp.dma_start(wte[:, n % 2], wte_v[n]).then_inc(wte_in[n % 2], 16)
            with sp.Fori(0, (WPIECE - 3) // 2) as it:
                for n0 in (3, 4):
                    sp.wait_ge(wte_added, it * 2 + (n0 - 2))
                    sp.dma_start(wte[:, n0 % 2], wte_v[it * 2 + n0]).then_inc(wte_in[n0 % 2], 16)
            sp.dma_start(wte_tail[:], io["wte"][VOCAB - WTAIL:VOCAB, :]).then_inc(tail_in, 16)
            sp.dma_start(keep["b2f"][:], io["ffn0_b2"]).then_inc(ff_in, 16)
            load_feed_forward(sp, io, keep, "ffn0", ff_in)
            sp.wait_ge(tail_in, 16)
            sp.wait_ge(ff_in, 16 * (FF_LOADS + 1))

        @block.gpsimd
        def _(pool):
            def wte_piece(n):
                if n == 1:
                    pool.wait_ge(wte_in[0], 16)
                if n >= 2:
                    pool.wait_ge(wte_added, n - 1)
                pool.wait_ge(wte_in[n % 2], 16 * (n // 2 + 1))
                nc.gpsimd.tensor_tensor(wte_acc[:], wte_acc[:], wte[:, n % 2],
                                        ALU.add).then_inc(wte_added, 1)

            def rstd_1(k, q):
                pool.wait_ge(ln1_stats, k + 1)
                nc.gpsimd.tensor_tensor(rstd1[:, q:q + 1], mv1[:, q, 1:2], nhalf[:], ALU.pow).then_inc(ln1_rstd, 1)

            def rstd_2(k, q):
                pool.wait_ge(ln2_stats, k + 1)
                nc.gpsimd.tensor_tensor(rstd2[:, q:q + 1], mv2[:, q, 1:2], nhalf[:], ALU.pow).then_inc(ln2_rstd, 1)

            def scale_1(k, q):
                pool.wait_ge(xt_ready, k + 1)
                nc.gpsimd.tensor_tensor(ys[:, 1], xt[q][:, 1, None, :].to_broadcast([DC, H, L]),
                                        wqk[:, 1, :, None].to_broadcast([DC, H, L]), ALU.mult).then_inc(ys1_ready, 1)

            def normalise(k, q):
                pool.wait_ge(rinv_ready, k + 1)
                nc.gpsimd.tensor_tensor(probs[:, q], probs[:, q], rinv[:, q, :, None].to_broadcast([L, H, L]),
                                        ALU.mult).then_inc(probs_ready, 1)

            def step(k, q, pieces, ahead2, ahead1):
                for n in pieces:
                    wte_piece(n)
                if ahead2:
                    rstd_1(k + 2, q)
                if ahead1:
                    scale_1(k + 1, 1 - q)
                if ahead2:
                    rstd_2(k + 2, q)
                normalise(k, q)

            pool.wait_ge(halo_set, 5)
            rstd_1(0, 0)
            rstd_2(0, 0)
            rstd_1(1, 1)
            pool.wait_ge(wqk_sq, 2)
            scale_1(0, 0)
            rstd_2(1, 1)
            pieces = list(range(1, WPIECE))
            step(0, 0, pieces[0:2], True, True)
            step(1, 1, pieces[2:3], True, True)
            first = pieces[3]
            with pool.Fori(0, 7) as it:
                for u in range(4):
                    k = it * 4 + (2 + u)
                    for j in ((0, 1), (2,), (3, 4), (5,))[u]:
                        n0 = first + j
                        pool.wait_ge(wte_added, it * 6 + (n0 - 1))
                        pool.wait_ge(wte_in[n0 % 2], it * 48 + 16 * ((n0 + 1) // 2 + (n0 % 2 == 0)))
                        nc.gpsimd.tensor_tensor(wte_acc[:], wte_acc[:], wte[:, n0 % 2],
                                                ALU.add).then_inc(wte_added, 1)
                    step(k, u % 2, (), True, True)
            done = first + 42
            rest = list(range(done, WPIECE))
            step(30, 0, rest[0:2], False, True)
            step(31, 1, rest[2:], False, False)
            pool.wait_ge(fix_ready, 1)
            pool.wait_ge(h_added, POOL_IMAGES)
            nc.gpsimd.tensor_tensor(h[:, 0:POOL_IMAGES, :], h[:, 0:POOL_IMAGES, :],
                                    fix[:, None, :].to_broadcast([L, POOL_IMAGES, D]), ALU.add).then_inc(h_fixed, 1)

        @block.vector
        def _(dve):
            def convolve(k, q, halves=(0, 1)):
                for c in halves:
                    for t in range(TAPS):
                        src = x_pad[:, c, k, t:t + L]
                        dst = conv[q][0:DC, c, :]
                        w = taps[:, c, t:t + 1]
                        if t == 0:
                            ins = nc.vector.tensor_scalar(dst, src, w, None, ALU.mult)
                        else:
                            dve.wait_ge(conv_step, k * (2 * (TAPS - 1)) + (c * (TAPS - 1) + t))
                            ins = nc.vector.scalar_tensor_tensor(dst, src, w, dst, ALU.mult, ALU.add)
                        if t < TAPS - 1:
                            ins.then_inc(conv_step, 1)
                        else:
                            ins.then_inc(conv_ready, 1)

            def ln1_a(k, q):
                dve.wait_ge(y_ready, k + 1)
                nc.vector.bn_stats(stats[:, 0], y_ps[:, 0:D]).then_inc(stats_step, 1)
                dve.drain()
                nc.vector.bn_aggr(mv1[:, q], stats[:, 0]).then_inc(stats_step, 1)
                dve.wait_ge(stats_step, k * 4 + 2)
                nc.vector.tensor_scalar(mv1[:, q, 1:2], mv1[:, q, 1:2], EPS_TOK, None, ALU.add).then_inc(ln1_stats, 1)

            def ln1_b(k, q):
                dve.wait_ge(ln1_rstd, k + 1)
                nc.vector.scalar_tensor_tensor(ytmp[:], y_ps[:, 0:D], mv1[:, q, 0:1], ln_g[:], ALU.subtract,
                                               ALU.mult).then_inc(y_bank_free, 1)
                dve.wait_ge(y_bank_free, k + 1)
                nc.vector.scalar_tensor_tensor(ypre[:], ytmp[:], rstd1[:, q:q + 1], ln_b[:], ALU.mult,
                                               ALU.add).then_inc(ypre_ready, 1)

            def ln2_a(k, q):
                dve.wait_ge(relu_ready, k + 1)
                nc.vector.bn_stats(stats[:, 1], h[:, k, :]).then_inc(stats_step, 1)
                dve.drain()
                nc.vector.bn_aggr(mv2[:, q], stats[:, 1]).then_inc(stats_step, 1)
                dve.wait_ge(stats_step, k * 4 + 4)
                nc.vector.tensor_scalar(mv2[:, q, 1:2], mv2[:, q, 1:2], 1.0 + EPS_LN, EPS_LN * EPS_LN, ALU.mult,
                                        ALU.add).then_inc(ln2_stats, 1)

            def ln2_b(k, q):
                dve.wait_ge(ln2_rstd, k + 1)
                nc.vector.scalar_tensor_tensor(hc[:, q], h[:, k, :], mv2[:, q, 0:1], ln_w[:], ALU.subtract,
                                               ALU.mult).then_inc(hc_ready, 1)

            def low_part(k, q):
                dve.wait_ge(xn_hi, k + 1)
                nc.vector.scalar_tensor_tensor(xn[q][:, D:2 * D], hc[:, q], rstd2[:, q:q + 1], f32(xn[q][:, 0:D]),
                                               ALU.mult, ALU.subtract).then_inc(xn_lo, 1)

            def take_xs(k, q):
                dve.wait_ge(xs_in_bank, k + 1)
                nc.vector.tensor_copy(xs[q][:].rearrange("p a b -> p (a b)"), ring[0][:, 0:3 * L]).then_inc(bank_free[0], 1)

            def scale_0(k, q):
                dve.wait_ge(xt_ready, k + 1)
                nc.vector.tensor_tensor(ys[:, 0], xt[q][:, 0, None, :].to_broadcast([DC, H, L]),
                                        wqk[:, 0, :, None].to_broadcast([DC, H, L]), ALU.mult).then_inc(ys0_ready, 1)

            def row_max(k, q):
                dve.wait_ge(s_ready, k + 1)
                nc.vector.tensor_reduce(nmax[:, q, :], s_ps[:].rearrange("p b (h l) -> p (b h) l", l=L), AX.X, ALU.max,
                                        negate=True).then_inc(nmax_ready, 1)

            def take_probs_t(k, j):
                dve.wait_ge(pt_in_bank, k * 3 + (j + 1))
                nc.vector.tensor_copy(probs_t[:, HG * j:HG * j + HG, :].rearrange("p h l -> p (h l)"),
                                      ring[j][:]).then_inc(bank_free[j], 1)

            def inverse_sum(k, q):
                dve.wait_ge(exp_ready, k + 1)
                nc.vector.reciprocal(rinv[:, q, :], rsum[:, q, :]).then_inc(rinv_step, 1)
                dve.wait_ge(rinv_step, k + 1)
                nc.vector.tensor_scalar(rinv[:, q, :], rinv[:, q, :], nreg[:], None, ALU.mult).then_inc(rinv_ready, 1)

            def add_to_h(k):
                dve.wait_ge(pv_ready, k + 1)
                nc.vector.tensor_tensor(h[:, k, :], o_ps[:, 0:D], h[:, k, :], ALU.add).then_inc(h_added, 1)

            def step(k, q, ahead2, ahead1, back1, back2):
                if ahead2:
                    convolve(k + 2, q)
                if back2:
                    add_to_h(k - 2)
                row_max(k, q)
                if back1:
                    take_probs_t(k - 1, 0)
                    take_probs_t(k - 1, 1)
                if ahead2:
                    ln1_a(k + 2, q)
                if ahead1:
                    take_xs(k + 1, 1 - q)
                    scale_0(k + 1, 1 - q)
                if ahead2:
                    ln1_b(k + 2, q)
                    ln2_a(k + 2, q)
                    ln2_b(k + 2, q)
                inverse_sum(k, q)
                if ahead2:
                    low_part(k + 2, q)

            nc.vector.memset(nhalf[:], -0.5).then_inc(halo_set, 1)
            for q in range(2):
                nc.vector.memset(conv[q][DC:DC + 1, 0, :], 1.0).then_inc(halo_set, 1)
            nc.vector.memset(x_pad[:, :, :, 0:HALO], 0.0).then_inc(halo_set, 1)
            nc.vector.memset(x_pad[:, :, :, HALO + L:LP], 0.0).then_inc(halo_set, 1)
            dve.wait_ge(conv_in, 16 * 3)
            dve.wait_ge(halo_set, 5)
            convolve(0, 0)
            dve.wait_ge(first_in, 16 * 7)
            nc.vector.tensor_copy(identr[:], ident[:]).then_inc(identr_ready, 1)
            nc.vector.tensor_tensor(wqk[:], wqk[:], wqk[:], ALU.mult).then_inc(wqk_sq, 1)
            dve.wait_ge(wqk_sq, 1)
            nc.vector.tensor_scalar(wqk[:], wqk[:], float(D) ** -0.5, None, ALU.mult).then_inc(wqk_sq, 1)
            nc.vector.tensor_scalar(nneg[:], nreg[:], -1.0, None, ALU.mult).then_inc(nneg_ready, 1)
            ln1_a(0, 0)
            convolve(1, 1, (0,))
            ln1_b(0, 0)
            convolve(1, 1, (1,))
            ln2_a(0, 0)
            nc.vector.tensor_copy(identb[:], ident[:]).then_inc(mask_ready, 1)
            nc.vector.tensor_copy(maskb[:], maskf[:, None, :].to_broadcast([L, HG, L])).then_inc(mask_ready, 1)
            ln2_b(0, 0)
            ln1_a(1, 1)
            low_part(0, 0)
            ln1_b(1, 1)
            dve.wait_ge(wqk_sq, 2)
            take_xs(0, 0)
            scale_0(0, 0)
            ln2_a(1, 1)
            ln2_b(1, 1)
            dve.wait_ge(w_in, 16 * 4)
            dve.wait_ge(w_hi, 1)
            nc.vector.tensor_tensor(w5[:, 3, :], raw[0], f32(w5[:, 0, :]), ALU.subtract).then_inc(w_lo, 1)
            dve.wait_ge(w_hi, 2)
            nc.vector.tensor_tensor(w5[0:64, 4, :], raw[1][0:64], f32(w5[0:64, 1, :]), ALU.subtract).then_inc(w_lo, 1)
            low_part(1, 1)
            dve.wait_ge(rest_in, 32)
            step(0, 0, True, True, False, False)
            step(1, 1, True, True, True, False)
            with dve.Fori(0, 14) as it:
                for q in range(2):
                    step(it * 2 + (2 + q), q, True, True, True, True)
            def sum_heads(i):
                rows = 64 if i == 3 else L
                src = f32(w5[0:rows, (0, 2, 3, 4)[i], :]).rearrange("p (h d) -> p d h", h=H)
                nc.vector.tensor_reduce(wo_sum[0:rows, i, :], src, AX.X, ALU.add).then_inc(wo_summed, 1)

            def add_fix(images):
                lo, hi = images
                nc.vector.tensor_tensor(h[:, lo:hi, :], h[:, lo:hi, :], fix[:, None, :].to_broadcast([L, hi - lo, D]),
                                        ALU.add).then_inc(h_fixed, 1)

            step(30, 0, False, True, True, True)
            nc.vector.memset(share[:], 1.0 / VOCAB).then_inc(share_set, 1)
            nc.vector.memset(avg[0:64, 1, :], 0.0).then_inc(avg_taken, 1)
            sum_heads(0)
            sum_heads(1)
            add_to_h(29)
            row_max(31, 1)
            take_probs_t(30, 0)
            take_probs_t(30, 1)
            dve.wait_ge(wte_added, WPIECE - 1)
            nc.vector.tensor_reduce(wte_sum[:], wte_acc[:].rearrange("p (r d) -> p d r", r=WR), AX.X,
                                    ALU.add).then_inc(wte_summed, 1)
            sum_heads(2)
            sum_heads(3)
            dve.wait_ge(avg_in_bank, 1)
            nc.vector.tensor_copy(avg[:, 0, :], y_ps[:, 0:1].to_broadcast([L, L])).then_inc(avg_taken, 1)
            nc.vector.tensor_copy(avg[64:128, 1, :], y_ps[64:128, 1:2].to_broadcast([64, L])).then_inc(avg_taken, 1)
            nc.vector.tensor_copy(avg[0:64, 2, :], y_ps[0:64, 2:3].to_broadcast([64, L])).then_inc(avg_taken, 1)
            inverse_sum(31, 1)
            dve.wait_ge(nneg_ready, 1)
            dve.wait_ge(fix_in_bank, 1)
            nc.vector.tensor_scalar(fix[:], s_ps[:, 0, 0:D], nneg[:], None, ALU.mult).then_inc(fix_ready, 1)
            dve.wait_ge(fix_ready, 1)
            add_fix((POOL_IMAGES, POOL_IMAGES + 7))
            take_probs_t(31, 0)
            take_probs_t(31, 1)
            add_to_h(30)
            dve.wait_ge(h_added, B - 1)
            add_fix((POOL_IMAGES + 7, B - 1))
            add_to_h(31)
            dve.wait_ge(h_added, B)
            add_fix((B - 1, B))

        @block.scalar
        def _(act):
            def relu(k):
                act.wait_ge(ypre_ready, k + 1)
                nc.scalar.activation(h[:, k, :], ypre[:], ACT.Relu).then_inc(relu_ready, 1)

            def high_part(k, q):
                act.wait_ge(hc_ready, k + 1)
                nc.scalar.activation(xn[q][:, 0:D], hc[:, q], ACT.Identity, scale=rstd2[:, q:q + 1]).then_inc(xn_hi, 1)

            def take_xt(k, q):
                act.wait_ge(xt_in_bank, k + 1)
                nc.scalar.activation(xt[q][:].rearrange("p c l -> p (c l)"), o_ps[0:DC, 0:2 * L],
                                     ACT.Copy).then_inc(xt_ready, 1)

            def take_probs_t(k):
                act.wait_ge(pt_in_bank, k * 3 + 3)
                nc.scalar.activation(probs_t[:, 2 * HG:H, :].rearrange("p h l -> p (h l)"), ring[2][:],
                                     ACT.Copy).then_inc(bank_free[2], 1)

            def exps(k, q, heads):
                assert heads
                for i in heads:
                    ins = nc.scalar.activation(probs[:, q, i, :], s_ps[:, i // HG, L * (i % HG):L * (i % HG) + L],
                                               ACT.Exp, bias=nmax[:, q, i:i + 1], accum_out=rsum[:, q, i:i + 1])
                if heads[-1] == H - 1:
                    ins.then_inc(exp_ready, 1)

            def take_g(k, q, j):
                lo, hi = G_COLS[j]
                act.wait_ge(g_in_bank, k * 5 + (j + 1))
                nc.scalar.activation(g[q][:, lo:hi], ring[G_BANK[j]][:, 0:hi - lo],
                                     ACT.Copy).then_inc(bank_free[G_BANK[j]], 1)

            def step(k, q, ahead2, ahead1, back1):
                if back1:
                    take_probs_t(k - 1)
                if ahead1:
                    take_xt(k + 1, 1 - q)
                act.wait_ge(nmax_ready, k + 1)
                exps(k, q, (0, 1))
                for j in range(5):
                    take_g(k, q, j)
                    exps(k, q, (2 + 2 * j, 3 + 2 * j))
                    if ahead2 and j == 1:
                        relu(k + 2)
                if ahead2:
                    high_part(k + 2, q)

            relu(0)
            high_part(0, 0)
            take_xt(0, 0)
            relu(1)
            act.wait_ge(w_in, 16 * 4)
            for i in range(3):
                nc.scalar.activation(w5[:, i, :], raw[i], ACT.Copy).then_inc(w_hi, 1)
            high_part(1, 1)
            act.wait_ge(w_lo, 2)
            act.wait_ge(w_hi, 3)
            step(0, 0, True, True, False)
            step(1, 1, True, True, True)
            with act.Fori(0, 14) as it:
                for q in range(2):
                    step(it * 2 + (2 + q), q, True, True, True)
            step(30, 0, False, True, True)
            step(31, 1, False, False, True)
            take_probs_t(31)

        @block.tensor
        def _(pe):
            def pointwise(k, q):
                pe.wait_ge(conv_ready, k * 2 + 2)
                if not (isinstance(k, int) and k == 0):
                    pe.wait_ge(y_bank_free, k)
                nc.tensor.matmul(y_ps[:, 0:D], conv[q][:, 0, :], pw[:, 0, :], start=True, stop=False)
                nc.tensor.matmul(y_ps[:, 0:D], conv[q][0:DC, 1, :], pw[0:DC, 1, :], start=False,
                                 stop=True).then_inc(y_ready, 1)

            def wait_bank(i, n):
                if not (isinstance(n, int) and n <= 0):
                    pe.wait_ge(bank_free[i], n)

            def transpose_xn(k, q, used, back2):
                pe.wait_ge(xn_lo, k + 1)
                wait_bank(0, used)
                for i in range(3):
                    ins = nc.tensor.transpose(ring[0][:, L * i:L * i + L].bitcast(F32R), xn[q][:, L * i:L * i + L],
                                              identr[:])
                ins.then_inc(xs_in_bank, 1)
                if back2:
                    pe.wait_ge(h_added, k - 2)
                for c in range(2):
                    nc.tensor.matmul(o_ps[0:DC, L * c:L * c + L], xn[q][:, DC * c:DC * c + DC], identr[:],
                                     start=(c == 0), stop=False, skip_group_check=True)
                    ins = nc.tensor.matmul(o_ps[0:DC, L * c:L * c + L], xn[q][:, D + DC * c:D + DC * c + DC],
                                           identr[:], start=False, stop=(c == 1), skip_group_check=True)
                ins.then_inc(xt_in_bank, 1)

            def scores(k, q):
                pe.wait_ge(ys0_ready, k + 1)
                pe.wait_ge(ys1_ready, k + 1)
                if not (isinstance(k, int) and k == 0):
                    pe.wait_ge(exp_ready, k)
                for j in range(3):
                    nc.tensor.matmul(s_ps[:, j, :], identb[:], maskb[:].rearrange("p h l -> p (h l)"), start=True,
                                     stop=False)
                    for c in range(2):
                        ins = nc.tensor.matmul(s_ps[:, j, :], xt[q][:, c, :],
                                               ys[:, c, HG * j:HG * j + HG, :].rearrange("p h l -> p (h l)"),
                                               start=False, stop=(c == 1))
                ins.then_inc(s_ready, 1)

            def transpose_probs(k, q, used):
                pe.wait_ge(probs_ready, k + 1)
                for j in range(3):
                    wait_bank(j, used[j])
                    for i in range(HG):
                        ins = nc.tensor.transpose(ring[j][:, L * i:L * i + L], probs[:, q, HG * j + i, :], ident[:])
                    ins.then_inc(pt_in_bank, 1)

            def value_products(k, q, used, start):
                pe.wait_ge(bank_free[0], start)
                stack = [xs[q][:, i, :] for i in (0, 1, 2, 0)]
                for j in range(5):
                    lo, hi = G_COLS[j]
                    b = G_BANK[j]
                    wait_bank(b, used[b] + (1 if j >= 3 else 0))
                    for i in range(4):
                        nc.tensor.matmul(ring[b][:, 0:hi - lo], stack[i], w5[:, i, lo:hi], start=(i == 0), stop=False)
                    nc.tensor.matmul(ring[b][:, 0:hi - lo], xs[q][0:64, 1, :], w5[0:64, 4, lo:hi], start=False,
                                     stop=True).then_inc(g_in_bank, 1)

            def attend(k, q):
                for j in range(H):
                    ins = nc.tensor.matmul(o_ps[:, 0:D], probs_t[:, j, :], g[q][:, D * j:D * j + D], start=(j == 0),
                                           stop=(j == H - 1))
                ins.then_inc(pv_ready, 1)

            def step(k, q, ahead2, ahead1, back1, b0, b1, b2, after):
                scores(k, q)
                if ahead2:
                    pointwise(k + 2, q)
                n = 0
                if back1:
                    transpose_probs(k - 1, 1 - q, (b0, b1, b2))
                    n = 1
                m = 0
                if ahead1:
                    transpose_xn(k + 1, 1 - q, b0 + n, after)
                    m = 1
                if isinstance(k, int) and k == 0:
                    pe.wait_ge(w_lo, 2)
                value_products(k, q, (b0 + n + m, b1 + n, b2 + n), b0)
                if back1:
                    if ahead1:
                        pe.wait_ge(xt_ready, k + 2)
                    else:
                        pe.wait_ge(h_added, k - 1)
                    attend(k - 1, 1 - q)

            pe.wait_ge(pw_in, 16 * 2)
            pointwise(0, 0)
            pointwise(1, 1)
            pe.wait_ge(identr_ready, 1)
            transpose_xn(0, 0, 0, False)
            pe.wait_ge(mask_ready, 2)
            step(0, 0, True, True, False, 1, 0, 0, False)
            step(1, 1, True, True, True, 3, 2, 2, False)
            with pe.Fori(0, 14) as it:
                for q in range(2):
                    k = it * 2 + (2 + q)
                    step(k, q, True, True, True, it * 6 + (6 + 3 * q), it * 6 + (5 + 3 * q), it * 6 + (5 + 3 * q), True)
            step(30, 0, False, True, True, 90, 89, 89, True)
            scores(31, 1)
            transpose_probs(30, 0, (93, 92, 92))
            value_products(31, 1, (94, 93, 93), 93)
            pe.wait_ge(share_set, 1)
            pe.wait_ge(tail_in, 16)
            pe.wait_ge(wte_summed, 1)
            pe.wait_ge(y_bank_free, B)
            for i, (lo, hi) in enumerate(((0, 128), (64, 192), (128, 192))):
                nc.tensor.matmul(y_ps[0:hi - lo, i:i + 1], wte_sum[:, lo:hi], share[:], start=True, stop=False,
                                 skip_group_check=True)
                ins = nc.tensor.matmul(y_ps[0:hi - lo, i:i + 1], wte_tail[:, lo:hi], share[0:WTAIL], start=False,
                                       stop=True, skip_group_check=True)
            ins.then_inc(avg_in_bank, 1)
            pe.wait_ge(h_added, 30)
            attend(30, 0)
            pe.wait_ge(avg_taken, 4)
            pe.wait_ge(wo_summed, 4)
            pe.wait_ge(exp_ready, B)
            fix_ps = s_ps[:, 0, 0:D]
            nc.tensor.matmul(fix_ps, avg[:, 0, :], wo_sum[:, 0, :], start=True, stop=False)
            nc.tensor.matmul(fix_ps, avg[:, 1, :], wo_sum[:, 1, :], start=False, stop=False)
            nc.tensor.matmul(fix_ps, avg[:, 0, :], wo_sum[:, 2, :], start=False, stop=False)
            nc.tensor.matmul(fix_ps, avg[0:64, 2, :], wo_sum[0:64, 3, :], start=False, stop=True).then_inc(fix_in_bank, 1)
            transpose_probs(31, 1, (95, 95, 95))
            pe.wait_ge(bank_free[0], 96)
            pe.wait_ge(bank_free[1], 96)
            pe.wait_ge(bank_free[2], 96)
            pe.wait_ge(h_added, 31)
            attend(31, 1)


PAIR = 2
NPAIR = B // PAIR
NCLS = 6
NEXP = 5
HD = D // H
ROWS = 4
GR = H // ROWS
GF = ROWS * HD
ONE = HD


def store_class_tokens(sp, h, res, lo, hi, stored):
    for i in range(NCLS):
        q, t = i // 2, i % 2
        sp.dma_start(h[i:i + 1, lo:hi, :], res[B * q + lo:B * q + hi, t, :]).then_inc(stored, 16)


def feed_forward_phase(nc, io, keep, layer):
    with ExitStack() as ctx:
        def sb(name, shape, dt=F32):
            return ctx.enter_context(nc.sbuf_tensor(f"{name}_f{layer}", shape, dt))

        def psum(name, shape, dt=F32):
            return ctx.enter_context(nc.psum_tensor(f"{name}_f{layer}", shape, dt))

        def sem(name):
            return ctx.enter_context(nc.semaphore(f"{name}_f{layer}"))

        h, ident, nhalf, identr = keep["h"], keep["ident"], keep["nhalf"], keep["identr"]
        first = layer == 0
        T2 = PAIR * L

        raw1, raw2, b1, w1, w2 = keep["raw1"], keep["raw2"], keep["b1"], keep["w1"], keep["w2"]
        xf = sb("xf", [L, PAIR, D])
        xn = [sb(f"xn{q}", [L, PAIR, 2 * D], F32R) for q in range(2)]
        xs = [sb(f"xs{q}", [128, 3, T2], F32R) for q in range(2)]
        gf = sb("gf", [128, HJ, T2])
        gh = [sb(f"gh{q}", [128, HJ, T2], F32R) for q in range(2)]
        gl = [sb(f"gl{q}", [128, HJ, T2], F32R) for q in range(2)]
        stats = sb("stats", [L, PAIR, 6])
        mv = sb("mv", [L, 2, PAIR, 2])
        rstd = sb("rstd", [L, 2, PAIR])
        if first:
            b2f, att = keep["b2f"], keep["att"]
            b2 = sb("b2", [1, 2, D], F32R)
            ones = sb("ones", [1, L], F32R)
            Q, R = 3, 3 * B
            c_stats = sb("c_stats", [R, 2, 6])
            c_mv = sb("c_mv", [R, 2, 2])
            c_rstd = sb("c_rstd", [R, 2])
            c_xf = sb("c_xf", [R, 2, D])
            xt = sb("xt", [DC, 2, 2, R])
            hid_q = sb("hid_q", [128, HJ, 2, R])
            hid_t = sb("hid_t", [128, HJ, 2, R])
            lg = sb("lg", [R, 2, 2])
            gm = sb("gm", [R, 2])
            ge = sb("ge", [R, 2, 2])
            gate = sb("gate", [R, 2, 2])
            part = sb("part", [R, 2, D])
            part2 = sb("part2", [R, 2, D])
            res = keep["cls_res"]

        x_ps = [psum(f"x_ps{i}", [128, BANK]) for i in range(PAIR)]
        hid_ps = [psum(f"hid_ps{i}", [128, BANK]) for i in range(3)]
        out_ps = [psum(f"out_ps{q}", [L, BANK]) for q in range(2)]
        if first:
            cls_ps = psum("cls_ps", [128, BANK])
            xt_ps, lg_ps = cls_ps[0:DC, 0:4 * R], cls_ps[0:R, 4 * R:4 * R + 4 * NCLS]
            high_ps = out_ps[0][0:R, 0:2 * D]
            low_ps = cls_ps[0:R, 0:2 * D]

        stats_ready = sem("stats_ready")
        stats_step = sem("stats_step")
        rstd_ready = sem("rstd_ready")
        xf_ready = sem("xf_ready")
        xf_used = sem("xf_used")
        xn_hi = sem("xn_hi")
        xn_lo = sem("xn_lo")
        x_in_bank = sem("x_in_bank")
        xs_ready = sem("xs_ready")
        hid_in_bank = sem("hid_in_bank")
        gelu_ready = sem("gelu_ready")
        g_hi = sem("g_hi")
        g_lo = sem("g_lo")
        out_ready = sem("out_ready")
        h_added = sem("h_added")
        stored = sem("stored")
        ATT_LOADS = 8 * ROWS + 2
        cls = keep["cls"] if first else None
        if first:
            w_hi = sem("w_hi")
            w_lo = sem("w_lo")
            b2_hi = sem("b2_hi")
            tok_in = sem("tok_in")
            cls_in = sem("cls_in")
            pads_set = sem("pads_set")
            att_in = sem("att_in")
            att_hi = sem("att_hi")
            c_step = sem("c_step")
            c_var_ready = sem("c_var_ready")
            c_rstd_ready = sem("c_rstd_ready")
            c_xf_ready = sem("c_xf_ready")
            xt_in_bank = sem("xt_in_bank")
            xt_ready = sem("xt_ready")
            lg_in_bank = sem("lg_in_bank")
            lg_shifted = sem("lg_shifted")
            exp_ready = sem("exp_ready")
            c_hid_in_bank = sem("c_hid_in_bank")
            c_gelu_ready = sem("c_gelu_ready")
            c_out_ready = sem("c_out_ready")
            res_ready = sem("res_ready")
            res_stored = sem("res_stored")

        block = ctx.enter_context(nc.Block())
        BREAK = NPAIR - 4

        @block.sync
        def _(sp):
            if first:
                for i in range(NCLS):
                    q, t = i // 2, i % 2
                    sp.dma_start(cls["tok"][B * q:B * q + B, t, :], h[i:i + 1, :, :]).then_inc(tok_in, 16)
                for e in range(NEXP):
                    sp.dma_start(cls["a1"][:, e], io["a1"][e].rearrange("(c p) f -> p c f", c=2)).then_inc(cls_in, 16)
                    sp.dma_start(cls["a2"][:, e], io["a2"][e].rearrange("(j p) d -> p j d", p=128)).then_inc(cls_in, 16)
                sp.dma_start(cls["a1b"][:], io["a1b"]).then_inc(cls_in, 16)
                sp.dma_start(cls["gw"][:], io["gw"].rearrange("(c p) n -> p c n", c=2)).then_inc(cls_in, 16)
                for t in range(2):
                    sp.dma_start(cls["b_high"][:, t, :], io["a2b"][3 + t:4 + t].to_broadcast([3 * B, D])).then_inc(cls_in, 16)
                for q in range(3):
                    sp.dma_start(cls["b_low"][B * q:B * q + B, :], io["a2b"][q:q + 1].to_broadcast([B, D])).then_inc(cls_in, 16)
                sp.wait_ge(pads_set, 4)
                w = io["w_qkv"].rearrange("(g p) d e -> p d g e", p=ROWS)
                for p in range(ROWS):
                    for part in range(2):
                        rows = slice(GF * part + HD * p, GF * part + HD * p + HD)
                        for i in range(2):
                            sp.dma_start(att["wqk_raw"][rows, :, i, 32 * p:32 * p + HD],
                                         w[p][:, :, HD * i:HD * i + HD]).then_inc(att_in, 16)
                        sp.dma_start(att["wv_raw"][rows, :, HD * p:HD * p + HD], w[p][:, :, 2 * HD:3 * HD]).then_inc(att_in, 16)
                    sp.dma_start(att["bqk"][32 * p:32 * p + HD], io["b_qk"][p]).then_inc(att_in, 16)
                sp.dma_start(att["bv"][:], io["b_v"].to_broadcast([L, D])).then_inc(att_in, 16)
                w = io["w_out"].rearrange("(g p d) e -> p d g e", p=ROWS, g=GR)
                for p in range(ROWS):
                    sp.dma_start(att["wo"][32 * p:32 * p + HD], w[p]).then_inc(att_in, 16)
                sp.dma_start(att["wo"][ONE:ONE + 1, 0, :], io["b_out"]).then_inc(att_in, 16)
                sp.wait_ge(att_in, 16 * ATT_LOADS)
                sp.wait_ge(cls_in, 16 * (2 * NEXP + 7))
                sp.wait_ge(res_ready, 1)
                sp.wait_ge(h_added, BREAK)
                store_class_tokens(sp, h, res, 0, BREAK * PAIR, res_stored)
                sp.wait_ge(res_stored, 16 * NCLS)
            else:
                out_v = io["out"].rearrange("b l d -> l b d")
                with sp.Fori(0, NPAIR) as u:
                    sp.wait_ge(h_added, u + 1)
                    sp.dma_start(out_v[:, bass.ds(u * PAIR, PAIR), :], h[:, bass.ds(u * PAIR, PAIR), :]).then_inc(stored, 16)
                sp.wait_ge(stored, 16 * NPAIR)

        @block.gpsimd
        def _(pool):
            def rstd_of(u, q):
                pool.wait_ge(stats_ready, u + 1)
                nc.gpsimd.tensor_tensor(rstd[:, q, :], mv[:, q, :, 1], nhalf[:].to_broadcast([L, PAIR]),
                                        ALU.pow).then_inc(rstd_ready, 1)

            rstd_of(0, 0)
            rstd_of(1, 1)
            if first:
                nc.gpsimd.memset(att["wqk_raw"][:].rearrange("p g i m -> p (g i m)"), 0.0).then_inc(pads_set, 1)
                nc.gpsimd.memset(att["wv_raw"][:], 0.0).then_inc(pads_set, 1)
                nc.gpsimd.memset(att["bqk"][:], 0.0).then_inc(pads_set, 1)
                nc.gpsimd.memset(att["wo"][:], 0.0).then_inc(pads_set, 1)
            rstd_of(2, 0)
            rstd_of(3, 1)
            if first:
                pool.wait_ge(c_var_ready, 1)
                nc.gpsimd.tensor_tensor(c_rstd[:], c_mv[:, :, 1], nhalf[0:R].to_broadcast([R, 2]),
                                        ALU.pow).then_inc(c_rstd_ready, 1)
            with pool.Fori(0, (NPAIR - 4) // 2) as it:
                for q in range(2):
                    rstd_of(it * 2 + (4 + q), q)

        @block.vector
        def _(dve):
            def normalise(u, q):
                for i in range(PAIR):
                    nc.vector.bn_stats(stats[:, i], h[:, u * PAIR + i, :])
                    dve.drain()
                    ins = nc.vector.bn_aggr(mv[:, q, i], stats[:, i])
                ins.then_inc(stats_step, 1)
                dve.wait_ge(stats_step, u + 1)
                nc.vector.tensor_scalar(mv[:, q, :, 1], mv[:, q, :, 1], EPS_LN, None, ALU.add).then_inc(stats_ready, 1)

            def centre(u, q):
                dve.wait_ge(rstd_ready, u + 1)
                for i in range(PAIR):
                    nc.vector.tensor_scalar(xf[:, i, :], h[:, u * PAIR + i, :], mv[:, q, i, 0:1], rstd[:, q, i:i + 1],
                                            ALU.subtract, ALU.mult).then_inc(xf_ready, 1)

            def low_part(u, q):
                dve.wait_ge(xn_hi, u + 1)
                nc.vector.tensor_tensor(xn[q][:, :, D:2 * D], xf[:], f32(xn[q][:, :, 0:D]),
                                        ALU.subtract).then_inc(xn_lo, 1)
                dve.wait_ge(xn_lo, u + 1)

            def take_xs(u, q):
                for i in range(PAIR):
                    dve.wait_ge(x_in_bank, u * PAIR + (i + 1))
                    nc.vector.tensor_copy(xs[q][:, :, L * i:L * i + L],
                                          x_ps[i][:, 0:3 * L].rearrange("p (s l) -> p s l", l=L)).then_inc(xs_ready, 1)

            def low_gelu(u, q):
                dve.wait_ge(g_hi, u + 1)
                nc.vector.tensor_tensor(gl[q][:], gf[:], f32(gh[q][:]), ALU.subtract).then_inc(g_lo, 1)

            def add_to_h(u, q):
                dve.wait_ge(out_ready, u + 1)
                hp = h[:, bass.ds(u * PAIR, PAIR), :] if not isinstance(u, int) else h[:, u * PAIR:u * PAIR + PAIR, :]
                nc.vector.tensor_tensor(hp, out_ps[q][:, 0:PAIR * D].rearrange("p (i d) -> p i d", i=PAIR), hp,
                                        ALU.add).then_inc(h_added, 1)

            steps = [0]

            def small(ins):
                steps[0] += 1
                ins.then_inc(c_step, 1)
                dve.wait_ge(c_step, steps[0])

            def class_statistics():
                for t in range(2):
                    small(nc.vector.bn_stats(c_stats[:, t], cls["tok"][:, t, :]))
                    small(nc.vector.bn_aggr(c_mv[:, t], c_stats[:, t]))
                nc.vector.tensor_scalar(c_mv[:, :, 1], c_mv[:, :, 1], EPS_LN, None, ALU.add).then_inc(c_var_ready, 1)

            def class_norm():
                dve.wait_ge(c_rstd_ready, 1)
                for t in range(2):
                    nc.vector.tensor_scalar(c_xf[:, t, :], cls["tok"][:, t, :], c_mv[:, t, 0:1], c_rstd[:, t:t + 1],
                                            ALU.subtract, ALU.mult).then_inc(c_xf_ready, 1)

            def class_gates():
                dve.wait_ge(lg_in_bank, 1)
                for t in range(2):
                    for q in range(Q):
                        rows, i = slice(B * q, B * q + B), 2 * q + t
                        at = 2 * NCLS * t + 2 * i
                        small(nc.vector.tensor_copy(lg[rows, t, :], lg_ps[rows, at:at + 2]))
                small(nc.vector.tensor_reduce(gm[:], lg[:], AX.X, ALU.max))
                nc.vector.tensor_tensor(lg[:], lg[:], gm[:, :, None].to_broadcast([R, 2, 2]),
                                        ALU.subtract).then_inc(lg_shifted, 1)
                dve.wait_ge(exp_ready, 1)
                small(nc.vector.tensor_reduce(gm[:], ge[:], AX.X, ALU.add))
                small(nc.vector.reciprocal(gm[:], gm[:]))
                small(nc.vector.tensor_tensor(ge[:], ge[:], gm[:, :, None].to_broadcast([R, 2, 2]), ALU.mult))
                small(nc.vector.tensor_reduce(gm[:], ge[:], AX.X, ALU.min))
                small(nc.vector.tensor_tensor(gate[:], ge[:], gm[:, :, None].to_broadcast([R, 2, 2]), ALU.is_gt))
                small(nc.vector.tensor_tensor(gate[:], gate[:], ge[:], ALU.mult))
                small(nc.vector.tensor_reduce(gm[:], gate[:], AX.X, ALU.add))
                small(nc.vector.tensor_scalar(gm[:], gm[:], 1e-6, None, ALU.max))
                small(nc.vector.reciprocal(gm[:], gm[:]))
                small(nc.vector.tensor_tensor(gate[:], gate[:], gm[:, :, None].to_broadcast([R, 2, 2]), ALU.mult))

            def class_results():
                dve.wait_ge(c_out_ready, 1)
                small(nc.vector.tensor_tensor(part[:].rearrange("p t d -> p (t d)"), high_ps,
                                              cls["b_high"][:].rearrange("p t d -> p (t d)"), ALU.add))
                small(nc.vector.tensor_tensor(part2[:], low_ps.rearrange("p (t d) -> p t d", t=2),
                                              cls["b_low"][:, None, :].to_broadcast([R, 2, D]), ALU.add))
                for t in range(2):
                    small(nc.vector.scalar_tensor_tensor(res[:, t, :], part[:, t, :], gate[:, t, 0:1],
                                                         cls["tok"][:, t, :], ALU.mult, ALU.add))
                for t in range(2):
                    ins = nc.vector.scalar_tensor_tensor(res[:, t, :], part2[:, t, :], gate[:, t, 1:2], res[:, t, :],
                                                         ALU.mult, ALU.add)
                    if t == 0:
                        small(ins)
                ins.then_inc(res_ready, 1)

            def step(u, q, ahead3, ahead2, ahead1, back1):
                if ahead2:
                    take_xs(u + 2, q)
                if back1:
                    add_to_h(u - 1, 1 - q)
                if ahead3:
                    normalise(u + 3, 1 - q)
                if ahead3:
                    centre(u + 3, 1 - q)
                    low_part(u + 3, 1 - q)
                if ahead1:
                    low_gelu(u + 1, 1 - q)

            for u in range(3):
                normalise(u, u % 2)
                centre(u, u % 2)
                low_part(u, u % 2)
                if u == 0 and first:
                    dve.wait_ge(w_hi, 3)
                    nc.vector.tensor_tensor(w1[:, 3, :], raw1[:, 0, :], f32(w1[:, 0, :]), ALU.subtract).then_inc(w_lo, 1)
                    nc.vector.tensor_tensor(w1[0:64, 4, :], raw1[0:64, 1, :], f32(w1[0:64, 1, :]),
                                            ALU.subtract).then_inc(w_lo, 1)
                if u == 0:
                    take_xs(0, 0)
                if u == 1 and first:
                    dve.wait_ge(w_hi, 4)
                    nc.vector.tensor_tensor(w2[:, 1], raw2[:], f32(w2[:, 0]), ALU.subtract).then_inc(w_lo, 1)
                    nc.vector.tensor_copy(b2[:, 0], b2f[:]).then_inc(b2_hi, 1)
                    dve.wait_ge(b2_hi, 1)
                    nc.vector.tensor_tensor(b2[:, 1], b2f[:], f32(b2[:, 0]), ALU.subtract).then_inc(w_lo, 1)
                    nc.vector.tensor_scalar(ones[:], ident[0:1, :], 0.0, 1.0, ALU.mult, ALU.add).then_inc(w_lo, 1)
                if u == 1:
                    take_xs(1, 1)
            low_gelu(0, 0)
            if first:
                dve.wait_ge(tok_in, 16 * NCLS)
            step(0, 0, True, True, True, False)
            if first:
                class_statistics()
            step(1, 1, True, True, True, True)
            if first:
                class_norm()
                dve.wait_ge(xt_in_bank, 1)
                nc.vector.tensor_copy(xt[:].rearrange("p c t r -> p (c t r)"), xt_ps).then_inc(xt_ready, 1)
            with dve.Fori(0, (BREAK - 2) // 2) as it:
                for q in range(2):
                    step(it * 2 + (2 + q), q, True, True, True, True)
            if first:
                class_gates()
                dve.wait_ge(cls_in, 16 * (2 * NEXP + 7))
                class_results()
            for u in range(BREAK, NPAIR):
                step(u, u % 2, u + 3 < NPAIR, u + 2 < NPAIR, u + 1 < NPAIR, True)
                if u == NPAIR - 3 and first:
                    dve.wait_ge(att_in, 16 * ATT_LOADS)
                    nc.vector.tensor_scalar(att["bqk"][:, :, 0:1], att["bqk"][:, :, 0:1], SCALE, None, ALU.mult)
                    nc.vector.tensor_copy(att["wqk"][:], att["wqk_raw"][:]).then_inc(att_hi, 1)
                    nc.vector.tensor_copy(att["wv"][:], att["wv_raw"][:]).then_inc(att_hi, 1)
                if u == NPAIR - 2 and first:
                    dve.wait_ge(att_hi, 2)
                    nc.vector.tensor_tensor(att["wqk_lo"][:], att["wqk_raw"][0:GF], f32(att["wqk"][0:GF]), ALU.subtract)
                    nc.vector.tensor_tensor(att["wv_lo"][:], att["wv_raw"][0:GF], f32(att["wv"][0:GF]), ALU.subtract)
            add_to_h(NPAIR - 1, (NPAIR - 1) % 2)

        @block.scalar
        def _(act):
            def high_part(u, q):
                act.wait_ge(xf_ready, u * PAIR + PAIR)
                nc.scalar.activation(xn[q][:, :, 0:D], xf[:], ACT.Copy).then_inc(xn_hi, 1)

            def high_gelu(u, q):
                act.wait_ge(gelu_ready, u * 3 + 3)
                nc.scalar.activation(gh[q][:], gf[:], ACT.Copy).then_inc(g_hi, 1)

            def gelu(u):
                for i in range(3):
                    act.wait_ge(hid_in_bank, u * 3 + (i + 1))
                    if i == 0 and not (isinstance(u, int) and u == 0):
                        act.wait_ge(g_lo, u)
                    for j in range(2):
                        c = 2 * i + j
                        ins = nc.scalar.activation(gf[:, c, :], hid_ps[i][:, T2 * j:T2 * j + T2], ACT.Gelu,
                                                   bias=b1[:, c:c + 1])
                    ins.then_inc(gelu_ready, 1)

            def step(u, q, ahead3, ahead1):
                if ahead1:
                    gelu(u + 1)
                if ahead3:
                    high_part(u + 3, 1 - q)
                if ahead1:
                    high_gelu(u + 1, 1 - q)

            def class_experts():
                act.wait_ge(lg_shifted, 1)
                nc.scalar.activation(ge[:], lg[:], ACT.Exp).then_inc(exp_ready, 1)
                for e in range(NEXP):
                    n = 2 * B if e < Q else R
                    for half in range(2):
                        act.wait_ge(c_hid_in_bank, 2 * e + half + 1)
                        for j in range(3):
                            f = 3 * half + j
                            src = hid_ps[(2 * e + half) % 3][:, n * j:n * j + n]
                            if e < Q:
                                src = src.rearrange("p (t b) -> p t b", t=2)
                                dst = hid_q[:, f, :, B * e:B * e + B]
                            else:
                                dst = hid_t[:, f, e - Q, :]
                            ins = nc.scalar.activation(dst, src, ACT.Gelu, bias=cls["a1b"][:, e, f:f + 1])
                        ins.then_inc(c_gelu_ready, 1)

            if first:
                for i in range(3):
                    nc.scalar.activation(w1[:, i, :], raw1[:, i, :], ACT.Copy).then_inc(w_hi, 1)
            high_part(0, 0)
            if first:
                nc.scalar.activation(w2[:, 0], raw2[:], ACT.Copy).then_inc(w_hi, 1)
            high_part(1, 1)
            gelu(0)
            high_part(2, 0)
            high_gelu(0, 0)
            step(0, 0, True, True)
            step(1, 1, True, True)
            with act.Fori(0, (BREAK - 2) // 2) as it:
                for q in range(2):
                    step(it * 2 + (2 + q), q, True, True)
            if first:
                act.wait_ge(cls_in, 16 * (2 * NEXP + 7))
                class_experts()
            for u in range(BREAK, NPAIR):
                step(u, u % 2, u + 3 < NPAIR, u + 1 < NPAIR)

        @block.tensor
        def _(pe):
            def transpose_x(u, q):
                pe.wait_ge(xn_lo, u + 1)
                if not (isinstance(u, int) and u == 0):
                    pe.wait_ge(xs_ready, u * PAIR)
                for i in range(PAIR):
                    for s in range(3):
                        ins = nc.tensor.transpose(x_ps[i][:, L * s:L * s + L].bitcast(F32R),
                                                  xn[q][:, i, L * s:L * s + L], identr[:])
                    ins.then_inc(x_in_bank, 1)

            def hidden(u, q):
                pe.wait_ge(xs_ready, u * PAIR + PAIR)
                for c in range(HJ):
                    bank, at = hid_ps[c // 2], T2 * (c % 2)
                    if c % 2 == 0 and not (isinstance(u, int) and u == 0):
                        pe.wait_ge(gelu_ready, u * 3 + (c // 2 - 2))
                    cols = slice(128 * c, 128 * c + 128)
                    for s in range(4):
                        nc.tensor.matmul(bank[:, at:at + T2], w1[:, s, cols], xs[q][:, s % 3, :], start=(s == 0),
                                         stop=False)
                    ins = nc.tensor.matmul(bank[:, at:at + T2], w1[0:64, 4, cols], xs[q][0:64, 1, :], start=False,
                                           stop=True)
                    if c % 2 == 1:
                        ins.then_inc(hid_in_bank, 1)

            def project(u, q):
                pe.wait_ge(g_hi, u + 1)
                pe.wait_ge(g_lo, u + 1)
                if not (isinstance(u, int) and u < 2):
                    pe.wait_ge(h_added, u - 1)
                for i in range(PAIR):
                    out = out_ps[q][:, D * i:D * i + D]
                    t = slice(L * i, L * i + L)
                    if first:
                        nc.tensor.matmul(out, ones[:], b2[:, 0], start=True, stop=False)
                        nc.tensor.matmul(out, ones[:], b2[:, 1], start=False, stop=False)
                    for c in range(HJ):
                        nc.tensor.matmul(out, gh[q][:, c, t], w2[:, 0, c, :], start=(c == 0 and not first), stop=False)
                        nc.tensor.matmul(out, gh[q][:, c, t], w2[:, 1, c, :], start=False, stop=False)
                        ins = nc.tensor.matmul(out, gl[q][:, c, t], w2[:, 0, c, :], start=False, stop=(c == HJ - 1))
                ins.then_inc(out_ready, 1)

            def transpose_classes():
                pe.wait_ge(c_xf_ready, 2)
                for t in range(2):
                    for c in range(2):
                        at = (2 * c + t) * R
                        ins = nc.tensor.transpose(xt_ps[:, at:at + R], c_xf[:, t, DC * c:DC * c + DC], ident[0:R, 0:R])
                ins.then_inc(xt_in_bank, 1)

            def columns(e):
                if e < Q:
                    return lambda c: xt[:, c, :, B * e:B * e + B]
                return lambda c: xt[:, c, e - Q, :]

            def class_experts():
                pe.wait_ge(xt_ready, 1)
                for t in range(2):
                    for c in range(2):
                        ins = nc.tensor.matmul(lg_ps[:, 2 * NCLS * t:2 * NCLS * (t + 1)], xt[:, c, t, :],
                                               cls["gw"][:, c, :], start=(c == 0), stop=(c == 1))
                ins.then_inc(lg_in_bank, 1)
                pe.wait_ge(gelu_ready, 3 * BREAK + 3)
                for e in range(NEXP):
                    n = 2 * B if e < Q else R
                    for half in range(2):
                        u = 2 * e + half
                        if u >= 3:
                            pe.wait_ge(c_gelu_ready, u - 2)
                        for j in range(3):
                            out = hid_ps[u % 3][:, n * j:n * j + n]
                            if e < Q:
                                out = out.rearrange("p (t b) -> p t b", t=2)
                            f = (3 * half + j) * 128
                            for c in range(2):
                                ins = nc.tensor.matmul(out, cls["a1"][:, e, c, f:f + 128], columns(e)(c),
                                                       start=(c == 0), stop=(c == 1))
                        ins.then_inc(c_hid_in_bank, 1)
                pe.wait_ge(h_added, BREAK - 1)
                pe.wait_ge(lg_shifted, 1)
                pe.wait_ge(c_gelu_ready, 2 * NEXP)
                for t in range(2):
                    for j in range(HJ):
                        nc.tensor.matmul(high_ps[:, D * t:D * t + D], hid_q[:, j, t, :], cls["a2"][:, Q + t, j, :],
                                         start=(j == 0), stop=(j == HJ - 1))
                    for q in range(Q):
                        rows = slice(B * q, B * q + B)
                        for j in range(HJ):
                            ins = nc.tensor.matmul(low_ps[rows, D * t:D * t + D], hid_t[:, j, t, rows],
                                                   cls["a2"][:, q, j, :], start=(j == 0), stop=(j == HJ - 1))
                ins.then_inc(c_out_ready, 1)

            def step(u, q, ahead2, ahead1):
                if ahead2:
                    transpose_x(u + 2, q)
                if ahead1:
                    hidden(u + 1, 1 - q)
                if isinstance(u, int) and u == BREAK and first:
                    pe.wait_ge(res_ready, 1)
                project(u, q)

            transpose_x(0, 0)
            if first:
                pe.wait_ge(w_lo, 2)
            hidden(0, 0)
            transpose_x(1, 1)
            hidden(1, 1)
            transpose_x(2, 0)
            if first:
                pe.wait_ge(w_lo, 5)
            project(0, 0)
            step(1, 1, True, True)
            if first:
                transpose_classes()
            with pe.Fori(0, (BREAK - 2) // 2) as it:
                for q in range(2):
                    step(it * 2 + (2 + q), q, True, True)
            if first:
                pe.wait_ge(cls_in, 16 * (2 * NEXP + 7))
                class_experts()
            for u in range(BREAK, NPAIR):
                step(u, u % 2, u + 2 < NPAIR, u + 1 < NPAIR)


def attention_phase(nc, io, keep):
    with ExitStack() as ctx:
        def sb(name, shape, dt=F32):
            return ctx.enter_context(nc.sbuf_tensor(f"{name}_a", shape, dt))

        def psum(name, shape, dt=F32):
            return ctx.enter_context(nc.psum_tensor(f"{name}_a", shape, dt))

        def sem(name):
            return ctx.enter_context(nc.semaphore(f"{name}_a"))

        h, ident, nhalf, identr = keep["h"], keep["ident"], keep["nhalf"], keep["identr"]
        att = keep["att"]
        wqk, wqk_lo, wv, wv_lo = att["wqk"], att["wqk_lo"], att["wv"], att["wv_lo"]
        bqk, bv, wo = att["bqk"], att["bv"], att["wo"]
        raw1, raw2, w1, w2 = keep["raw1"], keep["raw2"], keep["w1"], keep["w2"]
        stats = sb("stats", [L, 6])
        mv = sb("mv", [L, 2, 2])
        rstd = sb("rstd", [L, 2])
        xf = sb("xf", [L, D])
        xn = [sb(f"xn{q}", [L, GR, 2, GF], F32R) for q in range(2)]
        xs = [sb(f"xs{q}", [128, GR, L], F32R) for q in range(2)]
        qt = [sb(f"qt{q}", [128, GR, L]) for q in range(2)]
        kt = [sb(f"kt{q}", [128, GR, L]) for q in range(2)]
        v = [sb(f"v{q}", [L, GR, ROWS, 32]) for q in range(2)]
        nmax = sb("nmax", [L, 2, ROWS, GR])
        probs = sb("probs", [L, 2, ROWS * GR, L])
        probs_t = sb("probs_t", [L, ROWS * GR, L])
        rsum = sb("rsum", [L, 2, ROWS * GR])
        rinv = sb("rinv", [L, 2, ROWS * GR])
        ot = sb("ot", [128, GR, L])

        s_ps = psum("s_ps", [L, ROWS, BANK])
        r_ps = [psum(f"r_ps{i}", [128, BANK]) for i in range(4)]

        pads_set = sem("pads_set")
        ff_in = sem("ff_in")
        ff_hi = sem("ff_hi")
        cls_stored = sem("cls_stored")
        STORED = B - 4 * PAIR
        aggr_step = sem("aggr_step")
        var_ready = sem("var_ready")
        rstd_ready = sem("rstd_ready")
        xf_ready = sem("xf_ready")
        xn_hi = sem("xn_hi")
        xn_lo = sem("xn_lo")
        x_in_bank = sem("x_in_bank")
        q_in_bank = sem("q_in_bank")
        k_in_bank = sem("k_in_bank")
        v_in_bank = sem("v_in_bank")
        s_ready = sem("s_ready")
        nmax_ready = sem("nmax_ready")
        exp_ready = sem("exp_ready")
        pt_in_bank = sem("pt_in_bank")
        o_in_bank = sem("o_in_bank")
        rinv_ready = sem("rinv_ready")
        probs_ready = sem("probs_ready")
        y_in_bank = sem("y_in_bank")
        r_free = [sem(f"r_free{i}") for i in range(4)]
        block = ctx.enter_context(nc.Block())

        @block.sync
        def _(sp):
            store_class_tokens(sp, h, keep["cls_res"], STORED, B, cls_stored)
            load_feed_forward(sp, io, keep, "ffn1", ff_in)
            sp.wait_ge(cls_stored, 16 * NCLS)
            sp.wait_ge(ff_in, 16 * FF_LOADS)

        @block.gpsimd
        def _(pool):
            def rstd_of(k, q):
                pool.wait_ge(var_ready, k + 1)
                nc.gpsimd.tensor_tensor(rstd[:, q:q + 1], mv[:, q, 1:2], nhalf[:], ALU.pow).then_inc(rstd_ready, 1)

            def normalise(k, q):
                for half in range(2):
                    heads = slice(H // 2 * half, H // 2 * half + H // 2)
                    pool.wait_ge(rinv_ready, k * 2 + (half + 1))
                    nc.gpsimd.tensor_tensor(probs[:, q, heads], probs[:, q, heads],
                                            rinv[:, q, heads, None].to_broadcast([L, H // 2, L]),
                                            ALU.mult).then_inc(probs_ready, 1)

            rstd_of(0, 0)
            rstd_of(1, 1)
            with pool.Fori(0, (B - 2) // 2) as it:
                for q in range(2):
                    rstd_of(it * 2 + (2 + q), q)
                    normalise(it * 2 + q, q)
            normalise(B - 2, 0)
            normalise(B - 1, 1)

        @block.vector
        def _(dve):
            def variance(k, q):
                nc.vector.bn_stats(stats[:], h[:, k, :])
                dve.drain()
                nc.vector.bn_aggr(mv[:, q], stats[:]).then_inc(aggr_step, 1)
                dve.wait_ge(aggr_step, k + 1)
                nc.vector.tensor_scalar(mv[:, q, 1:2], mv[:, q, 1:2], EPS_LN, None, ALU.add).then_inc(var_ready, 1)

            def centre(k, q):
                dve.wait_ge(rstd_ready, k + 1)
                nc.vector.tensor_scalar(xf[:], h[:, k, :], mv[:, q, 0:1], rstd[:, q:q + 1], ALU.subtract,
                                        ALU.mult).then_inc(xf_ready, 1)

            def low_part(k, q):
                dve.wait_ge(xn_hi, k + 1)
                nc.vector.tensor_tensor(xn[q][:, :, 1, :], xf[:].rearrange("l (g f) -> l g f", g=GR),
                                        f32(xn[q][:, :, 0, :]), ALU.subtract).then_inc(xn_lo, 1)
                dve.wait_ge(xn_lo, k + 1)

            def take_xs(k, q):
                dve.wait_ge(x_in_bank, k + 1)
                nc.vector.tensor_copy(xs[q][:].rearrange("p g l -> p (g l)"), r_ps[0][:, 0:GR * L]).then_inc(r_free[0], 1)

            def take_qk(k, q):
                dve.wait_ge(q_in_bank, k + 1)
                nc.vector.scalar_tensor_tensor(qt[q][:], r_ps[1][:, 0:GR * L].rearrange("p (g l) -> p g l", g=GR), SCALE,
                                               bqk[:, :, 0:1].to_broadcast([128, GR, L]), ALU.mult,
                                               ALU.add).then_inc(r_free[1], 1)
                dve.wait_ge(k_in_bank, k + 1)
                nc.vector.tensor_tensor(kt[q][:], r_ps[2][:, 0:GR * L].rearrange("p (g l) -> p g l", g=GR),
                                        bqk[:, :, 1:2].to_broadcast([128, GR, L]), ALU.add).then_inc(r_free[2], 1)

            def take_v(k, q):
                dve.wait_ge(v_in_bank, k + 1)
                nc.vector.tensor_tensor(v[q][:].rearrange("l g p d -> l (g p) d")[:, :, 0:HD],
                                        r_ps[0][:, 0:D].rearrange("l (i d) -> l i d", i=H),
                                        bv[:].rearrange("l (i d) -> l i d", i=H), ALU.add).then_inc(r_free[0], 1)

            def row_max(k, q, half):
                dve.wait_ge(s_ready, k * 2 + (half + 1))
                nc.vector.tensor_reduce(nmax[:, q, 2 * half:2 * half + 2, :],
                                        s_ps[:, 2 * half:2 * half + 2, 0:GR * L].rearrange(
                                            "l p (g m) -> l p g m", g=GR),
                                        AX.X, ALU.max, negate=True).then_inc(nmax_ready, 1)

            def take_probs_t(k):
                dve.wait_ge(pt_in_bank, k * 3 + 1)
                nc.vector.tensor_copy(probs_t[:, 0:4, :].rearrange("t i l -> t (i l)"), r_ps[0][:]).then_inc(r_free[0], 1)

            def inverse_sum(k, q, half):
                heads = slice(H // 2 * half, H // 2 * half + H // 2)
                dve.wait_ge(exp_ready, k * 2 + (half + 1))
                nc.vector.reciprocal(rinv[:, q, heads], rsum[:, q, heads]).then_inc(rinv_ready, 1)

            def add_to_h(k):
                dve.wait_ge(y_in_bank, k + 1)
                nc.vector.tensor_tensor(h[:, k, :], r_ps[3][:, 0:D], h[:, k, :], ALU.add).then_inc(r_free[3], 1)

            def step(k, q, main, ahead2, ahead1, back1, back2):
                if ahead2:
                    variance(k + 2, q)
                if main:
                    row_max(k, q, 0)
                if ahead1:
                    take_xs(k + 1, 1 - q)
                if ahead2:
                    centre(k + 2, q)
                if main:
                    row_max(k, q, 1)
                    inverse_sum(k, q, 0)
                    take_v(k, q)
                if ahead1:
                    take_qk(k + 1, 1 - q)
                if ahead2:
                    low_part(k + 2, q)
                if back2:
                    add_to_h(k - 2)
                if main:
                    inverse_sum(k, q, 1)
                if back1:
                    take_probs_t(k - 1)

            for q in range(2):
                nc.vector.memset(v[q][:], 0.0).then_inc(pads_set, 1)
            for k in range(2):
                variance(k, k)
                centre(k, k)
                low_part(k, k)
            dve.wait_ge(pads_set, 2)
            take_xs(0, 0)
            take_qk(0, 0)
            step(0, 0, True, True, True, False, False)
            step(1, 1, True, True, True, True, False)
            dve.wait_ge(cls_stored, 16 * NCLS)
            with dve.Fori(0, (B - 4) // 2) as it:
                for q in range(2):
                    step(it * 2 + (2 + q), q, True, True, True, True, True)
            step(B - 2, 0, True, False, True, True, True)
            step(B - 1, 1, True, False, False, True, True)
            step(B, 0, False, False, False, True, True)
            dve.wait_ge(ff_hi, 2)
            nc.vector.tensor_tensor(w1[:, 3, :], raw1[:, 0, :], f32(w1[:, 0, :]), ALU.subtract)
            nc.vector.tensor_tensor(w1[0:64, 4, :], raw1[0:64, 1, :], f32(w1[0:64, 1, :]), ALU.subtract)
            nc.vector.tensor_tensor(w2[:, 1], raw2[:], f32(w2[:, 0]), ALU.subtract)
            step(B + 1, 1, False, False, False, False, True)

        @block.scalar
        def _(act):
            def high_part(k, q):
                act.wait_ge(xf_ready, k + 1)
                nc.scalar.activation(xn[q][:, :, 0, :], xf[:].rearrange("l (g f) -> l g f", g=GR),
                                     ACT.Copy).then_inc(xn_hi, 1)

            def exps(k, q, half):
                act.wait_ge(nmax_ready, k * 2 + (half + 1))
                for p in (2 * half, 2 * half + 1):
                    for g in range(GR):
                        ins = nc.scalar.activation(probs[:, q, GR * p + g, :], s_ps[:, p, L * g:L * g + L], ACT.Exp,
                                                   bias=nmax[:, q, p, g:g + 1],
                                                   accum_out=rsum[:, q, GR * p + g:GR * p + g + 1])
                ins.then_inc(exp_ready, 1)

            def take_probs_t(k, i):
                act.wait_ge(pt_in_bank, k * 3 + (i + 1))
                nc.scalar.activation(probs_t[:, 4 * i:4 * i + 4, :].rearrange("t i l -> t (i l)"), r_ps[i][:],
                                     ACT.Copy).then_inc(r_free[i], 1)

            def take_o(k):
                act.wait_ge(o_in_bank, k + 1)
                nc.scalar.activation(ot[:].rearrange("p g l -> p (g l)"), r_ps[3][:, 0:GR * L], ACT.Identity,
                                     bias=ident[:, ONE:ONE + 1]).then_inc(r_free[3], 1)

            def step(k, q, main, ahead2, back1, back2):
                if main:
                    exps(k, q, 0)
                if back2:
                    take_o(k - 2)
                if ahead2:
                    high_part(k + 2, q)
                if main:
                    exps(k, q, 1)
                if back1:
                    take_probs_t(k - 1, 1)
                    take_probs_t(k - 1, 2)

            high_part(0, 0)
            high_part(1, 1)
            step(0, 0, True, True, False, False)
            step(1, 1, True, True, True, False)
            with act.Fori(0, (B - 4) // 2) as it:
                for q in range(2):
                    step(it * 2 + (2 + q), q, True, True, True, True)
            step(B - 2, 0, True, False, True, True)
            step(B - 1, 1, True, False, True, True)
            act.wait_ge(ff_in, 16 * FF_LOADS)
            nc.scalar.activation(w1[:, 0:3, :], raw1[:], ACT.Copy).then_inc(ff_hi, 1)
            step(B, 0, False, False, True, True)
            nc.scalar.activation(w2[:, 0], raw2[:], ACT.Copy).then_inc(ff_hi, 1)
            step(B + 1, 1, False, False, False, True)

        @block.tensor
        def _(pe):
            def wait_free(i, n):
                if not (isinstance(n, int) and n <= 0):
                    pe.wait_ge(r_free[i], n)

            def transpose_x(k, q, used):
                pe.wait_ge(xn_lo, k + 1)
                wait_free(0, used)
                for g in range(GR):
                    ins = nc.tensor.transpose(r_ps[0][:, L * g:L * g + L].bitcast(F32R),
                                              xn[q][:, g].rearrange("l s f -> l (s f)"), identr[:])
                ins.then_inc(x_in_bank, 1)

            def project_qk(k, q, used_qk):
                for i, ready in ((0, q_in_bank), (1, k_in_bank)):
                    wait_free(1 + i, used_qk)
                    for g in range(GR):
                        out = r_ps[1 + i][:, L * g:L * g + L]
                        nc.tensor.matmul(out, wqk[:, g, i, :], xs[q][:, g, :], start=True, stop=False)
                        ins = nc.tensor.matmul(out, wqk_lo[:, g, i, :], xs[q][0:GF, g, :], start=False, stop=True)
                    ins.then_inc(ready, 1)

            def project_v(k, q, used):
                wait_free(0, used)
                for g in range(GR):
                    out = r_ps[0][:, GF * g:GF * g + GF]
                    nc.tensor.matmul(out, xs[q][:, g, :], wv[:, g, :], start=True, stop=False)
                    ins = nc.tensor.matmul(out, xs[q][0:GF, g, :], wv_lo[:, g, :], start=False, stop=True)
                ins.then_inc(v_in_bank, 1)

            def scores(k, q, half):
                if not (isinstance(k, int) and k == 0):
                    pe.wait_ge(exp_ready, k * 2 + (half - 1))
                for g in range(GR):
                    for p in (2 * half, 2 * half + 1):
                        rows = slice(32 * p, 32 * p + HD)
                        ins = nc.tensor.matmul(s_ps[:, p, L * g:L * g + L], qt[q][rows, g, :], kt[q][rows, g, :],
                                               start=True, stop=True)
                ins.then_inc(s_ready, 1)

            def transpose_probs(k, q, used):
                for i in range(3):
                    if i < 2:
                        pe.wait_ge(probs_ready, k * 2 + (i + 1))
                    wait_free(i, used[i])
                    for j in range(4):
                        ins = nc.tensor.transpose(r_ps[i][:, L * j:L * j + L], probs[:, q, 4 * i + j, :], ident[:])
                    ins.then_inc(pt_in_bank, 1)

            def attend(k, q, used_o):
                wait_free(3, used_o)
                for g in range(GR):
                    for p in range(ROWS):
                        ins = nc.tensor.matmul(r_ps[3][32 * p:32 * p + 32, L * g:L * g + L], v[q][:, g, p, :],
                                               probs_t[:, GR * p + g, :], start=True, stop=True)
                ins.then_inc(o_in_bank, 1)

            def project_out(k, used):
                wait_free(3, used)
                for g in range(GR):
                    ins = nc.tensor.matmul(r_ps[3][:, 0:D], ot[:, g, :], wo[:, g, :], start=(g == 0), stop=(g == GR - 1))
                ins.then_inc(y_in_bank, 1)

            def step(k, q, main, ahead1, back1, back2, r0, r12, r3):
                if main:
                    last_qk = r12 - 1 if back2 else r12
                    pe.wait_ge(r_free[1], last_qk)
                    pe.wait_ge(r_free[2], last_qk)
                    scores(k, q, 0)
                if back2:
                    pe.wait_ge(r_free[0], r0)
                    pe.wait_ge(r_free[1], r12)
                    pe.wait_ge(r_free[2], r12)
                    attend(k - 2, q, r3)
                if ahead1:
                    transpose_x(k + 1, 1 - q, r0)
                    r0 = r0 + 1
                if main:
                    scores(k, q, 1)
                    project_v(k, q, r0)
                    r0 = r0 + 1
                if ahead1:
                    project_qk(k + 1, 1 - q, r12)
                    r12 = r12 + 1
                if back2:
                    project_out(k - 2, r3 + 1)
                if back1:
                    transpose_probs(k - 1, 1 - q, (r0, r12, r12))

            transpose_x(0, 0, 0)
            pe.wait_ge(r_free[0], 1)
            project_qk(0, 0, 0)
            step(0, 0, True, True, False, False, 1, 1, 0)
            for k in range(1, 4):
                step(k, k % 2, True, True, True, k > 1, 3 * k, 2 * k, 2 * k - 4)
            with pe.Fori(0, (B - 6) // 2) as it:
                for q in range(2):
                    step(it * 2 + (4 + q), q, True, True, True, True, it * 6 + (12 + 3 * q), it * 4 + (8 + 2 * q),
                         it * 4 + (4 + 2 * q))
            step(B - 2, 0, True, True, True, True, 3 * B - 6, 2 * B - 4, 2 * B - 8)
            step(B - 1, 1, True, False, True, True, 3 * B - 3, 2 * B - 2, 2 * B - 6)
            step(B, 0, False, False, True, True, 3 * B - 1, 2 * B - 1, 2 * B - 4)
            step(B + 1, 1, False, False, False, True, 3 * B, 2 * B, 2 * B - 2)


def program(nc, io):
    with ExitStack() as ctx:
        def sb(name, shape, dt=F32):
            return ctx.enter_context(nc.sbuf_tensor(name, shape, dt))

        keep = {
            "h": sb("h", [L, B, D]),
            "ident": sb("ident", [L, L]),
            "identr": sb("identr", [L, L], F32R),
            "nhalf": sb("nhalf", [L, 1]),
            "raw1": sb("raw1", [128, 3, HID]),
            "raw2": sb("raw2", [128, HJ, D]),
            "b1": sb("b1", [128, HJ]),
            "b2f": sb("b2f", [1, D]),
        }
        mixing_phase(nc, io, keep)
        keep["w1"] = sb("w1", [128, 5, HID], F32R)
        keep["w2"] = sb("w2", [128, 2, HJ, D], F32R)
        keep["att"] = {
            "wqk_raw": sb("wqk_raw_a", [2 * GF, GR, 2, 128]),
            "wqk": sb("wqk_a", [2 * GF, GR, 2, 128], F32R),
            "wqk_lo": sb("wqk_lo_a", [GF, GR, 2, 128], F32R),
            "wv_raw": sb("wv_raw_a", [2 * GF, GR, GF]),
            "wv": sb("wv_a", [2 * GF, GR, GF], F32R),
            "wv_lo": sb("wv_lo_a", [GF, GR, GF], F32R),
            "bqk": sb("bqk_a", [128, GR, 2]),
            "bv": sb("bv_a", [L, D]),
            "wo": sb("wo_a", [128, GR, D]),
        }
        keep["cls_res"] = sb("cls_res", [3 * B, 2, D])
        with ExitStack() as classes:
            def cls_sb(name, shape):
                return classes.enter_context(nc.sbuf_tensor(f"cls_{name}", shape, F32))

            keep["cls"] = {
                "tok": cls_sb("tok", [3 * B, 2, D]),
                "a1": cls_sb("a1", [DC, NEXP, 2, HID]),
                "a1b": cls_sb("a1b", [128, NEXP, HJ]),
                "a2": cls_sb("a2", [128, NEXP, HJ, D]),
                "b_high": cls_sb("b_high", [3 * B, 2, D]),
                "b_low": cls_sb("b_low", [3 * B, D]),
                "gw": cls_sb("gw", [DC, 2, 2 * NCLS]),
            }
            feed_forward_phase(nc, io, keep, 0)
        attention_phase(nc, io, keep)
        feed_forward_phase(nc, io, keep, 1)


def kernel(**inputs):
    import numpy as np
    import concourse.bacc as bacc
    from concourse.bass_utils import run_bass_kernel_spmd

    def get(name):
        return np.asarray(inputs[name])

    data = {
        "x": get("x")[..., 0].transpose(2, 0, 1),
        "dw_w": get("L0_tok_dw_w")[:, 0, :, 0],
        "pw_w": get("L0_tok_pw_w").T,
        "pw_b": get("L0_tok_pw_b")[None],
        "ln_g": get("L0_tok_ln_g")[None],
        "ln_b": get("L0_tok_ln_b")[None],
        "ln_w": get("L0_attn_ln_w")[None],
        "w_qk": get("L0_attn_W_qk").T,
        "w_o": get("L0_attn_W_o").reshape(D, H, D).transpose(2, 1, 0).reshape(D, H * D),
        "wte": get("L0_attn_wte"),
        "ffn0_w1": get("L0_ffn_moe0_W1"),
        "ffn0_b1": get("L0_ffn_moe0_b1").reshape(HJ, 128).T,
        "ffn0_w2": get("L0_ffn_moe0_W2"),
        "ffn0_b2": get("L0_ffn_moe0_b2")[None],
        "a1": get("L0_ffn_A1_W"),
        "a1b": get("L0_ffn_A1_b").reshape(NEXP, HJ, 128).transpose(2, 0, 1),
        "a2": get("L0_ffn_A2_W"),
        "a2b": get("L0_ffn_A2_b"),
        "gw": get("L0_ffn_G_W").transpose(1, 0, 2).reshape(D, 2 * NCLS),
        "w_qkv": get("L1_attn_W_qkv"),
        "b_qk": get("L1_attn_b_qkv")[:, 0:2 * HD].reshape(GR, ROWS, 2, HD).transpose(1, 3, 0, 2),
        "b_v": get("L1_attn_b_qkv")[:, 2 * HD:].reshape(1, D),
        "w_out": get("L1_attn_W_out"),
        "b_out": get("L1_attn_b_out")[None],
        "ffn1_w1": get("L1_ffn_in_weight").T,
        "ffn1_b1": get("L1_ffn_in_bias").reshape(HJ, 128).T,
        "ffn1_w2": get("L1_ffn_out_weight"),
        "ident": np.eye(L, dtype=np.float32),
        "mask": np.triu(np.full((L, L), -1e30, np.float32), 1),
        "nreg": (1.0 / np.arange(1, L + 1, dtype=np.float32))[:, None].astype(np.float32),
    }
    nc = bacc.Bacc("TRN2", target_bir_lowering=False, num_devices=1)
    io, arrays = {}, {}
    for name, a in data.items():
        a = np.ascontiguousarray(a)
        arrays[f"in_{name}"] = a
        io[name] = nc.dram_tensor(f"in_{name}", a.shape, mybir.dt.from_np(a.dtype), kind="ExternalInput").ap()
    io["out"] = nc.dram_tensor("out_0", (B, L, D), F32, kind="ExternalOutput").ap()
    program(nc, io)
    r = run_bass_kernel_spmd(nc, [arrays], core_ids=[0])
    return r.results[0]["out_0"]
```

```python
from contextlib import ExitStack

import concourse.bass as bass
from concourse import mybir

F32 = mybir.dt.float32
F32R = mybir.dt.float32r
ALU = mybir.AluOpType
ACT = mybir.ActivationFunctionType
AX = mybir.AxisListType

B, L, D = 32, 128, 192
DC = D // 2
TAPS, HALO = 7, 3
LP = L + 2 * HALO
H = 12
HG = 4
BANK = 512
GW = H * D
VOCAB = 50257
WR = 8
WPIECE = VOCAB // (L * WR)
WTAIL = VOCAB - WPIECE * L * WR
EPS_TOK, EPS_LN = 1e-6, 1e-5


HID = 768
HJ = HID // 128
STACKS = ([(0, 128, 0)], [(128, 192, 0), (0, 64, 64)], [(64, 192, 0)])


def load_feed_forward(sp, io, keep, name, loaded):
    n = 0
    for i, parts in enumerate(STACKS):
        for lo, hi, at in parts:
            sp.dma_start(keep["raw1"][at:at + hi - lo, i, :], io[f"{name}_w1"][lo:hi]).then_inc(loaded, 16)
            n += 1
    sp.dma_start(keep["raw2"][:], io[f"{name}_w2"].rearrange("(j p) d -> p j d", p=128)).then_inc(loaded, 16)
    sp.dma_start(keep["b1"][:], io[f"{name}_b1"]).then_inc(loaded, 16)
    return n + 2


FF_LOADS = 6
SCALE = float(D) ** -0.5


def f32(ap):
    return ap.bitcast(F32)


def mixing_phase(nc, io, keep):
    with ExitStack() as ctx:
        def sb(name, shape, dt=F32):
            return ctx.enter_context(nc.sbuf_tensor(name, shape, dt))

        def psum(name, shape, dt=F32):
            return ctx.enter_context(nc.psum_tensor(name, shape, dt))

        def sem(name):
            return ctx.enter_context(nc.semaphore(name))

        h, ident, nhalf, identr = keep["h"], keep["ident"], keep["nhalf"], keep["identr"]

        wte_acc = sb("wte_acc", [L, WR * D])
        w5 = sb("w5", [L, 5, GW], F32R)
        x_pad = sb("x_pad", [DC, 2, B, LP])
        taps = sb("taps", [DC, 2, TAPS])
        pw = sb("pw", [DC + 1, 2, D])
        ln_g = sb("ln_g", [L, D])
        ln_b = sb("ln_b", [L, D])
        ln_w = sb("ln_w", [L, D])
        wqk = sb("wqk", [DC, 2, H])
        nreg = sb("nreg", [L, 1])
        mask = sb("mask", [L, L])
        conv = [sb(f"conv{q}", [DC + 1, 2, L]) for q in range(2)]
        stats = sb("stats", [L, 2, 6])
        mv1 = sb("mv1", [L, 2, 2])
        mv2 = sb("mv2", [L, 2, 2])
        rstd1 = sb("rstd1", [L, 2])
        rstd2 = sb("rstd2", [L, 2])
        ytmp = sb("ytmp", [L, D])
        ypre = sb("ypre", [L, D])
        hc = sb("hc", [L, 2, D])
        xn = [sb(f"xn{q}", [L, 2 * D], F32R) for q in range(2)]
        xs = [sb(f"xs{q}", [L, 3, L], F32R) for q in range(2)]
        xt = [sb(f"xt{q}", [DC, 2, L]) for q in range(2)]
        ys = sb("ys", [DC, 2, H, L])
        nmax = sb("nmax", [L, 2, H])
        rsum = sb("rsum", [L, 2, H])
        rinv = sb("rinv", [L, 2, H])
        probs = sb("probs", [L, 2, H, L])
        probs_t = sb("probs_t", [L, H, L])
        g = [sb(f"g{q}", [L, GW]) for q in range(2)]
        wte = sb("wte", [L, 2, WR * D])
        wte_tail = sb("wte_tail", [WTAIL, D])
        share = sb("share", [L, 1])
        nneg = sb("nneg", [L, 1])
        wo_sum = sb("wo_sum", [L, 4, D])
        wte_sum, fix = ypre, ytmp
        avg = hc[:].rearrange("l a d -> l (a d)").rearrange("l (i m) -> l i m", i=3)

        ring = [psum(f"ring{i}", [L, BANK]) for i in range(3)]
        y_ps = psum("y_ps", [L, BANK])
        o_ps = psum("o_ps", [L, BANK])
        s_ps = psum("s_ps", [L, 3, BANK])

        conv_in = sem("conv_in")
        pw_in = sem("pw_in")
        first_in = sem("first_in")
        rest_in = sem("rest_in")
        ff_in = sem("ff_in")
        w_in = sem("w_in")
        wte_in = [sem(f"wte_in{q}") for q in range(2)]
        halo_set = sem("halo_set")
        identr_ready = sem("identr_ready")
        wqk_sq = sem("wqk_sq")
        w_hi = sem("w_hi")
        w_lo = sem("w_lo")
        conv_ready = sem("conv_ready")
        conv_step = sem("conv_step")
        conv1_step = sem("conv1_step")
        y_ready = sem("y_ready")
        y_bank_free = sem("y_bank_free")
        stats_step = sem("stats_step")
        ln1_stats = sem("ln1_stats")
        ln1_rstd = sem("ln1_rstd")
        ypre_ready = sem("ypre_ready")
        relu_ready = sem("relu_ready")
        ln2_stats = sem("ln2_stats")
        ln2_rstd = sem("ln2_rstd")
        hc_ready = sem("hc_ready")
        xn_hi = sem("xn_hi")
        xn_lo = sem("xn_lo")
        xs_in_bank = sem("xs_in_bank")
        xt_in_bank = sem("xt_in_bank")
        xs_ready = sem("xs_ready")
        xt_ready = sem("xt_ready")
        ys0_ready = sem("ys0_ready")
        ys1_ready = sem("ys1_ready")
        s_ready = sem("s_ready")
        s_masked = sem("s_masked")
        nmax_ready = sem("nmax_ready")
        exp_ready = sem("exp_ready")
        rinv_step = sem("rinv_step")
        rinv_ready = sem("rinv_ready")
        probs_ready = sem("probs_ready")
        pt_in_bank = sem("pt_in_bank")
        g_in_bank = sem("g_in_bank")
        pv_ready = sem("pv_ready")
        h_added = sem("h_added")
        wte_added = sem("wte_added")
        bank_free = [sem(f"bank_free{i}") for i in range(3)]
        tail_in = sem("tail_in")
        nneg_ready = sem("nneg_ready")
        share_set = sem("share_set")
        wte_summed = sem("wte_summed")
        wo_summed = sem("wo_summed")
        avg_in_bank = sem("avg_in_bank")
        avg_taken = sem("avg_taken")
        fix_in_bank = sem("fix_in_bank")
        fix_ready = sem("fix_ready")
        h_fixed = sem("h_fixed")

        block = ctx.enter_context(nc.Block())

        x_v = io["x"].rearrange("(c p) b l -> p c b l", c=2)
        wo_v = io["w_o"]
        wte_v = io["wte"][0:WPIECE * L * WR, :].rearrange("(n p r) d -> n p (r d)", p=L, r=WR)
        WO_ROWS = ([(0, 128, 0)], [(128, 192, 0), (0, 64, 64)], [(64, 192, 0)])
        raw = [g[0][:, :], g[1][:, :], probs[:].rearrange("p a h l -> p (a h l)")[:, 0:GW]]
        POOL_IMAGES = 16
        G_BANK = (1, 2, 0, 1, 2)
        G_COLS = [(j * BANK, min((j + 1) * BANK, GW)) for j in range(5)]

        @block.sync
        def _(sp):
            for c in range(2):
                sp.dma_start(x_pad[:, c, 0:2, HALO:HALO + L], x_v[:, c, 0:2]).then_inc(conv_in, 16)
            sp.dma_start(taps[:], io["dw_w"].rearrange("(c p) k -> p c k", c=2)).then_inc(conv_in, 16)
            sp.dma_start(pw[0:DC], io["pw_w"].rearrange("(c p) e -> p c e", c=2)).then_inc(pw_in, 16)
            sp.dma_start(pw[DC:DC + 1, 0, :], io["pw_b"]).then_inc(pw_in, 16)
            sp.dma_start(ident[:], io["ident"]).then_inc(first_in, 16)
            sp.dma_start(ln_g[:], io["ln_g"].to_broadcast([L, D])).then_inc(first_in, 16)
            sp.dma_start(ln_b[:], io["ln_b"].to_broadcast([L, D])).then_inc(first_in, 16)
            sp.dma_start(ln_w[:], io["ln_w"].to_broadcast([L, D])).then_inc(first_in, 16)
            sp.dma_start(wqk[:], io["w_qk"].rearrange("(c p) h -> p c h", c=2)).then_inc(first_in, 16)
            sp.dma_start(nreg[:], io["nreg"]).then_inc(first_in, 16)
            sp.dma_start(mask[:], io["mask"]).then_inc(first_in, 16)
            for i, parts in enumerate(WO_ROWS):
                for lo, hi, at in parts:
                    sp.dma_start(raw[i][at:at + hi - lo], wo_v[lo:hi]).then_inc(w_in, 16)
            for c in range(2):
                sp.dma_start(x_pad[:, c, 2:B, HALO:HALO + L], x_v[:, c, 2:B]).then_inc(rest_in, 16)
            sp.dma_start(wte_acc[:], wte_v[0]).then_inc(wte_in[0], 16)
            for n in (1, 2):
                sp.dma_start(wte[:, n % 2], wte_v[n]).then_inc(wte_in[n % 2], 16)
            with sp.Fori(0, (WPIECE - 3) // 2) as it:
                for n0 in (3, 4):
                    sp.wait_ge(wte_added, it * 2 + (n0 - 2))
                    sp.dma_start(wte[:, n0 % 2], wte_v[it * 2 + n0]).then_inc(wte_in[n0 % 2], 16)
            sp.dma_start(wte_tail[:], io["wte"][VOCAB - WTAIL:VOCAB, :]).then_inc(tail_in, 16)
            sp.dma_start(keep["b2"][:], io["ffn0_b2"].to_broadcast([L, D])).then_inc(ff_in, 16)
            load_feed_forward(sp, io, keep, "ffn0", ff_in)
            sp.wait_ge(tail_in, 16)
            sp.wait_ge(ff_in, 16 * (FF_LOADS + 1))

        @block.gpsimd
        def _(pool):
            def wte_piece(n):
                if n == 1:
                    pool.wait_ge(wte_in[0], 16)
                if n >= 2:
                    pool.wait_ge(wte_added, n - 1)
                pool.wait_ge(wte_in[n % 2], 16 * (n // 2 + 1))
                nc.gpsimd.tensor_tensor(wte_acc[:], wte_acc[:], wte[:, n % 2],
                                        ALU.add).then_inc(wte_added, 1)

            def rstd_1(k, q):
                pool.wait_ge(ln1_stats, k + 1)
                nc.gpsimd.tensor_tensor(rstd1[:, q:q + 1], mv1[:, q, 1:2], nhalf[:], ALU.pow).then_inc(ln1_rstd, 1)

            def rstd_2(k, q):
                pool.wait_ge(ln2_stats, k + 1)
                nc.gpsimd.tensor_tensor(rstd2[:, q:q + 1], mv2[:, q, 1:2], nhalf[:], ALU.pow).then_inc(ln2_rstd, 1)

            def scale_1(k, q):
                pool.wait_ge(xt_ready, k + 1)
                nc.gpsimd.tensor_tensor(ys[:, 1], xt[q][:, 1, None, :].to_broadcast([DC, H, L]),
                                        wqk[:, 1, :, None].to_broadcast([DC, H, L]), ALU.mult).then_inc(ys1_ready, 1)

            def normalise(k, q):
                pool.wait_ge(rinv_ready, k + 1)
                nc.gpsimd.tensor_tensor(probs[:, q], probs[:, q], rinv[:, q, :, None].to_broadcast([L, H, L]),
                                        ALU.mult).then_inc(probs_ready, 1)

            def step(k, q, pieces, ahead2, ahead1):
                for n in pieces:
                    wte_piece(n)
                if ahead2:
                    rstd_1(k + 2, q)
                if ahead1:
                    scale_1(k + 1, 1 - q)
                if ahead2:
                    rstd_2(k + 2, q)
                normalise(k, q)

            pool.wait_ge(conv_in, 16 * 3)
            pool.wait_ge(halo_set, 5)
            dst, term = conv[1][0:DC, 0, :], probs_t[0:DC, 0, :]
            for t in range(TAPS):
                w = taps[:, 0, t:t + 1].to_broadcast([DC, L])
                nc.gpsimd.tensor_tensor(term if t else dst, x_pad[:, 0, 1, t:t + L], w, ALU.mult).then_inc(conv1_step, 1)
                pool.wait_ge(conv1_step, max(2 * t, 1))
                if t:
                    nc.gpsimd.tensor_tensor(dst, dst, term, ALU.add).then_inc(conv1_step, 1)
                    pool.wait_ge(conv1_step, 2 * t + 1)
            rstd_1(0, 0)
            rstd_2(0, 0)
            pool.wait_ge(wqk_sq, 2)
            scale_1(0, 0)
            rstd_1(1, 1)
            rstd_2(1, 1)
            pool.wait_ge(w_in, 16 * 4)
            pool.wait_ge(w_hi, 2)
            nc.gpsimd.tensor_tensor(w5[0:64, 4, :], raw[1][0:64], f32(w5[0:64, 1, :]), ALU.subtract).then_inc(w_lo, 1)
            pieces = list(range(1, WPIECE))
            step(0, 0, pieces[0:2], True, True)
            step(1, 1, pieces[2:3], True, True)
            first = pieces[3]
            with pool.Fori(0, 7) as it:
                for u in range(4):
                    k = it * 4 + (2 + u)
                    for j in ((0, 1), (2,), (3, 4), (5,))[u]:
                        n0 = first + j
                        pool.wait_ge(wte_added, it * 6 + (n0 - 1))
                        pool.wait_ge(wte_in[n0 % 2], it * 48 + 16 * ((n0 + 1) // 2 + (n0 % 2 == 0)))
                        nc.gpsimd.tensor_tensor(wte_acc[:], wte_acc[:], wte[:, n0 % 2],
                                                ALU.add).then_inc(wte_added, 1)
                    step(k, u % 2, (), True, True)
            done = first + 42
            rest = list(range(done, WPIECE))
            step(30, 0, rest[0:2], False, True)
            step(31, 1, rest[2:], False, False)
            pool.wait_ge(fix_ready, 1)
            pool.wait_ge(h_added, POOL_IMAGES)
            nc.gpsimd.tensor_tensor(h[:, 0:POOL_IMAGES, :], h[:, 0:POOL_IMAGES, :],
                                    fix[:, None, :].to_broadcast([L, POOL_IMAGES, D]), ALU.add).then_inc(h_fixed, 1)

        @block.vector
        def _(dve):
            def tap(k, q, c, t):
                src = x_pad[:, c, k, t:t + L]
                dst = conv[q][0:DC, c, :]
                w = taps[:, c, t:t + 1]
                if t == 0:
                    ins = nc.vector.tensor_scalar(dst, src, w, None, ALU.mult)
                else:
                    if isinstance(k, int) and k == 1:
                        dve.wait_ge(conv_step, 2 * (TAPS - 1) + t)
                    else:
                        before = 0 if isinstance(k, int) and k == 0 else TAPS - 1
                        dve.wait_ge(conv_step, k * (2 * (TAPS - 1)) + (2 * t + c - 1 - before))
                    ins = nc.vector.scalar_tensor_tensor(dst, src, w, dst, ALU.mult, ALU.add)
                ins.then_inc(conv_step if t < TAPS - 1 else conv_ready, 1)

            def convolve(k, q):
                for t in range(TAPS):
                    for c in range(2):
                        tap(k, q, c, t)

            def ln1_a(k, q):
                dve.wait_ge(y_ready, k + 1)
                nc.vector.bn_stats(stats[:, 0], y_ps[:, 0:D]).then_inc(stats_step, 1)
                dve.drain()
                nc.vector.bn_aggr(mv1[:, q], stats[:, 0]).then_inc(stats_step, 1)
                dve.wait_ge(stats_step, k * 4 + 2)
                nc.vector.tensor_scalar(mv1[:, q, 1:2], mv1[:, q, 1:2], EPS_TOK, None, ALU.add).then_inc(ln1_stats, 1)

            def ln1_b(k, q):
                dve.wait_ge(ln1_rstd, k + 1)
                nc.vector.scalar_tensor_tensor(ytmp[:], y_ps[:, 0:D], mv1[:, q, 0:1], ln_g[:], ALU.subtract,
                                               ALU.mult).then_inc(y_bank_free, 1)
                dve.wait_ge(y_bank_free, k + 1)
                nc.vector.scalar_tensor_tensor(ypre[:], ytmp[:], rstd1[:, q:q + 1], ln_b[:], ALU.mult,
                                               ALU.add).then_inc(ypre_ready, 1)

            def ln2_a(k, q):
                dve.wait_ge(relu_ready, k + 1)
                nc.vector.bn_stats(stats[:, 1], h[:, k, :]).then_inc(stats_step, 1)
                dve.drain()
                nc.vector.bn_aggr(mv2[:, q], stats[:, 1]).then_inc(stats_step, 1)
                dve.wait_ge(stats_step, k * 4 + 4)
                nc.vector.tensor_scalar(mv2[:, q, 1:2], mv2[:, q, 1:2], 1.0 + EPS_LN, EPS_LN * EPS_LN, ALU.mult,
                                        ALU.add).then_inc(ln2_stats, 1)

            def ln2_b(k, q):
                dve.wait_ge(ln2_rstd, k + 1)
                nc.vector.scalar_tensor_tensor(hc[:, q], h[:, k, :], mv2[:, q, 0:1], ln_w[:], ALU.subtract,
                                               ALU.mult).then_inc(hc_ready, 1)

            def low_part(k, q):
                dve.wait_ge(xn_hi, k + 1)
                nc.vector.scalar_tensor_tensor(xn[q][:, D:2 * D], hc[:, q], rstd2[:, q:q + 1], f32(xn[q][:, 0:D]),
                                               ALU.mult, ALU.subtract).then_inc(xn_lo, 1)

            def take_xs(k, q):
                dve.wait_ge(xs_in_bank, k + 1)
                nc.vector.tensor_copy(xs[q][:].rearrange("p a b -> p (a b)"), ring[0][:, 0:3 * L]).then_inc(bank_free[0], 1)

            def scale_0(k, q):
                dve.wait_ge(xt_ready, k + 1)
                nc.vector.tensor_tensor(ys[:, 0], xt[q][:, 0, None, :].to_broadcast([DC, H, L]),
                                        wqk[:, 0, :, None].to_broadcast([DC, H, L]), ALU.mult).then_inc(ys0_ready, 1)

            def row_max(k, q):
                dve.wait_ge(s_ready, k + 1)
                nc.vector.tensor_tensor(s_ps[:].rearrange("p b (h l) -> p (b h) l", l=L),
                                        s_ps[:].rearrange("p b (h l) -> p (b h) l", l=L),
                                        mask[:, None, :].to_broadcast([L, H, L]), ALU.add).then_inc(s_masked, 1)
                dve.wait_ge(s_masked, k + 1)
                nc.vector.tensor_reduce(nmax[:, q, :], s_ps[:].rearrange("p b (h l) -> p (b h) l", l=L), AX.X, ALU.max,
                                        negate=True).then_inc(nmax_ready, 1)

            def inverse_sum(k, q):
                dve.wait_ge(exp_ready, k + 1)
                nc.vector.reciprocal(rinv[:, q, :], rsum[:, q, :]).then_inc(rinv_step, 1)
                dve.wait_ge(rinv_step, k + 1)
                nc.vector.tensor_scalar(rinv[:, q, :], rinv[:, q, :], nreg[:], None, ALU.mult).then_inc(rinv_ready, 1)

            def add_to_h(k):
                dve.wait_ge(pv_ready, k + 1)
                nc.vector.tensor_tensor(h[:, k, :], o_ps[:, 0:D], h[:, k, :], ALU.add).then_inc(h_added, 1)

            def step(k, q, ahead2, ahead1, back1, back2):
                if ahead2:
                    convolve(k + 2, q)
                if isinstance(k, int) and k == 0:
                    low_part(1, 1)
                if back2:
                    add_to_h(k - 2)
                row_max(k, q)
                if ahead1:
                    take_xs(k + 1, 1 - q)
                if ahead2:
                    ln1_a(k + 2, q)
                if ahead1:
                    scale_0(k + 1, 1 - q)
                if ahead2:
                    ln1_b(k + 2, q)
                    ln2_a(k + 2, q)
                    ln2_b(k + 2, q)
                inverse_sum(k, q)
                if ahead2:
                    low_part(k + 2, q)

            nc.vector.memset(nhalf[:], -0.5).then_inc(halo_set, 1)
            for q in range(2):
                nc.vector.memset(conv[q][DC:DC + 1, 0, :], 1.0).then_inc(halo_set, 1)
            nc.vector.memset(x_pad[:, :, :, 0:HALO], 0.0).then_inc(halo_set, 1)
            nc.vector.memset(x_pad[:, :, :, HALO + L:LP], 0.0).then_inc(halo_set, 1)
            dve.wait_ge(conv_in, 16 * 3)
            dve.wait_ge(halo_set, 5)
            convolve(0, 0)
            dve.wait_ge(first_in, 16 * 7)
            nc.vector.tensor_copy(identr[:], ident[:]).then_inc(identr_ready, 1)
            nc.vector.tensor_tensor(wqk[:], wqk[:], wqk[:], ALU.mult).then_inc(wqk_sq, 1)
            dve.wait_ge(wqk_sq, 1)
            nc.vector.tensor_scalar(wqk[:], wqk[:], float(D) ** -0.5, None, ALU.mult).then_inc(wqk_sq, 1)
            nc.vector.tensor_scalar(nneg[:], nreg[:], -1.0, None, ALU.mult).then_inc(nneg_ready, 1)
            ln1_a(0, 0)
            tap(1, 1, 1, 0)
            tap(1, 1, 1, 1)
            ln1_b(0, 0)
            tap(1, 1, 1, 2)
            ln2_a(0, 0)
            tap(1, 1, 1, 3)
            tap(1, 1, 1, 4)
            ln2_b(0, 0)
            tap(1, 1, 1, 5)
            low_part(0, 0)
            tap(1, 1, 1, 6)
            dve.wait_ge(wqk_sq, 2)
            take_xs(0, 0)
            scale_0(0, 0)
            ln1_a(1, 1)
            ln1_b(1, 1)
            ln2_a(1, 1)
            ln2_b(1, 1)
            dve.wait_ge(w_in, 16 * 4)
            dve.wait_ge(w_hi, 1)
            nc.vector.tensor_tensor(w5[:, 3, :], raw[0], f32(w5[:, 0, :]), ALU.subtract).then_inc(w_lo, 1)
            dve.wait_ge(rest_in, 32)
            step(0, 0, True, True, False, False)
            step(1, 1, True, True, True, False)
            with dve.Fori(0, 14) as it:
                for q in range(2):
                    step(it * 2 + (2 + q), q, True, True, True, True)
            def sum_heads(i):
                rows = 64 if i == 3 else L
                src = f32(w5[0:rows, (0, 2, 3, 4)[i], :]).rearrange("p (h d) -> p d h", h=H)
                nc.vector.tensor_reduce(wo_sum[0:rows, i, :], src, AX.X, ALU.add).then_inc(wo_summed, 1)

            def add_fix(images):
                lo, hi = images
                nc.vector.tensor_tensor(h[:, lo:hi, :], h[:, lo:hi, :], fix[:, None, :].to_broadcast([L, hi - lo, D]),
                                        ALU.add).then_inc(h_fixed, 1)

            step(30, 0, False, True, True, True)
            nc.vector.memset(share[:], 1.0 / VOCAB).then_inc(share_set, 1)
            nc.vector.memset(avg[0:64, 1, :], 0.0).then_inc(avg_taken, 1)
            sum_heads(0)
            sum_heads(1)
            add_to_h(29)
            row_max(31, 1)
            dve.wait_ge(wte_added, WPIECE - 1)
            nc.vector.tensor_reduce(wte_sum[:], wte_acc[:].rearrange("p (r d) -> p d r", r=WR), AX.X,
                                    ALU.add).then_inc(wte_summed, 1)
            sum_heads(2)
            sum_heads(3)
            dve.wait_ge(avg_in_bank, 1)
            nc.vector.tensor_copy(avg[:, 0, :], y_ps[:, 0:1].to_broadcast([L, L])).then_inc(avg_taken, 1)
            nc.vector.tensor_copy(avg[64:128, 1, :], y_ps[64:128, 1:2].to_broadcast([64, L])).then_inc(avg_taken, 1)
            nc.vector.tensor_copy(avg[0:64, 2, :], y_ps[0:64, 2:3].to_broadcast([64, L])).then_inc(avg_taken, 1)
            inverse_sum(31, 1)
            dve.wait_ge(nneg_ready, 1)
            dve.wait_ge(fix_in_bank, 1)
            nc.vector.tensor_scalar(fix[:], s_ps[:, 0, 0:D], nneg[:], None, ALU.mult).then_inc(fix_ready, 1)
            dve.wait_ge(fix_ready, 1)
            add_fix((POOL_IMAGES, POOL_IMAGES + 7))
            add_to_h(30)
            dve.wait_ge(h_added, B - 1)
            add_fix((POOL_IMAGES + 7, B - 1))
            add_to_h(31)
            dve.wait_ge(h_added, B)
            add_fix((B - 1, B))

        @block.scalar
        def _(act):
            def relu(k):
                act.wait_ge(ypre_ready, k + 1)
                nc.scalar.activation(h[:, k, :], ypre[:], ACT.Relu).then_inc(relu_ready, 1)

            def high_part(k, q):
                act.wait_ge(hc_ready, k + 1)
                nc.scalar.activation(xn[q][:, 0:D], hc[:, q], ACT.Identity, scale=rstd2[:, q:q + 1]).then_inc(xn_hi, 1)

            def take_xt(k, q):
                act.wait_ge(xt_in_bank, k + 1)
                nc.scalar.activation(xt[q][:].rearrange("p c l -> p (c l)"), o_ps[0:DC, 0:2 * L],
                                     ACT.Copy).then_inc(xt_ready, 1)

            def take_probs_t(k):
                for j in range(3):
                    act.wait_ge(pt_in_bank, k * 3 + (j + 1))
                    nc.scalar.activation(probs_t[:, HG * j:HG * j + HG, :].rearrange("p h l -> p (h l)"), ring[j][:],
                                         ACT.Copy).then_inc(bank_free[j], 1)

            def exps(k, q, heads):
                assert heads
                for i in heads:
                    ins = nc.scalar.activation(probs[:, q, i, :], s_ps[:, i // HG, L * (i % HG):L * (i % HG) + L],
                                               ACT.Exp, bias=nmax[:, q, i:i + 1], accum_out=rsum[:, q, i:i + 1])
                if heads[-1] == H - 1:
                    ins.then_inc(exp_ready, 1)

            def take_g(k, q, j):
                lo, hi = G_COLS[j]
                act.wait_ge(g_in_bank, k * 5 + (j + 1))
                nc.scalar.activation(g[q][:, lo:hi], ring[G_BANK[j]][:, 0:hi - lo],
                                     ACT.Copy).then_inc(bank_free[G_BANK[j]], 1)

            def step(k, q, ahead2, ahead1, back1):
                if back1:
                    take_probs_t(k - 1)
                if ahead1:
                    take_xt(k + 1, 1 - q)
                act.wait_ge(nmax_ready, k + 1)
                exps(k, q, (0, 1))
                for j in range(5):
                    take_g(k, q, j)
                    exps(k, q, (2 + 2 * j, 3 + 2 * j))
                    if ahead2 and j == 1:
                        relu(k + 2)
                if ahead2:
                    high_part(k + 2, q)

            relu(0)
            high_part(0, 0)
            take_xt(0, 0)
            relu(1)
            act.wait_ge(w_in, 16 * 4)
            for i in range(3):
                nc.scalar.activation(w5[:, i, :], raw[i], ACT.Copy).then_inc(w_hi, 1)
            high_part(1, 1)
            act.wait_ge(w_lo, 2)
            act.wait_ge(w_hi, 3)
            step(0, 0, True, True, False)
            step(1, 1, True, True, True)
            with act.Fori(0, 14) as it:
                for q in range(2):
                    step(it * 2 + (2 + q), q, True, True, True)
            step(30, 0, False, True, True)
            step(31, 1, False, False, True)
            take_probs_t(31)

        @block.tensor
        def _(pe):
            def pointwise(k, q):
                if isinstance(k, int) and k == 1:
                    pe.wait_ge(conv1_step, 2 * TAPS - 1)
                if isinstance(k, int) and k == 0:
                    pe.wait_ge(conv_ready, 2)
                else:
                    pe.wait_ge(conv_ready, k * 2 + 1)
                if not (isinstance(k, int) and k == 0):
                    pe.wait_ge(y_bank_free, k)
                nc.tensor.matmul(y_ps[:, 0:D], conv[q][:, 0, :], pw[:, 0, :], start=True, stop=False)
                nc.tensor.matmul(y_ps[:, 0:D], conv[q][0:DC, 1, :], pw[0:DC, 1, :], start=False,
                                 stop=True).then_inc(y_ready, 1)

            def wait_bank(i, n):
                if not (isinstance(n, int) and n <= 0):
                    pe.wait_ge(bank_free[i], n)

            def transpose_xn(k, q, used, back2):
                pe.wait_ge(xn_lo, k + 1)
                wait_bank(0, used)
                for i in range(3):
                    ins = nc.tensor.transpose(ring[0][:, L * i:L * i + L].bitcast(F32R), xn[q][:, L * i:L * i + L],
                                              identr[:])
                ins.then_inc(xs_in_bank, 1)
                if back2:
                    pe.wait_ge(h_added, k - 2)
                for c in range(2):
                    nc.tensor.matmul(o_ps[0:DC, L * c:L * c + L], xn[q][:, DC * c:DC * c + DC], identr[:],
                                     start=(c == 0), stop=False, skip_group_check=True)
                    ins = nc.tensor.matmul(o_ps[0:DC, L * c:L * c + L], xn[q][:, D + DC * c:D + DC * c + DC],
                                           identr[:], start=False, stop=(c == 1), skip_group_check=True)
                ins.then_inc(xt_in_bank, 1)

            def scores(k, q):
                pe.wait_ge(ys0_ready, k + 1)
                pe.wait_ge(ys1_ready, k + 1)
                if not (isinstance(k, int) and k == 0):
                    pe.wait_ge(exp_ready, k)
                for j in range(3):
                    for c in range(2):
                        ins = nc.tensor.matmul(s_ps[:, j, :], xt[q][:, c, :],
                                               ys[:, c, HG * j:HG * j + HG, :].rearrange("p h l -> p (h l)"),
                                               start=(c == 0), stop=(c == 1))
                ins.then_inc(s_ready, 1)

            def transpose_probs(k, q, used):
                pe.wait_ge(probs_ready, k + 1)
                for j in range(3):
                    wait_bank(j, used[j])
                    for i in range(HG):
                        ins = nc.tensor.transpose(ring[j][:, L * i:L * i + L], probs[:, q, HG * j + i, :], ident[:])
                    ins.then_inc(pt_in_bank, 1)

            def value_products(k, q, used, start):
                pe.wait_ge(bank_free[0], start)
                stack = [xs[q][:, i, :] for i in (0, 1, 2, 0)]
                for j in range(5):
                    lo, hi = G_COLS[j]
                    b = G_BANK[j]
                    wait_bank(b, used[b] + (1 if j >= 3 else 0))
                    for i in range(4):
                        nc.tensor.matmul(ring[b][:, 0:hi - lo], stack[i], w5[:, i, lo:hi], start=(i == 0), stop=False)
                    nc.tensor.matmul(ring[b][:, 0:hi - lo], xs[q][0:64, 1, :], w5[0:64, 4, lo:hi], start=False,
                                     stop=True).then_inc(g_in_bank, 1)

            def attend(k, q):
                for j in range(H):
                    ins = nc.tensor.matmul(o_ps[:, 0:D], probs_t[:, j, :], g[q][:, D * j:D * j + D], start=(j == 0),
                                           stop=(j == H - 1))
                ins.then_inc(pv_ready, 1)

            def step(k, q, ahead2, ahead1, back1, b0, b1, b2, after):
                scores(k, q)
                n = 0
                if back1:
                    transpose_probs(k - 1, 1 - q, (b0, b1, b2))
                    n = 1
                if ahead2:
                    pointwise(k + 2, q)
                m = 0
                if ahead1:
                    transpose_xn(k + 1, 1 - q, b0 + n, after)
                    m = 1
                if isinstance(k, int) and k == 0:
                    pe.wait_ge(w_lo, 2)
                value_products(k, q, (b0 + n + m, b1 + n, b2 + n), b0)
                if back1:
                    if ahead1:
                        pe.wait_ge(xt_ready, k + 2)
                    else:
                        pe.wait_ge(h_added, k - 1)
                    attend(k - 1, 1 - q)

            pe.wait_ge(pw_in, 16 * 2)
            pointwise(0, 0)
            pe.wait_ge(identr_ready, 1)
            transpose_xn(0, 0, 0, False)
            pointwise(1, 1)
            step(0, 0, True, True, False, 1, 0, 0, False)
            step(1, 1, True, True, True, 3, 2, 2, False)
            with pe.Fori(0, 14) as it:
                for q in range(2):
                    k = it * 2 + (2 + q)
                    step(k, q, True, True, True, it * 6 + (6 + 3 * q), it * 6 + (5 + 3 * q), it * 6 + (5 + 3 * q), True)
            step(30, 0, False, True, True, 90, 89, 89, True)
            scores(31, 1)
            transpose_probs(30, 0, (93, 92, 92))
            value_products(31, 1, (94, 93, 93), 93)
            pe.wait_ge(share_set, 1)
            pe.wait_ge(tail_in, 16)
            pe.wait_ge(wte_summed, 1)
            pe.wait_ge(y_bank_free, B)
            for i, (lo, hi) in enumerate(((0, 128), (64, 192), (128, 192))):
                nc.tensor.matmul(y_ps[0:hi - lo, i:i + 1], wte_sum[:, lo:hi], share[:], start=True, stop=False,
                                 skip_group_check=True)
                ins = nc.tensor.matmul(y_ps[0:hi - lo, i:i + 1], wte_tail[:, lo:hi], share[0:WTAIL], start=False,
                                       stop=True, skip_group_check=True)
            ins.then_inc(avg_in_bank, 1)
            pe.wait_ge(h_added, 30)
            attend(30, 0)
            pe.wait_ge(avg_taken, 4)
            pe.wait_ge(wo_summed, 4)
            pe.wait_ge(exp_ready, B)
            fix_ps = s_ps[:, 0, 0:D]
            nc.tensor.matmul(fix_ps, avg[:, 0, :], wo_sum[:, 0, :], start=True, stop=False)
            nc.tensor.matmul(fix_ps, avg[:, 1, :], wo_sum[:, 1, :], start=False, stop=False)
            nc.tensor.matmul(fix_ps, avg[:, 0, :], wo_sum[:, 2, :], start=False, stop=False)
            nc.tensor.matmul(fix_ps, avg[0:64, 2, :], wo_sum[0:64, 3, :], start=False, stop=True).then_inc(fix_in_bank, 1)
            transpose_probs(31, 1, (95, 95, 95))
            pe.wait_ge(bank_free[0], 96)
            pe.wait_ge(bank_free[1], 96)
            pe.wait_ge(bank_free[2], 96)
            pe.wait_ge(h_added, 31)
            attend(31, 1)


PAIR = 2
NPAIR = B // PAIR
NCLS = 6
NEXP = 5
HD = D // H
ROWS = 4
GR = H // ROWS
GF = ROWS * HD
GROUP_STACK = (0, 0, 1)
ONE = HD


def store_class_tokens(sp, h, res, lo, hi, stored):
    for i in range(NCLS):
        q, t = i // 2, i % 2
        sp.dma_start(h[i:i + 1, lo:hi, :], res[B * q + lo:B * q + hi, t, :]).then_inc(stored, 16)


def feed_forward_phase(nc, io, keep, layer):
    with ExitStack() as ctx:
        def sb(name, shape, dt=F32):
            return ctx.enter_context(nc.sbuf_tensor(f"{name}_f{layer}", shape, dt))

        def psum(name, shape, dt=F32):
            return ctx.enter_context(nc.psum_tensor(f"{name}_f{layer}", shape, dt))

        def sem(name):
            return ctx.enter_context(nc.semaphore(f"{name}_f{layer}"))

        h, ident, nhalf, identr = keep["h"], keep["ident"], keep["nhalf"], keep["identr"]
        first = layer == 0
        T2 = PAIR * L

        raw1, raw2, b1, w1, w2 = keep["raw1"], keep["raw2"], keep["b1"], keep["w1"], keep["w2"]
        xf = sb("xf", [L, PAIR, D])
        xn = [sb(f"xn{q}", [L, PAIR, 2 * D], F32R) for q in range(2)]
        xs = [sb(f"xs{q}", [128, 3, T2], F32R) for q in range(2)]
        gf = sb("gf", [128, HJ, T2])
        gh = [sb(f"gh{q}", [128, HJ, T2], F32R) for q in range(2)]
        gl = [sb(f"gl{q}", [128, HJ, T2], F32R) for q in range(2)]
        stats = sb("stats", [L, PAIR, 6])
        mv = sb("mv", [L, 2, PAIR, 2])
        rstd = sb("rstd", [L, 2, PAIR])
        if first:
            b2, att = keep["b2"], keep["att"]
            Q, R = 3, 3 * B
            c_stats = sb("c_stats", [R, 2, 6])
            c_mv = sb("c_mv", [R, 2, 2])
            c_rstd = sb("c_rstd", [R, 2])
            c_xf = sb("c_xf", [R, 2, D])
            xt = sb("xt", [DC, 2, 2, R])
            hid_q = sb("hid_q", [128, HJ, 2, R])
            hid_t = sb("hid_t", [128, HJ, 2, R])
            lg = sb("lg", [R, 2, 2])
            gm = sb("gm", [R, 2])
            ge = sb("ge", [R, 2, 2])
            gate = sb("gate", [R, 2, 2])
            part = sb("part", [R, 2, D])
            part2 = sb("part2", [R, 2, D])
            res = keep["cls_res"]

        x_ps = [psum(f"x_ps{i}", [128, BANK]) for i in range(PAIR)]
        hid_ps = [psum(f"hid_ps{i}", [128, BANK]) for i in range(3)]
        out_ps = psum("out_ps", [L, PAIR, BANK])
        if first:
            cls_ps = psum("cls_ps", [128, BANK])
            xt_ps, lg_ps = cls_ps[0:DC, 0:4 * R], cls_ps[0:R, 4 * R:4 * R + 4 * NCLS]
            high_ps = out_ps[0:R, 0, 0:2 * D]
            low_ps = cls_ps[0:R, 0:2 * D]

        stats_ready = sem("stats_ready")
        stats_step = sem("stats_step")
        rstd_ready = sem("rstd_ready")
        xf_ready = sem("xf_ready")
        xn_hi = sem("xn_hi")
        xn_lo = sem("xn_lo")
        x_in_bank = sem("x_in_bank")
        xs_ready = sem("xs_ready")
        hid_in_bank = sem("hid_in_bank")
        gelu_ready = sem("gelu_ready")
        g_hi = sem("g_hi")
        g_lo = sem("g_lo")
        out_ready = sem("out_ready")
        half_added = sem("half_added")
        h_added = sem("h_added")
        stored = sem("stored")
        ATT_LOADS = 8 * ROWS + 2
        cls = keep["cls"] if first else None
        if first:
            w_hi = sem("w_hi")
            w_lo = sem("w_lo")
            b2_added = sem("b2_added")
            tok_in = sem("tok_in")
            cls_in = sem("cls_in")
            pads_set = sem("pads_set")
            att_in = sem("att_in")
            c_step = sem("c_step")
            c_var_ready = sem("c_var_ready")
            c_rstd_ready = sem("c_rstd_ready")
            c_xf_ready = sem("c_xf_ready")
            xt_in_bank = sem("xt_in_bank")
            xt_ready = sem("xt_ready")
            lg_in_bank = sem("lg_in_bank")
            lg_shifted = sem("lg_shifted")
            exp_ready = sem("exp_ready")
            c_hid_in_bank = sem("c_hid_in_bank")
            c_gelu_ready = sem("c_gelu_ready")
            c_out_ready = sem("c_out_ready")
            res_ready = sem("res_ready")
            res_stored = sem("res_stored")

        block = ctx.enter_context(nc.Block())
        BREAK = NPAIR - 4

        @block.sync
        def _(sp):
            if first:
                for i in range(NCLS):
                    q, t = i // 2, i % 2
                    sp.dma_start(cls["tok"][B * q:B * q + B, t, :], h[i:i + 1, :, :]).then_inc(tok_in, 16)
                for e in range(NEXP):
                    sp.dma_start(cls["a1"][:, e], io["a1"][e].rearrange("(c p) f -> p c f", c=2)).then_inc(cls_in, 16)
                    sp.dma_start(cls["a2"][:, e], io["a2"][e].rearrange("(j p) d -> p j d", p=128)).then_inc(cls_in, 16)
                sp.dma_start(cls["a1b"][:], io["a1b"]).then_inc(cls_in, 16)
                sp.dma_start(cls["gw"][:], io["gw"].rearrange("(c p) n -> p c n", c=2)).then_inc(cls_in, 16)
                for t in range(2):
                    sp.dma_start(cls["b_high"][:, t, :], io["a2b"][3 + t:4 + t].to_broadcast([3 * B, D])).then_inc(cls_in, 16)
                for q in range(3):
                    sp.dma_start(cls["b_low"][B * q:B * q + B, :], io["a2b"][q:q + 1].to_broadcast([B, D])).then_inc(cls_in, 16)
                sp.wait_ge(pads_set, 4)
                w = io["w_qkv"].rearrange("(g p) d e -> p d g e", p=ROWS)
                for p in range(ROWS):
                    for at, groups in ((0, slice(0, 1)), (GF, slice(1, GR))):
                        rows = slice(at + HD * p, at + HD * p + HD)
                        for i in range(2):
                            sp.dma_start(att["wqk"][rows, groups, i, 32 * p:32 * p + HD],
                                         w[p][:, groups, HD * i:HD * i + HD]).then_inc(att_in, 16)
                        sp.dma_start(att["wv"][rows, groups, HD * p:HD * p + HD],
                                     w[p][:, groups, 2 * HD:3 * HD]).then_inc(att_in, 16)
                    sp.dma_start(att["bqk"][32 * p:32 * p + HD], io["b_qk"][p]).then_inc(att_in, 16)
                sp.dma_start(att["bv"][:], io["b_v"].to_broadcast([L, D])).then_inc(att_in, 16)
                w = io["w_out"].rearrange("(g p d) e -> p d g e", p=ROWS, g=GR)
                for p in range(ROWS):
                    sp.dma_start(att["wo"][32 * p:32 * p + HD], w[p]).then_inc(att_in, 16)
                sp.dma_start(att["wo"][ONE:ONE + 1, 0, :], io["b_out"]).then_inc(att_in, 16)
                sp.wait_ge(att_in, 16 * ATT_LOADS)
                sp.wait_ge(cls_in, 16 * (2 * NEXP + 7))
                sp.wait_ge(res_ready, 1)
                sp.wait_ge(h_added, BREAK)
                store_class_tokens(sp, h, res, 0, BREAK * PAIR, res_stored)
                sp.wait_ge(res_stored, 16 * NCLS)
            else:
                out_v = io["out"].rearrange("b l d -> l b d")
                with sp.Fori(0, NPAIR) as u:
                    sp.wait_ge(h_added, u + 1)
                    sp.dma_start(out_v[:, bass.ds(u * PAIR, PAIR), :], h[:, bass.ds(u * PAIR, PAIR), :]).then_inc(stored, 16)
                sp.wait_ge(stored, 16 * NPAIR)

        @block.gpsimd
        def _(pool):
            def rstd_of(u, q):
                pool.wait_ge(stats_ready, u + 1)
                nc.gpsimd.tensor_tensor(rstd[:, q, :], mv[:, q, :, 1], nhalf[:].to_broadcast([L, PAIR]),
                                        ALU.pow).then_inc(rstd_ready, 1)

            def add_b2(u):
                pool.wait_ge(xf_ready, u * PAIR + PAIR)
                pair = bass.ds(u * PAIR, PAIR) if not isinstance(u, int) else slice(u * PAIR, u * PAIR + PAIR)
                nc.gpsimd.tensor_tensor(h[:, pair, :], h[:, pair, :], b2[:, None, :].to_broadcast([L, PAIR, D]),
                                        ALU.add).then_inc(b2_added, 1)

            for u in range(3):
                rstd_of(u, u % 2)
            if first:
                nc.gpsimd.memset(att["wqk"][:].rearrange("p g i m -> p (g i m)"), 0.0).then_inc(pads_set, 1)
                nc.gpsimd.memset(att["wv"][:], 0.0).then_inc(pads_set, 1)
                nc.gpsimd.memset(att["bqk"][:], 0.0).then_inc(pads_set, 1)
                nc.gpsimd.memset(att["wo"][:], 0.0).then_inc(pads_set, 1)
                pool.wait_ge(tok_in, 16 * NCLS)
                for u in range(3):
                    add_b2(u)
            rstd_of(3, 1)
            rstd_of(4, 0)
            if first:
                add_b2(3)
                pool.wait_ge(c_var_ready, 1)
                nc.gpsimd.tensor_tensor(c_rstd[:], c_mv[:, :, 1], nhalf[0:R].to_broadcast([R, 2]),
                                        ALU.pow).then_inc(c_rstd_ready, 1)
            rstd_of(5, 1)
            if first:
                add_b2(4)
            with pool.Fori(0, (NPAIR - 6) // 2) as it:
                for q in range(2):
                    rstd_of(it * 2 + (6 + q), q)
                    if first:
                        add_b2(it * 2 + (5 + q))
            if first:
                add_b2(NPAIR - 1)

        @block.vector
        def _(dve):
            def normalise(u, q):
                for i in range(PAIR):
                    nc.vector.bn_stats(stats[:, i], h[:, u * PAIR + i, :])
                    dve.drain()
                    ins = nc.vector.bn_aggr(mv[:, q, i], stats[:, i])
                ins.then_inc(stats_step, 1)
                dve.wait_ge(stats_step, u + 1)
                nc.vector.tensor_scalar(mv[:, q, :, 1], mv[:, q, :, 1], EPS_LN, None, ALU.add).then_inc(stats_ready, 1)

            def centre(u, q):
                dve.wait_ge(rstd_ready, u + 1)
                for i in range(PAIR):
                    nc.vector.tensor_scalar(xf[:, i, :], h[:, u * PAIR + i, :], mv[:, q, i, 0:1], rstd[:, q, i:i + 1],
                                            ALU.subtract, ALU.mult).then_inc(xf_ready, 1)

            def low_part(u, q):
                dve.wait_ge(xn_hi, u + 1)
                nc.vector.tensor_tensor(xn[q][:, :, D:2 * D], xf[:], f32(xn[q][:, :, 0:D]),
                                        ALU.subtract).then_inc(xn_lo, 1)
                dve.wait_ge(xn_lo, u + 1)

            def take_xs(u, q):
                for i in range(PAIR):
                    dve.wait_ge(x_in_bank, u * PAIR + (i + 1))
                    nc.vector.tensor_copy(xs[q][:, :, L * i:L * i + L],
                                          x_ps[i][:, 0:3 * L].rearrange("p (s l) -> p s l", l=L)).then_inc(xs_ready, 1)

            def low_gelu(u, q, i):
                c = slice(2 * i, 2 * i + 2)
                dve.wait_ge(g_hi, u * 3 + (i + 1))
                nc.vector.tensor_tensor(gl[q][:, c], gf[:, c], f32(gh[q][:, c]), ALU.subtract).then_inc(g_lo, 1)

            def add_to_h(u):
                if first:
                    dve.wait_ge(b2_added, u + 1)
                dve.wait_ge(out_ready, u + 1)
                hp = h[:, bass.ds(u * PAIR, PAIR), :] if not isinstance(u, int) else h[:, u * PAIR:u * PAIR + PAIR, :]
                nc.vector.tensor_tensor(hp, out_ps[:, :, 0:D], hp, ALU.add).then_inc(half_added, 1)
                dve.wait_ge(half_added, u + 1)
                nc.vector.tensor_tensor(hp, out_ps[:, :, D:2 * D], hp, ALU.add).then_inc(h_added, 1)

            steps = [0]

            def small(ins):
                steps[0] += 1
                ins.then_inc(c_step, 1)
                dve.wait_ge(c_step, steps[0])

            def class_statistics():
                for t in range(2):
                    small(nc.vector.bn_stats(c_stats[:, t], cls["tok"][:, t, :]))
                    small(nc.vector.bn_aggr(c_mv[:, t], c_stats[:, t]))
                nc.vector.tensor_scalar(c_mv[:, :, 1], c_mv[:, :, 1], EPS_LN, None, ALU.add).then_inc(c_var_ready, 1)

            def class_norm():
                dve.wait_ge(c_rstd_ready, 1)
                for t in range(2):
                    nc.vector.tensor_scalar(c_xf[:, t, :], cls["tok"][:, t, :], c_mv[:, t, 0:1], c_rstd[:, t:t + 1],
                                            ALU.subtract, ALU.mult).then_inc(c_xf_ready, 1)

            def class_gates():
                dve.wait_ge(lg_in_bank, 1)
                for t in range(2):
                    for q in range(Q):
                        rows, i = slice(B * q, B * q + B), 2 * q + t
                        at = 2 * NCLS * t + 2 * i
                        small(nc.vector.tensor_copy(lg[rows, t, :], lg_ps[rows, at:at + 2]))
                small(nc.vector.tensor_reduce(gm[:], lg[:], AX.X, ALU.max))
                nc.vector.tensor_tensor(lg[:], lg[:], gm[:, :, None].to_broadcast([R, 2, 2]),
                                        ALU.subtract).then_inc(lg_shifted, 1)
                dve.wait_ge(exp_ready, 1)
                small(nc.vector.tensor_reduce(gm[:], ge[:], AX.X, ALU.add))
                small(nc.vector.reciprocal(gm[:], gm[:]))
                small(nc.vector.tensor_tensor(ge[:], ge[:], gm[:, :, None].to_broadcast([R, 2, 2]), ALU.mult))
                small(nc.vector.tensor_reduce(gm[:], ge[:], AX.X, ALU.min))
                small(nc.vector.tensor_tensor(gate[:], ge[:], gm[:, :, None].to_broadcast([R, 2, 2]), ALU.is_gt))
                small(nc.vector.tensor_tensor(gate[:], gate[:], ge[:], ALU.mult))
                small(nc.vector.tensor_reduce(gm[:], gate[:], AX.X, ALU.add))
                small(nc.vector.tensor_scalar(gm[:], gm[:], 1e-6, None, ALU.max))
                small(nc.vector.reciprocal(gm[:], gm[:]))
                small(nc.vector.tensor_tensor(gate[:], gate[:], gm[:, :, None].to_broadcast([R, 2, 2]), ALU.mult))

            def class_results():
                dve.wait_ge(c_out_ready, 1)
                small(nc.vector.tensor_tensor(part[:].rearrange("p t d -> p (t d)"), high_ps,
                                              cls["b_high"][:].rearrange("p t d -> p (t d)"), ALU.add))
                small(nc.vector.tensor_tensor(part2[:], low_ps.rearrange("p (t d) -> p t d", t=2),
                                              cls["b_low"][:, None, :].to_broadcast([R, 2, D]), ALU.add))
                for t in range(2):
                    small(nc.vector.scalar_tensor_tensor(res[:, t, :], part[:, t, :], gate[:, t, 0:1],
                                                         cls["tok"][:, t, :], ALU.mult, ALU.add))
                for t in range(2):
                    ins = nc.vector.scalar_tensor_tensor(res[:, t, :], part2[:, t, :], gate[:, t, 1:2], res[:, t, :],
                                                         ALU.mult, ALU.add)
                    if t == 0:
                        small(ins)
                ins.then_inc(res_ready, 1)

            def step(u, q, ahead4, ahead3, ahead2, ahead1, back1):
                if back1:
                    add_to_h(u - 1)
                if ahead2:
                    take_xs(u + 2, q)
                if ahead3:
                    centre(u + 3, 1 - q)
                if ahead1:
                    low_gelu(u + 1, 1 - q, 0)
                if ahead4:
                    normalise(u + 4, q)
                if ahead3:
                    low_part(u + 3, 1 - q)
                if ahead1:
                    low_gelu(u + 1, 1 - q, 1)
                    low_gelu(u + 1, 1 - q, 2)

            normalise(0, 0)
            normalise(1, 1)
            centre(0, 0)
            normalise(2, 0)
            low_part(0, 0)
            if first:
                dve.wait_ge(w_hi, 3)
                nc.vector.tensor_tensor(w1[:, 3, :], raw1[:, 0, :], f32(w1[:, 0, :]), ALU.subtract).then_inc(w_lo, 1)
                nc.vector.tensor_tensor(w1[0:64, 4, :], raw1[0:64, 1, :], f32(w1[0:64, 1, :]),
                                        ALU.subtract).then_inc(w_lo, 1)
            take_xs(0, 0)
            centre(1, 1)
            normalise(3, 1)
            low_part(1, 1)
            if first:
                dve.wait_ge(w_hi, 4)
                nc.vector.tensor_tensor(w2[:, :, 1, :], raw2[:], f32(w2[:, :, 0, :]), ALU.subtract).then_inc(w_lo, 1)
            take_xs(1, 1)
            centre(2, 0)
            low_part(2, 0)
            for i in range(3):
                low_gelu(0, 0, i)
            if first:
                dve.wait_ge(tok_in, 16 * NCLS)
            step(0, 0, True, True, True, True, False)
            if first:
                class_statistics()
            step(1, 1, True, True, True, True, True)
            if first:
                class_norm()
            with dve.Fori(0, (BREAK - 2) // 2) as it:
                for q in range(2):
                    step(it * 2 + (2 + q), q, True, True, True, True, True)
            if first:
                dve.wait_ge(xt_in_bank, 1)
                nc.vector.tensor_copy(xt[:].rearrange("p c t r -> p (c t r)"), xt_ps).then_inc(xt_ready, 1)
                add_to_h(BREAK - 1)
                class_gates()
                dve.wait_ge(cls_in, 16 * (2 * NEXP + 7))
                class_results()
            for u in range(BREAK, NPAIR):
                step(u, u % 2, False, u + 3 < NPAIR, u + 2 < NPAIR, u + 1 < NPAIR, not (first and u == BREAK))
                if u == NPAIR - 3 and first:
                    dve.wait_ge(att_in, 16 * ATT_LOADS)
                    nc.vector.tensor_scalar(att["bqk"][:, :, 0:1], att["bqk"][:, :, 0:1], SCALE, None, ALU.mult)
            add_to_h(NPAIR - 1)

        @block.scalar
        def _(act):
            def high_part(u, q):
                act.wait_ge(xf_ready, u * PAIR + PAIR)
                nc.scalar.activation(xn[q][:, :, 0:D], xf[:], ACT.Copy).then_inc(xn_hi, 1)

            def gelu(u, q, i):
                act.wait_ge(hid_in_bank, u * 3 + (i + 1))
                if not (isinstance(u, int) and u == 0):
                    act.wait_ge(g_lo, u * 3 + (i - 2))
                for c in (2 * i, 2 * i + 1):
                    ins = nc.scalar.activation(gf[:, c, :], hid_ps[i][:, T2 * (c % 2):T2 * (c % 2) + T2], ACT.Gelu,
                                               bias=b1[:, c:c + 1])
                ins.then_inc(gelu_ready, 1)
                c = slice(2 * i, 2 * i + 2)
                act.wait_ge(gelu_ready, u * 3 + (i + 1))
                nc.scalar.activation(gh[q][:, c], gf[:, c], ACT.Copy).then_inc(g_hi, 1)

            def step(u, q, ahead3, ahead1):
                if ahead1:
                    gelu(u + 1, 1 - q, 0)
                    gelu(u + 1, 1 - q, 1)
                if ahead3:
                    high_part(u + 3, 1 - q)
                if ahead1:
                    gelu(u + 1, 1 - q, 2)

            def class_experts():
                act.wait_ge(lg_shifted, 1)
                nc.scalar.activation(ge[:], lg[:], ACT.Exp).then_inc(exp_ready, 1)
                for e in range(NEXP):
                    n = 2 * B if e < Q else R
                    for half in range(2):
                        act.wait_ge(c_hid_in_bank, 2 * e + half + 1)
                        for j in range(3):
                            f = 3 * half + j
                            src = hid_ps[(2 * e + half) % 3][:, n * j:n * j + n]
                            if e < Q:
                                src = src.rearrange("p (t b) -> p t b", t=2)
                                dst = hid_q[:, f, :, B * e:B * e + B]
                            else:
                                dst = hid_t[:, f, e - Q, :]
                            ins = nc.scalar.activation(dst, src, ACT.Gelu, bias=cls["a1b"][:, e, f:f + 1])
                        ins.then_inc(c_gelu_ready, 1)

            if first:
                for i in range(3):
                    nc.scalar.activation(w1[:, i, :], raw1[:, i, :], ACT.Copy).then_inc(w_hi, 1)
            high_part(0, 0)
            if first:
                nc.scalar.activation(w2[:, :, 0, :], raw2[:], ACT.Copy).then_inc(w_hi, 1)
            high_part(1, 1)
            gelu(0, 0, 0)
            gelu(0, 0, 1)
            high_part(2, 0)
            gelu(0, 0, 2)
            step(0, 0, True, True)
            step(1, 1, True, True)
            with act.Fori(0, (BREAK - 2) // 2) as it:
                for q in range(2):
                    step(it * 2 + (2 + q), q, True, True)
            if first:
                act.wait_ge(cls_in, 16 * (2 * NEXP + 7))
                class_experts()
            for u in range(BREAK, NPAIR):
                step(u, u % 2, u + 3 < NPAIR, u + 1 < NPAIR)

        @block.tensor
        def _(pe):
            def transpose_x(u, q):
                pe.wait_ge(xn_lo, u + 1)
                if not (isinstance(u, int) and u == 0):
                    pe.wait_ge(xs_ready, u * PAIR)
                for i in range(PAIR):
                    for s in range(3):
                        ins = nc.tensor.transpose(x_ps[i][:, L * s:L * s + L].bitcast(F32R),
                                                  xn[q][:, i, L * s:L * s + L], identr[:])
                    ins.then_inc(x_in_bank, 1)

            def hidden(u, q):
                pe.wait_ge(xs_ready, u * PAIR + PAIR)
                for c in range(HJ):
                    bank, at = hid_ps[c // 2], T2 * (c % 2)
                    if c % 2 == 0 and not (isinstance(u, int) and u == 0):
                        pe.wait_ge(gelu_ready, u * 3 + (c // 2 - 2))
                    cols = slice(128 * c, 128 * c + 128)
                    for s in range(4):
                        nc.tensor.matmul(bank[:, at:at + T2], w1[:, s, cols], xs[q][:, s % 3, :], start=(s == 0),
                                         stop=False)
                    ins = nc.tensor.matmul(bank[:, at:at + T2], w1[0:64, 4, cols], xs[q][0:64, 1, :], start=False,
                                           stop=True)
                    if c % 2 == 1:
                        ins.then_inc(hid_in_bank, 1)

            def project(u, q):
                pe.wait_ge(g_hi, u * 3 + 3)
                pe.wait_ge(g_lo, u * 3 + 3)
                if not (isinstance(u, int) and u == 0):
                    pe.wait_ge(h_added, u)
                for i in range(PAIR):
                    t = slice(L * i, L * i + L)
                    for c in range(HJ):
                        nc.tensor.matmul(out_ps[:, i, 0:2 * D], gh[q][:, c, t], w2[:, c].rearrange("f s d -> f (s d)"),
                                         start=(c == 0), stop=False, skip_group_check=True)
                        ins = nc.tensor.matmul(out_ps[:, i, 0:D], gl[q][:, c, t], w2[:, c, 0, :], start=False,
                                               stop=(c == HJ - 1), skip_group_check=True)
                ins.then_inc(out_ready, 1)

            def transpose_classes():
                pe.wait_ge(c_xf_ready, 2)
                for t in range(2):
                    for c in range(2):
                        at = (2 * c + t) * R
                        ins = nc.tensor.transpose(xt_ps[:, at:at + R], c_xf[:, t, DC * c:DC * c + DC], ident[0:R, 0:R])
                ins.then_inc(xt_in_bank, 1)

            def columns(e):
                if e < Q:
                    return lambda c: xt[:, c, :, B * e:B * e + B]
                return lambda c: xt[:, c, e - Q, :]

            def class_experts():
                pe.wait_ge(xt_ready, 1)
                for t in range(2):
                    for c in range(2):
                        ins = nc.tensor.matmul(lg_ps[:, 2 * NCLS * t:2 * NCLS * (t + 1)], xt[:, c, t, :],
                                               cls["gw"][:, c, :], start=(c == 0), stop=(c == 1))
                ins.then_inc(lg_in_bank, 1)
                pe.wait_ge(gelu_ready, 3 * BREAK + 3)
                for e in range(NEXP):
                    n = 2 * B if e < Q else R
                    for half in range(2):
                        u = 2 * e + half
                        if u >= 3:
                            pe.wait_ge(c_gelu_ready, u - 2)
                        for j in range(3):
                            out = hid_ps[u % 3][:, n * j:n * j + n]
                            if e < Q:
                                out = out.rearrange("p (t b) -> p t b", t=2)
                            f = (3 * half + j) * 128
                            for c in range(2):
                                ins = nc.tensor.matmul(out, cls["a1"][:, e, c, f:f + 128], columns(e)(c),
                                                       start=(c == 0), stop=(c == 1))
                        ins.then_inc(c_hid_in_bank, 1)
                pe.wait_ge(h_added, BREAK)
                pe.wait_ge(lg_shifted, 1)
                pe.wait_ge(c_gelu_ready, 2 * NEXP)
                for t in range(2):
                    for j in range(HJ):
                        nc.tensor.matmul(high_ps[:, D * t:D * t + D], hid_q[:, j, t, :], cls["a2"][:, Q + t, j, :],
                                         start=(j == 0), stop=(j == HJ - 1))
                    for q in range(Q):
                        rows = slice(B * q, B * q + B)
                        for j in range(HJ):
                            ins = nc.tensor.matmul(low_ps[rows, D * t:D * t + D], hid_t[:, j, t, rows],
                                                   cls["a2"][:, q, j, :], start=(j == 0), stop=(j == HJ - 1))
                ins.then_inc(c_out_ready, 1)

            def step(u, q, ahead2, ahead1):
                if ahead2:
                    transpose_x(u + 2, q)
                if ahead1:
                    hidden(u + 1, 1 - q)
                if isinstance(u, int) and u == BREAK and first:
                    pe.wait_ge(res_ready, 1)
                project(u, q)

            transpose_x(0, 0)
            if first:
                pe.wait_ge(w_lo, 2)
            hidden(0, 0)
            transpose_x(1, 1)
            hidden(1, 1)
            transpose_x(2, 0)
            if first:
                pe.wait_ge(w_lo, 3)
            project(0, 0)
            step(1, 1, True, True)
            with pe.Fori(0, (BREAK - 2) // 2) as it:
                for q in range(2):
                    step(it * 2 + (2 + q), q, True, True)
            if first:
                transpose_classes()
                pe.wait_ge(cls_in, 16 * (2 * NEXP + 7))
                class_experts()
            for u in range(BREAK, NPAIR):
                step(u, u % 2, u + 2 < NPAIR, u + 1 < NPAIR)


def attention_phase(nc, io, keep):
    with ExitStack() as ctx:
        def sb(name, shape, dt=F32):
            return ctx.enter_context(nc.sbuf_tensor(f"{name}_a", shape, dt))

        def psum(name, shape, dt=F32):
            return ctx.enter_context(nc.psum_tensor(f"{name}_a", shape, dt))

        def sem(name):
            return ctx.enter_context(nc.semaphore(f"{name}_a"))

        h, ident, nhalf = keep["h"], keep["ident"], keep["nhalf"]
        att = keep["att"]
        wqk, wv, bqk, bv, wo = att["wqk"], att["wv"], att["bqk"], att["bv"], att["wo"]
        raw1, raw2, w1, w2 = keep["raw1"], keep["raw2"], keep["w1"], keep["w2"]
        stats = sb("stats", [L, 6])
        mv = sb("mv", [L, 2, 2])
        rstd = sb("rstd", [L, 2])
        xn = [sb(f"xn{q}", [L, D]) for q in range(2)]
        xs = [sb(f"xs{q}", [128, 2, L]) for q in range(2)]
        qt = [sb(f"qt{q}", [128, GR, L]) for q in range(2)]
        kt = [sb(f"kt{q}", [128, GR, L]) for q in range(2)]
        v = [sb(f"v{q}", [L, GR, ROWS, 32]) for q in range(2)]
        nmax = sb("nmax", [L, 2, ROWS, GR])
        probs = sb("probs", [L, 2, ROWS * GR, L])
        probs_t = sb("probs_t", [L, ROWS * GR, L])
        rsum = sb("rsum", [L, 2, ROWS * GR])
        rinv = sb("rinv", [L, 2, ROWS * GR])
        ot = sb("ot", [128, GR, L])

        s_ps = psum("s_ps", [L, ROWS, BANK])
        r_ps = [psum(f"r_ps{i}", [128, BANK]) for i in range(4)]

        pads_set = sem("pads_set")
        ff_in = sem("ff_in")
        w1_hi = sem("w1_hi")
        w2_hi = sem("w2_hi")
        cls_stored = sem("cls_stored")
        STORED = B - 4 * PAIR
        aggr_step = sem("aggr_step")
        var_ready = sem("var_ready")
        rstd_ready = sem("rstd_ready")
        xn_ready = sem("xn_ready")
        x_in_bank = sem("x_in_bank")
        q_in_bank = sem("q_in_bank")
        k_in_bank = sem("k_in_bank")
        v_in_bank = sem("v_in_bank")
        s_ready = sem("s_ready")
        nmax_ready = sem("nmax_ready")
        exp_ready = sem("exp_ready")
        pt_in_bank = sem("pt_in_bank")
        o_in_bank = sem("o_in_bank")
        rinv_ready = sem("rinv_ready")
        probs_ready = sem("probs_ready")
        y_in_bank = sem("y_in_bank")
        r_free = [sem(f"r_free{i}") for i in range(4)]
        block = ctx.enter_context(nc.Block())

        @block.sync
        def _(sp):
            store_class_tokens(sp, h, keep["cls_res"], STORED, B, cls_stored)
            load_feed_forward(sp, io, keep, "ffn1", ff_in)
            sp.wait_ge(cls_stored, 16 * NCLS)
            sp.wait_ge(ff_in, 16 * FF_LOADS)

        @block.gpsimd
        def _(pool):
            def rstd_of(k, q):
                pool.wait_ge(var_ready, k + 1)
                nc.gpsimd.tensor_tensor(rstd[:, q:q + 1], mv[:, q, 1:2], nhalf[:], ALU.pow).then_inc(rstd_ready, 1)

            def normalise(k, q):
                for half in range(2):
                    heads = slice(H // 2 * half, H // 2 * half + H // 2)
                    pool.wait_ge(rinv_ready, k * 2 + (half + 1))
                    nc.gpsimd.tensor_tensor(probs[:, q, heads], probs[:, q, heads],
                                            rinv[:, q, heads, None].to_broadcast([L, H // 2, L]),
                                            ALU.mult).then_inc(probs_ready, 1)

            rstd_of(0, 0)
            rstd_of(1, 1)
            with pool.Fori(0, (B - 2) // 2) as it:
                for q in range(2):
                    rstd_of(it * 2 + (2 + q), q)
                    normalise(it * 2 + q, q)
            normalise(B - 2, 0)
            normalise(B - 1, 1)

        @block.vector
        def _(dve):
            def variance(k, q):
                nc.vector.bn_stats(stats[:], h[:, k, :])
                dve.drain()
                nc.vector.bn_aggr(mv[:, q], stats[:]).then_inc(aggr_step, 1)
                dve.wait_ge(aggr_step, k + 1)
                nc.vector.tensor_scalar(mv[:, q, 1:2], mv[:, q, 1:2], EPS_LN, None, ALU.add).then_inc(var_ready, 1)

            def centre(k, q):
                dve.wait_ge(rstd_ready, k + 1)
                nc.vector.tensor_scalar(xn[q][:], h[:, k, :], mv[:, q, 0:1], rstd[:, q:q + 1], ALU.subtract,
                                        ALU.mult).then_inc(xn_ready, 1)

            def take_xs(k, q):
                dve.wait_ge(x_in_bank, k + 1)
                nc.vector.tensor_copy(xs[q][:].rearrange("p g l -> p (g l)"), r_ps[0][:, 0:2 * L]).then_inc(r_free[0], 1)

            def take_qk(k, q):
                dve.wait_ge(q_in_bank, k + 1)
                nc.vector.scalar_tensor_tensor(qt[q][:], r_ps[1][:, 0:GR * L].rearrange("p (g l) -> p g l", g=GR), SCALE,
                                               bqk[:, :, 0:1].to_broadcast([128, GR, L]), ALU.mult,
                                               ALU.add).then_inc(r_free[1], 1)
                dve.wait_ge(k_in_bank, k + 1)
                nc.vector.tensor_tensor(kt[q][:], r_ps[2][:, 0:GR * L].rearrange("p (g l) -> p g l", g=GR),
                                        bqk[:, :, 1:2].to_broadcast([128, GR, L]), ALU.add).then_inc(r_free[2], 1)

            def take_v(k, q):
                dve.wait_ge(v_in_bank, k + 1)
                nc.vector.tensor_tensor(v[q][:].rearrange("l g p d -> l (g p) d")[:, :, 0:HD],
                                        r_ps[0][:, 0:D].rearrange("l (i d) -> l i d", i=H),
                                        bv[:].rearrange("l (i d) -> l i d", i=H), ALU.add).then_inc(r_free[0], 1)

            def row_max(k, q, half):
                dve.wait_ge(s_ready, k * 2 + (half + 1))
                nc.vector.tensor_reduce(nmax[:, q, 2 * half:2 * half + 2, :],
                                        s_ps[:, 2 * half:2 * half + 2, 0:GR * L].rearrange(
                                            "l p (g m) -> l p g m", g=GR),
                                        AX.X, ALU.max, negate=True).then_inc(nmax_ready, 1)

            def take_probs_t(k):
                dve.wait_ge(pt_in_bank, k * 3 + 1)
                nc.vector.tensor_copy(probs_t[:, 0:4, :].rearrange("t i l -> t (i l)"), r_ps[0][:]).then_inc(r_free[0], 1)

            def inverse_sum(k, q, half):
                heads = slice(H // 2 * half, H // 2 * half + H // 2)
                dve.wait_ge(exp_ready, k * 2 + (half + 1))
                nc.vector.reciprocal(rinv[:, q, heads], rsum[:, q, heads]).then_inc(rinv_ready, 1)

            def add_to_h(k):
                dve.wait_ge(y_in_bank, k + 1)
                nc.vector.tensor_tensor(h[:, k, :], r_ps[3][:, 0:D], h[:, k, :], ALU.add).then_inc(r_free[3], 1)

            def step(k, q, main, ahead2, ahead1, back1, back2):
                if ahead2:
                    variance(k + 2, q)
                if main:
                    row_max(k, q, 0)
                if ahead1:
                    take_xs(k + 1, 1 - q)
                if ahead2:
                    centre(k + 2, q)
                if main:
                    row_max(k, q, 1)
                    inverse_sum(k, q, 0)
                    take_v(k, q)
                if ahead1:
                    take_qk(k + 1, 1 - q)
                if back2:
                    add_to_h(k - 2)
                if main:
                    inverse_sum(k, q, 1)
                if back1:
                    take_probs_t(k - 1)

            for q in range(2):
                nc.vector.memset(v[q][:], 0.0).then_inc(pads_set, 1)
            for k in range(2):
                variance(k, k)
                centre(k, k)
            dve.wait_ge(pads_set, 2)
            take_xs(0, 0)
            take_qk(0, 0)
            step(0, 0, True, True, True, False, False)
            step(1, 1, True, True, True, True, False)
            dve.wait_ge(cls_stored, 16 * NCLS)
            with dve.Fori(0, (B - 4) // 2) as it:
                for q in range(2):
                    step(it * 2 + (2 + q), q, True, True, True, True, True)
            step(B - 2, 0, True, False, True, True, True)
            step(B - 1, 1, True, False, False, True, True)
            dve.wait_ge(w1_hi, 1)
            nc.vector.tensor_tensor(w1[:, 3, :], raw1[:, 0, :], f32(w1[:, 0, :]), ALU.subtract)
            nc.vector.tensor_tensor(w1[0:64, 4, :], raw1[0:64, 1, :], f32(w1[0:64, 1, :]), ALU.subtract)
            step(B, 0, False, False, False, True, True)
            dve.wait_ge(w2_hi, 1)
            nc.vector.tensor_tensor(w2[:, :, 1, :], raw2[:], f32(w2[:, :, 0, :]), ALU.subtract)
            step(B + 1, 1, False, False, False, False, True)

        @block.scalar
        def _(act):
            def exps(k, q, half):
                act.wait_ge(nmax_ready, k * 2 + (half + 1))
                for p in (2 * half, 2 * half + 1):
                    for g in range(GR):
                        ins = nc.scalar.activation(probs[:, q, GR * p + g, :], s_ps[:, p, L * g:L * g + L], ACT.Exp,
                                                   bias=nmax[:, q, p, g:g + 1],
                                                   accum_out=rsum[:, q, GR * p + g:GR * p + g + 1])
                ins.then_inc(exp_ready, 1)

            def take_probs_t(k, i):
                act.wait_ge(pt_in_bank, k * 3 + (i + 1))
                nc.scalar.activation(probs_t[:, 4 * i:4 * i + 4, :].rearrange("t i l -> t (i l)"), r_ps[i][:],
                                     ACT.Copy).then_inc(r_free[i], 1)

            def take_o(k):
                act.wait_ge(o_in_bank, k + 1)
                nc.scalar.activation(ot[:].rearrange("p g l -> p (g l)"), r_ps[3][:, 0:GR * L], ACT.Identity,
                                     bias=ident[:, ONE:ONE + 1]).then_inc(r_free[3], 1)

            def step(k, q, main, back1, back2):
                if main:
                    exps(k, q, 0)
                if back2:
                    take_o(k - 2)
                if main:
                    exps(k, q, 1)
                if back1:
                    take_probs_t(k - 1, 1)
                    take_probs_t(k - 1, 2)

            step(0, 0, True, False, False)
            step(1, 1, True, True, False)
            with act.Fori(0, (B - 4) // 2) as it:
                for q in range(2):
                    step(it * 2 + (2 + q), q, True, True, True)
            step(B - 2, 0, True, True, True)
            step(B - 1, 1, True, True, True)
            act.wait_ge(ff_in, 16 * FF_LOADS)
            nc.scalar.activation(w1[:, 0:3, :], raw1[:], ACT.Copy).then_inc(w1_hi, 1)
            step(B, 0, False, True, True)
            nc.scalar.activation(w2[:, :, 0, :], raw2[:], ACT.Copy).then_inc(w2_hi, 1)
            step(B + 1, 1, False, False, True)

        @block.tensor
        def _(pe):
            def wait_free(i, n):
                if not (isinstance(n, int) and n <= 0):
                    pe.wait_ge(r_free[i], n)

            def transpose_x(k, q, used):
                pe.wait_ge(xn_ready, k + 1)
                wait_free(0, used)
                for i in range(2):
                    ins = nc.tensor.transpose(r_ps[0][:, L * i:L * i + L], xn[q][:, GF * i:GF * i + 128], ident[:])
                ins.then_inc(x_in_bank, 1)

            def project_qk(k, q, used_qk):
                for i, ready in ((0, q_in_bank), (1, k_in_bank)):
                    wait_free(1 + i, used_qk)
                    for g in range(GR):
                        ins = nc.tensor.matmul(r_ps[1 + i][:, L * g:L * g + L], wqk[:, g, i, :],
                                               xs[q][:, GROUP_STACK[g], :], start=True, stop=True)
                    ins.then_inc(ready, 1)

            def project_v(k, q, used):
                wait_free(0, used)
                nc.tensor.matmul(r_ps[0][:, 0:2 * GF], xs[q][:, 0, :], wv[:, 0:2, :].rearrange("f g e -> f (g e)"),
                                 start=True, stop=True)
                nc.tensor.matmul(r_ps[0][:, 2 * GF:D], xs[q][:, 1, :], wv[:, 2, :], start=True,
                                 stop=True).then_inc(v_in_bank, 1)

            def scores(k, q, half):
                if not (isinstance(k, int) and k == 0):
                    pe.wait_ge(exp_ready, k * 2 + (half - 1))
                for g in range(GR):
                    for p in (2 * half, 2 * half + 1):
                        rows = slice(32 * p, 32 * p + HD)
                        ins = nc.tensor.matmul(s_ps[:, p, L * g:L * g + L], qt[q][rows, g, :], kt[q][rows, g, :],
                                               start=True, stop=True)
                ins.then_inc(s_ready, 1)

            def transpose_probs(k, q, used):
                for i in range(3):
                    if i < 2:
                        pe.wait_ge(probs_ready, k * 2 + (i + 1))
                    wait_free(i, used[i])
                    for j in range(4):
                        ins = nc.tensor.transpose(r_ps[i][:, L * j:L * j + L], probs[:, q, 4 * i + j, :], ident[:])
                    ins.then_inc(pt_in_bank, 1)

            def attend(k, q, used_o):
                wait_free(3, used_o)
                for g in range(GR):
                    for p in range(ROWS):
                        ins = nc.tensor.matmul(r_ps[3][32 * p:32 * p + 32, L * g:L * g + L], v[q][:, g, p, :],
                                               probs_t[:, GR * p + g, :], start=True, stop=True)
                ins.then_inc(o_in_bank, 1)

            def project_out(k, used):
                wait_free(3, used)
                for g in range(GR):
                    ins = nc.tensor.matmul(r_ps[3][:, 0:D], ot[:, g, :], wo[:, g, :], start=(g == 0), stop=(g == GR - 1))
                ins.then_inc(y_in_bank, 1)

            def step(k, q, main, ahead1, back1, back2, r0, r12, r3):
                if main:
                    last_qk = r12 - 1 if back2 else r12
                    pe.wait_ge(r_free[1], last_qk)
                    pe.wait_ge(r_free[2], last_qk)
                    scores(k, q, 0)
                if back2:
                    pe.wait_ge(r_free[0], r0)
                    pe.wait_ge(r_free[1], r12)
                    pe.wait_ge(r_free[2], r12)
                    attend(k - 2, q, r3)
                if ahead1:
                    transpose_x(k + 1, 1 - q, r0)
                    r0 = r0 + 1
                if main:
                    scores(k, q, 1)
                    project_v(k, q, r0)
                    r0 = r0 + 1
                if ahead1:
                    project_qk(k + 1, 1 - q, r12)
                    r12 = r12 + 1
                if back2:
                    project_out(k - 2, r3 + 1)
                if back1:
                    transpose_probs(k - 1, 1 - q, (r0, r12, r12))

            transpose_x(0, 0, 0)
            pe.wait_ge(r_free[0], 1)
            project_qk(0, 0, 0)
            step(0, 0, True, True, False, False, 1, 1, 0)
            for k in range(1, 4):
                step(k, k % 2, True, True, True, k > 1, 3 * k, 2 * k, 2 * k - 4)
            with pe.Fori(0, (B - 6) // 2) as it:
                for q in range(2):
                    step(it * 2 + (4 + q), q, True, True, True, True, it * 6 + (12 + 3 * q), it * 4 + (8 + 2 * q),
                         it * 4 + (4 + 2 * q))
            step(B - 2, 0, True, True, True, True, 3 * B - 6, 2 * B - 4, 2 * B - 8)
            step(B - 1, 1, True, False, True, True, 3 * B - 3, 2 * B - 2, 2 * B - 6)
            step(B, 0, False, False, True, True, 3 * B - 1, 2 * B - 1, 2 * B - 4)
            step(B + 1, 1, False, False, False, True, 3 * B, 2 * B, 2 * B - 2)


def program(nc, io):
    with ExitStack() as ctx:
        def sb(name, shape, dt=F32):
            return ctx.enter_context(nc.sbuf_tensor(name, shape, dt))

        keep = {
            "h": sb("h", [L, B, D]),
            "ident": sb("ident", [L, L]),
            "identr": sb("identr", [L, L], F32R),
            "nhalf": sb("nhalf", [L, 1]),
            "raw1": sb("raw1", [128, 3, HID]),
            "raw2": sb("raw2", [128, HJ, D]),
            "b1": sb("b1", [128, HJ]),
            "b2": sb("b2", [L, D]),
        }
        mixing_phase(nc, io, keep)
        keep["w1"] = sb("w1", [128, 5, HID], F32R)
        keep["w2"] = sb("w2", [128, HJ, 2, D], F32R)
        keep["att"] = {
            "wqk": sb("wqk_a", [2 * GF, GR, 2, 128]),
            "wv": sb("wv_a", [2 * GF, GR, GF]),
            "bqk": sb("bqk_a", [128, GR, 2]),
            "bv": sb("bv_a", [L, D]),
            "wo": sb("wo_a", [128, GR, D]),
        }
        keep["cls_res"] = sb("cls_res", [3 * B, 2, D])
        with ExitStack() as classes:
            def cls_sb(name, shape):
                return classes.enter_context(nc.sbuf_tensor(f"cls_{name}", shape, F32))

            keep["cls"] = {
                "tok": cls_sb("tok", [3 * B, 2, D]),
                "a1": cls_sb("a1", [DC, NEXP, 2, HID]),
                "a1b": cls_sb("a1b", [128, NEXP, HJ]),
                "a2": cls_sb("a2", [128, NEXP, HJ, D]),
                "b_high": cls_sb("b_high", [3 * B, 2, D]),
                "b_low": cls_sb("b_low", [3 * B, D]),
                "gw": cls_sb("gw", [DC, 2, 2 * NCLS]),
            }
            feed_forward_phase(nc, io, keep, 0)
        attention_phase(nc, io, keep)
        feed_forward_phase(nc, io, keep, 1)


def kernel(**inputs):
    import numpy as np
    import concourse.bacc as bacc
    from concourse.bass_utils import run_bass_kernel_spmd

    def get(name):
        return np.asarray(inputs[name])

    data = {
        "x": get("x")[..., 0].transpose(2, 0, 1),
        "dw_w": get("L0_tok_dw_w")[:, 0, :, 0],
        "pw_w": get("L0_tok_pw_w").T,
        "pw_b": get("L0_tok_pw_b")[None],
        "ln_g": get("L0_tok_ln_g")[None],
        "ln_b": get("L0_tok_ln_b")[None],
        "ln_w": get("L0_attn_ln_w")[None],
        "w_qk": get("L0_attn_W_qk").T,
        "w_o": get("L0_attn_W_o").reshape(D, H, D).transpose(2, 1, 0).reshape(D, H * D),
        "wte": get("L0_attn_wte"),
        "ffn0_w1": get("L0_ffn_moe0_W1"),
        "ffn0_b1": get("L0_ffn_moe0_b1").reshape(HJ, 128).T,
        "ffn0_w2": get("L0_ffn_moe0_W2"),
        "ffn0_b2": get("L0_ffn_moe0_b2")[None],
        "a1": get("L0_ffn_A1_W"),
        "a1b": get("L0_ffn_A1_b").reshape(NEXP, HJ, 128).transpose(2, 0, 1),
        "a2": get("L0_ffn_A2_W"),
        "a2b": get("L0_ffn_A2_b"),
        "gw": get("L0_ffn_G_W").transpose(1, 0, 2).reshape(D, 2 * NCLS),
        "w_qkv": get("L1_attn_W_qkv"),
        "b_qk": get("L1_attn_b_qkv")[:, 0:2 * HD].reshape(GR, ROWS, 2, HD).transpose(1, 3, 0, 2),
        "b_v": get("L1_attn_b_qkv")[:, 2 * HD:].reshape(1, D),
        "w_out": get("L1_attn_W_out"),
        "b_out": get("L1_attn_b_out")[None],
        "ffn1_w1": get("L1_ffn_in_weight").T,
        "ffn1_b1": get("L1_ffn_in_bias").reshape(HJ, 128).T,
        "ffn1_w2": get("L1_ffn_out_weight"),
        "ident": np.eye(L, dtype=np.float32),
        "mask": np.triu(np.full((L, L), -1e30, np.float32), 1),
        "nreg": (1.0 / np.arange(1, L + 1, dtype=np.float32))[:, None].astype(np.float32),
    }
    nc = bacc.Bacc("TRN2", target_bir_lowering=False, num_devices=1)
    io, arrays = {}, {}
    for name, a in data.items():
        a = np.ascontiguousarray(a)
        arrays[f"in_{name}"] = a
        io[name] = nc.dram_tensor(f"in_{name}", a.shape, mybir.dt.from_np(a.dtype), kind="ExternalInput").ap()
    io["out"] = nc.dram_tensor("out_0", (B, L, D), F32, kind="ExternalOutput").ap()
    program(nc, io)
    r = run_bass_kernel_spmd(nc, [arrays], core_ids=[0])
    return r.results[0]["out_0"]
```
